# Optimizing a Trainium2 kernel written in Bass

```python
import numpy as np
import jax
import jax.numpy as jnp

def _softmax(x, axis=-1):
    return jax.nn.softmax(x, axis=axis)

def _gelu(x):
    return jax.nn.gelu(x, approximate=True)

def _silu(x):
    return jax.nn.silu(x)

def _sigmoid(x):
    return jax.nn.sigmoid(x)

def _layernorm(x, axis=-1, eps=1e-05):
    m = jnp.mean(x, axis=axis, keepdims=True)
    v = jnp.var(x, axis=axis, keepdims=True)
    return (x - m) / jnp.sqrt(v + eps)

def _scatter_add(tgt, idx, src, axis=0):
    return tgt.at[idx].add(src)

def _segment_sum(src, seg, n):
    return jax.ops.segment_sum(src, seg, n)
kernel_name = 'mk_gnn_resnorm_d4_gnn_r16_ef6dd1'

def setup_inputs(seed: int=0):
    np.random.seed(seed)
    _w = jnp.asarray

    def _rec_inputs():
        import jax
        import jax.numpy as jnp
        _gk = jax.random.key(seed)
        x = 8.953e-05 + 1 * jax.random.normal(jax.random.fold_in(_gk, 1), (6250, 32), jnp.float32)
        src = jax.random.randint(jax.random.fold_in(_gk, 2), (100000,), 0, 6250, jnp.int32)
        dst = jnp.minimum((6250 * jax.random.uniform(jax.random.fold_in(_gk, 3), (100000,)) ** 2.0).astype(jnp.int32), 99999)
        _o = jnp.argsort(dst, stable=True)
        src = src[_o]
        dst = dst[_o]
        edge_attr_3 = jax.random.uniform(jax.random.fold_in(_gk, 11), (100000, 3), jnp.float32, 0.0, 0.999998)
        node_vec1 = -0.00396605 + 0.997609 * jax.random.normal(jax.random.fold_in(_gk, 13), (6250, 1), jnp.float32)
        return (x, src, dst, edge_attr_3, node_vec1)
    x, src, dst, edge_attr_3, node_vec1 = _rec_inputs()

    def _L0_gnn_setup():
        import jax, jax.numpy as jnp
        import numpy as np
        D = 3
        KS = 5
        K = KS ** D
        S = 2 ** D
        _COMBOS = np.array([[s >> d & 1 for d in range(D)] for s in range(S)], dtype=np.int32)
        _STRIDES = np.array([KS ** (D - 1 - d) for d in range(D)], dtype=np.int32)

        def spline_basis(pseudo):
            pos = pseudo * (KS - 1)
            i0 = jnp.clip(jnp.floor(pos), 0, KS - 2).astype(jnp.int32)
            frac = pos - i0
            combos = jnp.asarray(_COMBOS)
            basis = jnp.prod(jnp.where(combos[None] == 1, frac[:, None, :], 1.0 - frac[:, None, :]), axis=-1)
            idx = jnp.sum((i0[:, None, :] + combos[None]) * jnp.asarray(_STRIDES)[None, None, :], axis=-1)
            return (basis, idx)

        def spline_conv(x, row, col, basis, idx, W, b):
            N = x.shape[0]
            Fout = W.shape[2]
            z = jnp.einsum('ni,kio->nko', x, W).reshape(N * K, Fout)
            gathered = z[col[:, None] * K + idx]
            msg = jnp.einsum('es,eso->eo', basis, gathered)
            out = jax.ops.segment_sum(msg, row, num_segments=N)
            deg = jax.ops.segment_sum(jnp.ones_like(msg[:, 0]), row, num_segments=N)
            return out / jnp.maximum(deg, 1.0)[:, None] + b
        key = jax.random.key(seed)
        ks = jax.random.split(key, 13)
        N, E, Fin, Fout = (1250, 20000, 32, 32)

        def u(k, shape, size):
            bound = 1.0 / np.sqrt(size)
            return jax.random.uniform(k, shape, jnp.float32, -bound, bound)
        return dict(x=jax.random.normal(ks[0], (N, Fin), jnp.float32), edge_index=jax.random.randint(ks[1], (2, E), 0, N, dtype=jnp.int32), pseudo=jax.random.uniform(ks[2], (E, D), jnp.float32), stn1_w=u(ks[3], (K, 1, 64), 1 * S), stn1_b=u(ks[4], (64,), 1 * S), stn2_w=u(ks[5], (K, 64, 64), 64 * S), stn2_b=u(ks[6], (64,), 64 * S), stn3_w=u(ks[7], (64, 64), 64), stn3_b=u(ks[8], (64,), 64), stn4_w=u(ks[9], (64, 3), 64), stn4_b=u(ks[10], (3,), 64), conv_w=u(ks[11], (K, Fin, Fout), Fin * S), conv_b=u(ks[12], (Fout,), Fin * S))
    _L0_gnn_all = _L0_gnn_setup()
    _L0_gnn_in = {k: v for k, v in _L0_gnn_all.items() if k in ('stn1_w', 'stn1_b', 'stn2_w', 'stn2_b', 'stn3_w', 'stn3_b', 'stn4_w', 'stn4_b', 'conv_w', 'conv_b')}
    del _L0_gnn_all

    def _L1_gnn_setup():
        import jax, jax.numpy as jnp
        import numpy as np
        N_NODES = 1250
        N_EDGES = 40000
        D_IN = 32
        HEADS = 6
        C_HID = 6
        NEG_SLOPE = 0.2

        def _gat_conv(x, src, dst, W, a_src, a_dst, bias, concat, n_nodes):
            H, C = a_src.shape
            xw = (x @ W).reshape(n_nodes, H, C)
            al_s = jnp.sum(xw * a_src[None], axis=-1)
            al_d = jnp.sum(xw * a_dst[None], axis=-1)
            e = jax.nn.leaky_relu(al_s[src] + al_d[dst], NEG_SLOPE)
            e_max = jax.ops.segment_max(e, dst, num_segments=n_nodes)
            ex = jnp.exp(e - e_max[dst])
            denom = jax.ops.segment_sum(ex, dst, num_segments=n_nodes)
            alpha = ex / denom[dst]
            msg = xw[src] * alpha[..., None]
            out = jax.ops.segment_sum(msg, dst, num_segments=n_nodes)
            out = out.reshape(n_nodes, H * C) if concat else out.mean(axis=1)
            return out + bias

        def _glorot(key, shape):
            fan = shape[0] + shape[-1]
            return jax.random.uniform(key, shape, jnp.float32, -1.0, 1.0) * np.sqrt(6.0 / fan)
        key = jax.random.key(seed)
        ks = jax.random.split(key, 12)
        x = jax.random.normal(ks[0], (N_NODES, D_IN), jnp.float32)
        edge_index = jax.random.randint(ks[1], (2, N_EDGES), 0, N_NODES, jnp.int64)
        HC = HEADS * C_HID
        params = {'W1': _glorot(ks[2], (D_IN, HC)), 'a_src1': _glorot(ks[3], (HEADS, C_HID)), 'a_dst1': _glorot(ks[4], (HEADS, C_HID)), 'b1': jnp.zeros((HC,), jnp.float32), 'W2': _glorot(ks[5], (HC, HC)), 'a_src2': _glorot(ks[6], (HEADS, C_HID)), 'a_dst2': _glorot(ks[7], (HEADS, C_HID)), 'b2': jnp.zeros((HC,), jnp.float32), 'W3': _glorot(ks[8], (HC, HEADS * D_IN)), 'a_src3': _glorot(ks[9], (HEADS, D_IN)), 'a_dst3': _glorot(ks[10], (HEADS, D_IN)), 'b3': jnp.zeros((D_IN,), jnp.float32)}
        return {'x': x, 'edge_index': edge_index, **params}
    _L1_gnn_all = _L1_gnn_setup()
    _L1_gnn_in = {k: v for k, v in _L1_gnn_all.items() if k in ('W1', 'a_src1', 'a_dst1', 'b1', 'W2', 'a_src2', 'a_dst2', 'b2', 'W3', 'a_src3', 'a_dst3', 'b3')}
    del _L1_gnn_all

    def _L2_gnn_setup():
        import jax, jax.numpy as jnp
        import numpy as np
        N_NODES = 6250
        N_EDGES = 100000
        IN_DIM, HID_DIM, OUT_DIM = (33, 64, 32)

        def _gcn_conv(x, W, b, src, dst, n_nodes):
            h = x @ W
            ones = jnp.ones(dst.shape, dtype=h.dtype)
            deg = jax.ops.segment_sum(ones, dst, num_segments=n_nodes)
            dinv = jnp.where(deg > 0, jax.lax.rsqrt(deg), 0.0)
            norm = dinv[src] * dinv[dst]
            msg = h[src] * norm[:, None]
            out = jax.ops.segment_sum(msg, dst, num_segments=n_nodes)
            return out + b
        key = jax.random.key(seed)
        ks = jax.random.split(key, 8)
        z = jax.random.normal(ks[0], (N_NODES, 32), dtype=jnp.float32)
        action = jax.random.normal(ks[1], (N_NODES, 1), dtype=jnp.float32)
        edge_index = jax.random.randint(ks[2], (2, N_EDGES), 0, N_NODES, dtype=jnp.int64)
        W1 = jax.random.normal(ks[3], (IN_DIM, HID_DIM), dtype=jnp.float32) * (1.0 / np.sqrt(IN_DIM))
        b1 = jnp.zeros((HID_DIM,), dtype=jnp.float32)
        W2 = jax.random.normal(ks[4], (HID_DIM, OUT_DIM), dtype=jnp.float32) * (1.0 / np.sqrt(HID_DIM))
        b2 = jnp.zeros((OUT_DIM,), dtype=jnp.float32)
        return {'z': z, 'action': action, 'edge_index': edge_index, 'W1': W1, 'b1': b1, 'W2': W2, 'b2': b2}
    _L2_gnn_all = _L2_gnn_setup()
    _L2_gnn_in = {k: v for k, v in _L2_gnn_all.items() if k in ('W1', 'b1', 'W2', 'b2')}
    del _L2_gnn_all

    def _L3_gnn_setup():
        import jax, jax.numpy as jnp
        import numpy as np
        N_NODES = 6250
        N_EDGES = 100000
        LATENT_DIM = 32
        NUM_LAYERS = 3
        key = jax.random.key(seed)
        k_x, k_e = jax.random.split(key)
        x = jax.random.normal(k_x, (N_NODES, LATENT_DIM), dtype=jnp.float32)
        edge_index = jax.random.randint(k_e, (2, N_EDGES), 0, N_NODES, dtype=jnp.int64)
        return {'x': x, 'edge_index': edge_index, 'num_layers': NUM_LAYERS}
    _L3_gnn_all = _L3_gnn_setup()
    _L3_gnn_in = {k: v for k, v in _L3_gnn_all.items() if k in ()}
    del _L3_gnn_all
    return {'x': x, 'src': src, 'dst': dst, 'edge_attr_3': edge_attr_3, 'node_vec1': node_vec1, 'L0_gnn_stn1_w': _L0_gnn_in['stn1_w'], 'L0_gnn_stn1_b': _L0_gnn_in['stn1_b'], 'L0_gnn_stn2_w': _L0_gnn_in['stn2_w'], 'L0_gnn_stn2_b': _L0_gnn_in['stn2_b'], 'L0_gnn_stn3_w': _L0_gnn_in['stn3_w'], 'L0_gnn_stn3_b': _L0_gnn_in['stn3_b'], 'L0_gnn_stn4_w': _L0_gnn_in['stn4_w'], 'L0_gnn_stn4_b': _L0_gnn_in['stn4_b'], 'L0_gnn_conv_w': _L0_gnn_in['conv_w'], 'L0_gnn_conv_b': _L0_gnn_in['conv_b'], 'L1_gnn_W1': _L1_gnn_in['W1'], 'L1_gnn_a_src1': _L1_gnn_in['a_src1'], 'L1_gnn_a_dst1': _L1_gnn_in['a_dst1'], 'L1_gnn_b1': _L1_gnn_in['b1'], 'L1_gnn_W2': _L1_gnn_in['W2'], 'L1_gnn_a_src2': _L1_gnn_in['a_src2'], 'L1_gnn_a_dst2': _L1_gnn_in['a_dst2'], 'L1_gnn_b2': _L1_gnn_in['b2'], 'L1_gnn_W3': _L1_gnn_in['W3'], 'L1_gnn_a_src3': _L1_gnn_in['a_src3'], 'L1_gnn_a_dst3': _L1_gnn_in['a_dst3'], 'L1_gnn_b3': _L1_gnn_in['b3'], 'L2_gnn_W1': _L2_gnn_in['W1'], 'L2_gnn_b1': _L2_gnn_in['b1'], 'L2_gnn_W2': _L2_gnn_in['W2'], 'L2_gnn_b2': _L2_gnn_in['b2']}

def reference(x, src, dst, edge_attr_3, node_vec1, L0_gnn_stn1_w, L0_gnn_stn1_b, L0_gnn_stn2_w, L0_gnn_stn2_b, L0_gnn_stn3_w, L0_gnn_stn3_b, L0_gnn_stn4_w, L0_gnn_stn4_b, L0_gnn_conv_w, L0_gnn_conv_b, L1_gnn_W1, L1_gnn_a_src1, L1_gnn_a_dst1, L1_gnn_b1, L1_gnn_W2, L1_gnn_a_src2, L1_gnn_a_dst2, L1_gnn_b2, L1_gnn_W3, L1_gnn_a_src3, L1_gnn_a_dst3, L1_gnn_b3, L2_gnn_W1, L2_gnn_b1, L2_gnn_W2, L2_gnn_b2):
    import jax
    import jax.numpy as jnp

    def _L0_gnn_ref(x, edge_index, pseudo, stn1_w, stn1_b, stn2_w, stn2_b, stn3_w, stn3_b, stn4_w, stn4_b, conv_w, conv_b):
        import jax, jax.numpy as jnp
        import numpy as np
        D = 3
        KS = 5
        K = KS ** D
        S = 2 ** D
        _COMBOS = np.array([[s >> d & 1 for d in range(D)] for s in range(S)], dtype=np.int32)
        _STRIDES = np.array([KS ** (D - 1 - d) for d in range(D)], dtype=np.int32)

        def spline_basis(pseudo):
            pos = pseudo * (KS - 1)
            i0 = jnp.clip(jnp.floor(pos), 0, KS - 2).astype(jnp.int32)
            frac = pos - i0
            combos = jnp.asarray(_COMBOS)
            basis = jnp.prod(jnp.where(combos[None] == 1, frac[:, None, :], 1.0 - frac[:, None, :]), axis=-1)
            idx = jnp.sum((i0[:, None, :] + combos[None]) * jnp.asarray(_STRIDES)[None, None, :], axis=-1)
            return (basis, idx)

        def spline_conv(x, row, col, basis, idx, W, b):
            N = x.shape[0]
            Fout = W.shape[2]
            z = jnp.einsum('ni,kio->nko', x, W).reshape(N * K, Fout)
            gathered = z[col[:, None] * K + idx]
            msg = jnp.einsum('es,eso->eo', basis, gathered)
            out = jax.ops.segment_sum(msg, row, num_segments=N)
            deg = jax.ops.segment_sum(jnp.ones_like(msg[:, 0]), row, num_segments=N)
            return out / jnp.maximum(deg, 1.0)[:, None] + b
        N = x.shape[0]
        row, col = (edge_index[0], edge_index[1])
        basis, idx = spline_basis(pseudo)
        h = jnp.ones((N, 1), x.dtype)
        h = jax.nn.elu(spline_conv(h, row, col, basis, idx, stn1_w, stn1_b))
        h = jax.nn.elu(spline_conv(h, row, col, basis, idx, stn2_w, stn2_b))
        h = jax.nn.elu(h @ stn3_w + stn3_b)
        t = h @ stn4_w + stn4_b
        new_pseudo = jnp.clip(pseudo + t[col] - t[row], 0.0, 1.0)
        basis2, idx2 = spline_basis(new_pseudo)
        return spline_conv(x, row, col, basis2, idx2, conv_w, conv_b)

    def _L1_gnn_ref(x, edge_index, W1, a_src1, a_dst1, b1, W2, a_src2, a_dst2, b2, W3, a_src3, a_dst3, b3):
        import jax, jax.numpy as jnp
        import numpy as np
        N_NODES = 1250
        N_EDGES = 40000
        D_IN = 32
        HEADS = 6
        C_HID = 6
        NEG_SLOPE = 0.2

        def _gat_conv(x, src, dst, W, a_src, a_dst, bias, concat, n_nodes):
            H, C = a_src.shape
            xw = (x @ W).reshape(n_nodes, H, C)
            al_s = jnp.sum(xw * a_src[None], axis=-1)
            al_d = jnp.sum(xw * a_dst[None], axis=-1)
            e = jax.nn.leaky_relu(al_s[src] + al_d[dst], NEG_SLOPE)
            e_max = jax.ops.segment_max(e, dst, num_segments=n_nodes)
            ex = jnp.exp(e - e_max[dst])
            denom = jax.ops.segment_sum(ex, dst, num_segments=n_nodes)
            alpha = ex / denom[dst]
            msg = xw[src] * alpha[..., None]
            out = jax.ops.segment_sum(msg, dst, num_segments=n_nodes)
            out = out.reshape(n_nodes, H * C) if concat else out.mean(axis=1)
            return out + bias

        def _glorot(key, shape):
            fan = shape[0] + shape[-1]
            return jax.random.uniform(key, shape, jnp.float32, -1.0, 1.0) * np.sqrt(6.0 / fan)
        n = x.shape[0]
        loop = jnp.arange(n, dtype=edge_index.dtype)
        src = jnp.concatenate([edge_index[0], loop])
        dst = jnp.concatenate([edge_index[1], loop])
        h = _gat_conv(x, src, dst, W1, a_src1, a_dst1, b1, True, n)
        h = jax.nn.relu(h)
        h = _gat_conv(h, src, dst, W2, a_src2, a_dst2, b2, True, n)
        h = jax.nn.relu(h)
        h = _gat_conv(h, src, dst, W3, a_src3, a_dst3, b3, False, n)
        return jax.nn.softmax(h, axis=0)

    def _L2_gnn_ref(z, action, edge_index, W1, b1, W2, b2):
        import jax, jax.numpy as jnp
        import numpy as np
        N_NODES = 6250
        N_EDGES = 100000
        IN_DIM, HID_DIM, OUT_DIM = (33, 64, 32)

        def _gcn_conv(x, W, b, src, dst, n_nodes):
            h = x @ W
            ones = jnp.ones(dst.shape, dtype=h.dtype)
            deg = jax.ops.segment_sum(ones, dst, num_segments=n_nodes)
            dinv = jnp.where(deg > 0, jax.lax.rsqrt(deg), 0.0)
            norm = dinv[src] * dinv[dst]
            msg = h[src] * norm[:, None]
            out = jax.ops.segment_sum(msg, dst, num_segments=n_nodes)
            return out + b
        n = z.shape[0]
        loop = jnp.arange(n, dtype=edge_index.dtype)
        src = jnp.concatenate([edge_index[0], loop])
        dst = jnp.concatenate([edge_index[1], loop])
        x = jnp.concatenate([z, action], axis=-1)
        x = jax.nn.relu(_gcn_conv(x, W1, b1, src, dst, n))
        x = _gcn_conv(x, W2, b2, src, dst, n)
        return x

    def _L3_gnn_ref(x, edge_index, num_layers):
        import jax, jax.numpy as jnp
        import numpy as np
        N_NODES = 6250
        N_EDGES = 100000
        LATENT_DIM = 32
        NUM_LAYERS = 3
        N = x.shape[0]
        src = edge_index[0]
        dst = edge_index[1]
        cnt = jax.ops.segment_sum(jnp.ones((edge_index.shape[1],), x.dtype), dst, num_segments=N)
        denom = jnp.maximum(cnt, 1.0)[:, None]
        scale = 1.0 / (num_layers + 1)
        final = x * scale
        for _ in range(num_layers):
            summed = jax.ops.segment_sum(x[src], dst, num_segments=N)
            x = summed / denom
            final = final + x * scale
        return final
    edge_index = jnp.stack([src, dst])
    x = _layernorm(x + _L0_gnn_ref(x, edge_index, edge_attr_3, L0_gnn_stn1_w, L0_gnn_stn1_b, L0_gnn_stn2_w, L0_gnn_stn2_b, L0_gnn_stn3_w, L0_gnn_stn3_b, L0_gnn_stn4_w, L0_gnn_stn4_b, L0_gnn_conv_w, L0_gnn_conv_b), axis=-1)
    x = _layernorm(x + _L1_gnn_ref(x, edge_index, L1_gnn_W1, L1_gnn_a_src1, L1_gnn_a_dst1, L1_gnn_b1, L1_gnn_W2, L1_gnn_a_src2, L1_gnn_a_dst2, L1_gnn_b2, L1_gnn_W3, L1_gnn_a_src3, L1_gnn_a_dst3, L1_gnn_b3), axis=-1)
    x = _layernorm(x + _L2_gnn_ref(x, node_vec1, edge_index, L2_gnn_W1, L2_gnn_b1, L2_gnn_W2, L2_gnn_b2), axis=-1)
    x = _layernorm(x + _L3_gnn_ref(x, edge_index, 3), axis=-1)
    return x

_drawn_inputs = setup_inputs


def setup_inputs(seed=0):
    import zlib

    import numpy as np

    out = dict(_drawn_inputs(seed))
    spreads = {'L1_gnn_b1': (0.0, 2.0),
     'L1_gnn_b2': (0.0, 2.0),
     'L1_gnn_b3': (0.0, 2.0),
     'L2_gnn_b1': (0.0, 0.1),
     'L2_gnn_b2': (0.0, 0.1)}
    factors = {'node_vec1': 6.673,
     'L0_gnn_stn1_w': 8.0,
     'L0_gnn_stn1_b': 8.0,
     'L0_gnn_stn2_w': 8.0,
     'L0_gnn_stn2_b': 8.0,
     'L0_gnn_stn3_w': 8.0,
     'L0_gnn_stn3_b': 8.0,
     'L0_gnn_stn4_w': 8.0,
     'L0_gnn_stn4_b': 200.0,
     'L1_gnn_W1': 198.78,
     'L1_gnn_a_src1': 200.0,
     'L1_gnn_a_dst1': 200.0,
     'L1_gnn_W2': 200.0,
     'L1_gnn_a_src2': 197.145,
     'L1_gnn_a_dst2': 64.0,
     'L1_gnn_W3': 200.0,
     'L1_gnn_a_src3': 197.071,
     'L1_gnn_a_dst3': 64.0}
    for name, (base, spread) in spreads.items():
        noise = np.random.default_rng([zlib.crc32(name.encode()), seed]).standard_normal(out[name].shape)
        drawn = base * np.exp(spread * noise) if base else spread * noise
        out[name] = jnp.asarray(drawn.astype(out[name].dtype))
    for name, factor in factors.items():
        out[name] = (out[name] * factor).astype(out[name].dtype)
    return out
```

```python
import concourse.bass as bass
from concourse import mybir
from contextlib import ExitStack

F32 = mybir.dt.float32
I32 = mybir.dt.int32
BF16 = mybir.dt.bfloat16
ALU = mybir.AluOpType
ACT = mybir.ActivationFunctionType
AXX = mybir.AxisListType.X
RMAX = bass.bass_isa.ReduceOp.max
RADD = bass.bass_isa.ReduceOp.add
BIG = 3.0e38
P = 128


def gnn_stack_kernel(nc, t, out, stop=None):
    N, FX = t["x"].shape
    E = t["src"].shape[0]
    NT = 7 * -(-N // (7 * P))
    TB = 7
    NB = NT // TB
    NP = NT * P
    PAD = NP - 1
    J = 56 * -(-E // (56 * P))
    EP = J * P
    LASTP, LASTC = E // J, E % J
    CH = 28
    CC = 14
    BC = 56
    KD, D3 = 5, 3
    K3 = KD ** D3
    H1 = t["L0_gnn_stn1_w"].shape[2]
    NH, NC = t["L1_gnn_a_src1"].shape
    HC = NH * NC
    HW = NH + HC
    HW3 = NH + NH * HC
    HID = t["L2_gnn_W1"].shape[1]
    FG = FX + 1
    LOB = 6
    DLO = 1 << LOB
    DHI = NP // DLO
    DMP = EP + 1

    ctx = ExitStack()
    sems, counts = {}, {}

    def sem(name):
        if name not in sems:
            sems[name] = ctx.enter_context(nc.semaphore(name))
        return sems[name]

    class Counted:

        def __init__(self, name):
            self.sem, self.base = sem(name), 0

    def counted(name):
        if name not in counts:
            counts[name] = Counted(name)
        return counts[name]

    uid, n_sweeps = [0], [0]

    def sb(st, name, shape, dt=F32):
        uid[0] += 1
        return st.enter_context(nc.sbuf_tensor(f"{name}_{uid[0]}", shape, dt))

    def ps(st, name, shape, dt=F32):
        uid[0] += 1
        return st.enter_context(nc.psum_tensor(f"{name}_{uid[0]}", shape, dt))

    def dram(name, shape):
        return nc.dram_tensor(name, shape, F32, kind="Internal").ap()

    def edges_of(d, w):
        return d[0:EP, :].rearrange("(p j) w -> p j w", p=P)

    def nodes_of(d):
        return d.rearrange("(t p) w -> p t w", p=P)

    with ctx:
        sorted1 = dram("sorted1", [EP, 8])
        sorted2 = dram("sorted2", [EP, 8])
        run_basis = dram("run_basis", [EP + 1, P])
        run_stn2 = dram("run_stn2", [EP + 1, H1])
        run_conv = dram("run_conv", [EP + 1, FX])
        run_max = dram("run_max", [EP + 1, NH])
        run_gat = dram("run_gat", [EP + 1, HW])
        run_gat3 = dram("run_gat3", [EP + 1, HW3])
        run_gcn = dram("run_gcn", [EP + 1, FG])
        starts_t = dram("starts_t", [DMP + NP, 4])
        starts_h = dram("starts_h", [DMP + NP, NH])
        z_stn2 = dram("z_stn2", [NP * K3, H1])
        z_conv = dram("z_conv", [NP * K3, FX])
        tab_t = dram("tab_t", [NP, 4])
        tab_gat = dram("tab_gat", [NP, HW])
        tab_h = dram("tab_h", [NP, NH])
        tab_gcn1 = dram("tab_gcn1", [NP, FG])
        tab_gcn2 = dram("tab_gcn2", [NP, FX])

        dve_step, act_step, pe_step, pool_step = (sem(n) for n in ("dve_step", "act_step", "pe_step", "pool_step"))

        keep_all = ctx
        ident = sb(keep_all, "ident", [P, P])
        upper = sb(keep_all, "upper", [P, P])
        strict = sb(keep_all, "strict", [P, P])
        ones = sb(keep_all, "ones", [P, P])
        lane = sb(keep_all, "lane", [P, 1])
        iota = sb(keep_all, "iota", [P, TB * P])
        xcur = sb(keep_all, "xcur", [P, NT, FX])
        deg_d = sb(keep_all, "deg_d", [P, NT])
        end_d = sb(keep_all, "end_d", [P, NT], I32)
        start_d = sb(keep_all, "start_d", [P, NT], I32)
        src_d = sb(keep_all, "src_d", [P, J], I32)
        key_d = sb(keep_all, "key_d", [P, J])
        keep_d = sb(keep_all, "keep_d", [P, J])
        open_d = sb(keep_all, "open_d", [P, 1])
        head_d = sb(keep_all, "head_d", [P, 1], I32)

        weights = {}
        for name in ("L0_gnn_stn3_w", "L0_gnn_stn4_w", "L1_gnn_W1", "L1_gnn_W2", "L1_gnn_W3", "L2_gnn_W1", "L2_gnn_W2"):
            weights[name] = (t[name], sb(keep_all, name, list(t[name].shape)))
        w1 = t["L0_gnn_stn1_w"].rearrange("k i o -> k (i o)")
        weights["L0_gnn_stn1_w"] = (w1, sb(keep_all, "stn1_w", [K3, H1]))
        W3H = NH // 2 * HC
        w3rows = t["L1_gnn_W3"].rearrange("i (h o) -> h i o", h=NH)
        w3a = sb(keep_all, "w3a", [W3H, FX])
        w3b = sb(keep_all, "w3b", [W3H, FX])
        bcast = {}
        for name in ("L0_gnn_stn1_b", "L0_gnn_stn2_b", "L0_gnn_stn3_b", "L0_gnn_stn4_b", "L0_gnn_conv_b",
                     "L1_gnn_b1", "L1_gnn_b2", "L1_gnn_b3", "L2_gnn_b1", "L2_gnn_b2",
                     "L1_gnn_a_src1", "L1_gnn_a_dst1", "L1_gnn_a_src2", "L1_gnn_a_dst2", "L1_gnn_a_src3", "L1_gnn_a_dst3"):
            a = t[name]
            if len(a.shape) == 2:
                a = a.rearrange("h c -> (h c)")
            bcast[name] = (a, sb(keep_all, name, [P, a.shape[0]]))

        def W(name):
            return weights[name][1]

        def B(name):
            return bcast[name][1]

        def row(ap, shape):
            return ap[:, :].unsqueeze(1).to_broadcast(shape)


        def stage_constants(zeros, negs):
            with nc.Block() as block:
                c = counted("const_load")
                n_load = [0]

                @block.sync
                def _(sp):
                    def load(dst, src):
                        sp.dma_start(dst, src).then_inc(c.sem, 16)
                        n_load[0] += 1
                    for src, dst in weights.values():
                        load(dst[:, :], src)
                    for h in range(NH):
                        dst = w3a if h < NH // 2 else w3b
                        h0 = h % (NH // 2)
                        load(dst[h0 * HC:(h0 + 1) * HC, :], w3rows[h])
                    for src, dst in bcast.values():
                        load(dst[:, :], src.partition_broadcast(P))
                    sp.wait_ge(sem("x_zeroed"), 1)
                    sp.sem_inc(sem("x_zeroed"), -1)
                    full = N // P
                    load(xcur[:, 0:full, :], t["x"][0:full * P, :].rearrange("(t p) f -> p t f", p=P))
                    if N % P:
                        load(xcur[0:N % P, full, :], t["x"][full * P:N, :])
                    sp.wait_ge(sem("zeros_set"), 1)
                    sp.sem_inc(sem("zeros_set"), -1)
                    for d in (starts_t, starts_h):
                        w = d.shape[1]
                        load(edges_of(d, w).rearrange("p j w -> p (j w)"), zeros[:, 0:J * w])
                    for d in (run_basis, run_stn2, run_conv, run_gat, run_gat3, run_gcn):
                        load(d[EP:EP + 1, :], zeros[0:1, 0:d.shape[1]])
                    load(run_max[EP:EP + 1, :], negs[0:1, :])
                    sp.wait_ge(c.sem, 16 * n_load[0])
                    c.base += 16 * n_load[0]

                @block.vector
                def _(v):
                    v.memset(xcur[:, :, :], 0.0).then_inc(dve_step, 1)
                    v.wait_ge(dve_step, 1)
                    v.sem_inc(dve_step, -1)
                    v.sem_inc(sem("x_zeroed"), 1)
                    v.memset(negs[:, :], -BIG)
                    v.memset(zeros[:, :], 0.0).then_inc(dve_step, 1)
                    v.wait_ge(dve_step, 1)
                    v.sem_inc(dve_step, -1)
                    v.sem_inc(sem("zeros_set"), 1)

                @block.gpsimd
                def _(g):
                    g.iota(iota[:, :], pattern=[[1, TB * P]], base=0, channel_multiplier=0,
                           allow_small_or_imprecise_dtypes=True)
                    g.iota(lane[:, :], pattern=[[0, 1]], base=0, channel_multiplier=1,
                           allow_small_or_imprecise_dtypes=True)
                    g.memset(ones[:, :], 1.0).then_inc(pool_step, 1)
                    g.wait_ge(pool_step, 1)
                    g.sem_inc(pool_step, -1)
                    g.affine_select(out=upper[:, :], in_=ones[:, :], compare_op=ALU.is_ge, fill=0.0,
                                    base=0, pattern=[[1, P]], channel_multiplier=-1)
                    g.affine_select(out=strict[:, :], in_=ones[:, :], compare_op=ALU.is_gt, fill=0.0,
                                    base=0, pattern=[[1, P]], channel_multiplier=-1)
                    g.affine_select(out=ident[:, :], in_=ones[:, :], compare_op=ALU.is_equal,
                                    fill=0.0, base=0, pattern=[[1, P]], channel_multiplier=-1).then_inc(pool_step, 1)
                    g.wait_ge(pool_step, 1)
                    g.sem_inc(pool_step, -1)

        def stage_load_edges(src_f, dst_f, pseudo, src_i, dst_i):
            with nc.Block() as block:
                c = counted("edge_load")

                @block.sync
                def _(sp):
                    sp.wait_ge(sem("edges_padded"), 1)
                    sp.sem_inc(sem("edges_padded"), -1)
                    k = 0
                    for dst, s in ((src_i, t["src"]), (dst_i, t["dst"])):
                        sp.dma_start(dst[0:LASTP, :], s[0:LASTP * J].rearrange("(p j) -> p j", j=J)).then_inc(c.sem, 16)
                        sp.dma_start(dst[LASTP:LASTP + 1, 0:LASTC],
                                     s[LASTP * J:E].rearrange("(p j) -> p j", p=1)).then_inc(c.sem, 16)
                        k += 2
                    a = t["edge_attr_3"]
                    sp.dma_start(pseudo[0:LASTP, :, :], a[0:LASTP * J, :].rearrange("(p j) w -> p j w", j=J)).then_inc(c.sem, 16)
                    sp.dma_start(pseudo[LASTP:LASTP + 1, 0:LASTC, :],
                                 a[LASTP * J:E, :].rearrange("(p j) w -> p j w", p=1)).then_inc(c.sem, 16)
                    sp.wait_ge(c.sem, 16 * (k + 2))
                    sp.sem_inc(sem("edges_in"), 1)

                @block.vector
                def _(v):
                    v.memset(src_i[:, :], PAD)
                    v.memset(dst_i[:, :], PAD)
                    v.memset(pseudo[:, :, :], 0.0).then_inc(dve_step, 1)
                    v.wait_ge(dve_step, 1)
                    v.sem_inc(dve_step, -1)
                    v.sem_inc(sem("edges_padded"), 1)
                    v.wait_ge(sem("edges_in"), 1)
                    v.sem_inc(sem("edges_in"), -1)
                    v.tensor_copy(src_f[:, :], src_i[:, :])
                    v.tensor_copy(dst_f[:, :], dst_i[:, :]).then_inc(dve_step, 1)
                    v.wait_ge(dve_step, 1)
                    v.sem_inc(dve_step, -1)

        def stage_histogram(key_i, deg):
            with ExitStack() as st, nc.Block() as block:
                lo = sb(st, "lo", [P, J], I32)
                hi = sb(st, "hi", [P, J], I32)
                lo_f = sb(st, "lo_f", [P, J])
                hi_f = sb(st, "hi_f", [P, J])
                hot_lo = sb(st, "hot_lo", [P, CH, P], BF16)
                hot_hi = sb(st, "hot_hi", [P, CH, NT], BF16)
                part = ps(st, "part", [P, NT])
                made, counted_, = sem("hot_made"), sem("hot_counted")

                @block.vector
                def _(v):
                    v.memset(deg[:, :], 0.0)
                    v.tensor_scalar(lo[:, :], key_i[:, :], P - 1, None, ALU.bitwise_and)
                    v.tensor_scalar(hi[:, :], key_i[:, :], 7, None, ALU.logical_shift_right).then_inc(dve_step, 1)
                    v.wait_ge(dve_step, 1)
                    v.sem_inc(dve_step, -1)
                    v.tensor_copy(lo_f[:, :], lo[:, :])
                    v.tensor_copy(hi_f[:, :], hi[:, :]).then_inc(dve_step, 1)
                    v.wait_ge(dve_step, 1)
                    v.sem_inc(dve_step, -1)
                    with v.Fori(0, J // CH) as it:
                        v.tensor_tensor(hot_lo[:, :, :], lo_f[:, bass.ds(it * CH, CH)].unsqueeze(2).to_broadcast([P, CH, P]),
                                        iota[:, 0:P].unsqueeze(1).to_broadcast([P, CH, P]), ALU.is_equal)
                        v.tensor_tensor(
         hot_hi[:, :, :], hi_f[:, bass.ds(it * CH, CH)].unsqueeze(2).to_broadcast([P, CH, NT]),
         iota[:, 0:NT].unsqueeze(1).to_broadcast([P, CH, NT]), ALU.is_equal).then_inc(dve_step, 1)
                        v.wait_ge(dve_step, 1)
                        v.sem_inc(dve_step, -1)
                        v.sem_inc(made, 1)
                        v.wait_ge(counted_, 1)
                        v.sem_inc(counted_, -1)
                        v.tensor_tensor(deg[:, :], deg[:, :], part[:, :], ALU.add).then_inc(dve_step, 1)
                        v.wait_ge(dve_step, 1)
                        v.sem_inc(dve_step, -1)

                @block.tensor
                def _(pe):
                    with pe.Fori(0, J // CH):
                        pe.wait_ge(made, 1)
                        pe.sem_inc(made, -1)
                        for c in range(CH):
                            last = pe.matmul(part[:, :], hot_lo[:, c, :], hot_hi[:, c, :], start=(c == 0), stop=(c == CH - 1))
                        last.then_inc(counted_, 1)

        def stage_bounds(deg, end_i, start_i):
            with ExitStack() as st, nc.Block() as block:
                within = ps(st, "within", [P, NT])
                total = ps(st, "total", [P, NT])
                run = sb(st, "run", [P, NT])
                tot = sb(st, "tot", [P, NT])
                has = sb(st, "has", [P, NT])
                fin = sb(st, "fin", [P, NT])
                beg = sb(st, "beg", [P, NT])
                zero = sb(st, "zero", [P, NT])
                dump = sb(st, "dump", [P, NT])
                summed = sem("bounds_summed")

                @block.tensor
                def _(pe):
                    pe.matmul(within[:, :], upper[:, :], deg[:, :], start=True, stop=True)
                    pe.matmul(total[:, :], ones[:, :], deg[:, :], start=True, stop=True).then_inc(summed, 1)

                @block.vector
                def _(v):
                    v.memset(zero[:, :], 0.0)
                    v.tensor_scalar(dump[:, :], iota[:, 0:NT], float(P), float(DMP), ALU.mult, ALU.add).then_inc(dve_step, 1)
                    v.wait_ge(dve_step, 1)
                    v.sem_inc(dve_step, -1)
                    v.tensor_scalar(dump[:, :], dump[:, :], lane[:, 0:1], None, ALU.add)
                    v.tensor_scalar(has[:, :], deg[:, :], 0.5, None, ALU.is_gt).then_inc(dve_step, 1)
                    v.wait_ge(dve_step, 1)
                    v.sem_inc(dve_step, -1)
                    v.wait_ge(summed, 1)
                    v.sem_inc(summed, -1)
                    v.tensor_copy(tot[:, :], total[:, :]).then_inc(dve_step, 1)
                    v.wait_ge(dve_step, 1)
                    v.sem_inc(dve_step, -1)
                    v.tensor_tensor_scan(run[:, :], tot[:, :], zero[:, :], 0.0, ALU.add, ALU.add).then_inc(dve_step, 1)
                    v.wait_ge(dve_step, 1)
                    v.sem_inc(dve_step, -1)
                    v.tensor_tensor(run[:, :], run[:, :], tot[:, :], ALU.subtract).then_inc(dve_step, 1)
                    v.wait_ge(dve_step, 1)
                    v.sem_inc(dve_step, -1)
                    v.tensor_tensor(fin[:, :], run[:, :], within[:, :], ALU.add).then_inc(dve_step, 1)
                    v.wait_ge(dve_step, 1)
                    v.sem_inc(dve_step, -1)
                    v.tensor_tensor(beg[:, :], fin[:, :], deg[:, :], ALU.subtract).then_inc(dve_step, 1)
                    v.wait_ge(dve_step, 1)
                    v.sem_inc(dve_step, -1)
                    v.tensor_scalar(fin[:, :], fin[:, :], -1.0 - EP, None, ALU.add)
                    v.tensor_tensor(beg[:, :], beg[:, :], dump[:, :], ALU.subtract).then_inc(dve_step, 1)
                    v.wait_ge(dve_step, 1)
                    v.sem_inc(dve_step, -1)
                    v.tensor_tensor(fin[:, :], fin[:, :], has[:, :], ALU.mult)
                    v.tensor_tensor(beg[:, :], beg[:, :], has[:, :], ALU.mult).then_inc(dve_step, 1)
                    v.wait_ge(dve_step, 1)
                    v.sem_inc(dve_step, -1)
                    v.tensor_scalar(end_i[:, :], fin[:, :], float(EP), None, ALU.add)
                    v.tensor_tensor(start_i[:, :], beg[:, :], dump[:, :], ALU.add).then_inc(dve_step, 1)
                    v.wait_ge(dve_step, 1)
                    v.sem_inc(dve_step, -1)

        def stage_order(key, next_head_src, next_is_int, keep, open_, head):
            with ExitStack() as st, nc.Block() as block:
                nxt_raw = sb(st, "nxt_raw", [P, 1], I32 if next_is_int else F32)
                nxt = sb(st, "nxt", [P, 1])
                same = sb(st, "same", [P, 1])
                c = counted("order_load")

                @block.sync
                def _(sp):
                    sp.wait_ge(sem("next_cleared"), 1)
                    sp.sem_inc(sem("next_cleared"), -1)
                    with nc.allow_non_contiguous_dma(reason="one value per partition"):
                        sp.dma_start(nxt_raw[0:P - 1, :], next_head_src).then_inc(c.sem, 16)
                    sp.wait_ge(c.sem, c.base + 16)
                    sp.sem_inc(sem("next_in"), 1)
                c.base += 16

                @block.vector
                def _(v):
                    v.memset(nxt_raw[:, :], -1).then_inc(dve_step, 1)
                    v.wait_ge(dve_step, 1)
                    v.sem_inc(dve_step, -1)
                    v.sem_inc(sem("next_cleared"), 1)
                    v.memset(keep[:, 0:1], 0.0)
                    v.tensor_copy(head[:, :], key[:, 0:1])
                    v.tensor_tensor(keep[:, 1:J], key[:, 1:J], key[:, 0:J - 1], ALU.is_equal)
                    v.wait_ge(sem("next_in"), 1)
                    v.sem_inc(sem("next_in"), -1)
                    v.tensor_copy(nxt[:, :], nxt_raw[:, :]).then_inc(dve_step, 1)
                    v.wait_ge(dve_step, 1)
                    v.sem_inc(dve_step, -1)
                    v.tensor_tensor(same[:, :], nxt[:, :], key[:, J - 1:J], ALU.is_equal).then_inc(dve_step, 1)
                    v.wait_ge(dve_step, 1)
                    v.sem_inc(dve_step, -1)
                    v.scalar_tensor_tensor(open_[:, :], key[:, J - 1:J], 1.0, same[:, :], ALU.add, ALU.mult).then_inc(dve_step, 1)
                    v.wait_ge(dve_step, 1)
                    v.sem_inc(dve_step, -1)
                    v.tensor_scalar(open_[:, :], open_[:, :], -1.0, None, ALU.add).then_inc(dve_step, 1)
                    v.wait_ge(dve_step, 1)
                    v.sem_inc(dve_step, -1)

        def stage_radix(payload, shift, bins, dest):
            with ExitStack() as st, nc.Block() as block:
                key_i = sb(st, "key_i", [P, J], I32)
                digit = sb(st, "digit", [P, J])
                nxt = sb(st, "nxt", [P, bins])
                total = sb(st, "total", [P, bins])
                zero = sb(st, "zero", [P, bins])
                junk = sb(st, "junk", [P, bins])
                hot = sb(st, "hot", [P, CH, bins])
                rank = [sb(st, f"rank{b}", [P, CH]) for b in range(2)]
                at = [sb(st, f"at{b}", [P, CH], I32) for b in range(2)]
                rows = [sb(st, f"rows{b}", [P, CH, 8]) for b in range(2)]
                below = ps(st, "below", [P, bins])
                every = ps(st, "every", [P, bins])
                c = [counted(f"scattered{b}") for b in range(2)]
                base = [k.base for k in c]
                steps = J // CH // 2

                @block.vector
                def _(v):
                    v.memset(nxt[:, :], 0.0)
                    v.memset(zero[:, :], 0.0)
                    v.tensor_copy(key_i[:, :], payload[:, :, 0]).then_inc(dve_step, 1)
                    v.wait_ge(dve_step, 1)
                    v.sem_inc(dve_step, -1)
                    if shift:
                        v.tensor_scalar(key_i[:, :], key_i[:, :], shift, None, ALU.logical_shift_right).then_inc(dve_step, 1)
                        v.wait_ge(dve_step, 1)
                        v.sem_inc(dve_step, -1)
                    else:
                        v.tensor_scalar(key_i[:, :], key_i[:, :], bins - 1, None, ALU.bitwise_and).then_inc(dve_step, 1)
                        v.wait_ge(dve_step, 1)
                        v.sem_inc(dve_step, -1)
                    v.tensor_copy(digit[:, :], key_i[:, :]).then_inc(dve_step, 1)
                    v.wait_ge(dve_step, 1)
                    v.sem_inc(dve_step, -1)
                    with v.Fori(0, J // CH) as it:
                        sh = [P, CH, bins]
                        v.tensor_tensor(hot[:, :, :], digit[:, bass.ds(it * CH, CH)].unsqueeze(2).to_broadcast(sh),
                                        iota[:, 0:bins].unsqueeze(1).to_broadcast(sh), ALU.is_equal).then_inc(dve_step, 1)
                        v.wait_ge(dve_step, 1)
                        v.sem_inc(dve_step, -1)
                        v.tensor_reduce(junk[:, :], hot[:, :, :].rearrange("p c k -> p k c"), AXX, ALU.add).then_inc(dve_step, 1)
                        v.wait_ge(dve_step, 1)
                        v.sem_inc(dve_step, -1)
                        v.tensor_tensor(nxt[:, :], nxt[:, :], junk[:, :], ALU.add).then_inc(dve_step, 1)
                        v.wait_ge(dve_step, 1)
                        v.sem_inc(dve_step, -1)
                    v.sem_inc(sem("digits_counted"), 1)
                    v.wait_ge(sem("digits_summed"), 1)
                    v.sem_inc(sem("digits_summed"), -1)
                    v.tensor_copy(total[:, :], every[:, :])
                    v.tensor_copy(nxt[:, :], below[:, :]).then_inc(dve_step, 1)
                    v.wait_ge(dve_step, 1)
                    v.sem_inc(dve_step, -1)
                    v.tensor_tensor_scan(junk[:, :], total[:, :], zero[:, :], 0.0, ALU.add, ALU.add).then_inc(dve_step, 1)
                    v.wait_ge(dve_step, 1)
                    v.sem_inc(dve_step, -1)
                    v.tensor_tensor(junk[:, :], junk[:, :], total[:, :], ALU.subtract).then_inc(dve_step, 1)
                    v.wait_ge(dve_step, 1)
                    v.sem_inc(dve_step, -1)
                    v.tensor_tensor(nxt[:, :], nxt[:, :], junk[:, :], ALU.add).then_inc(dve_step, 1)
                    v.wait_ge(dve_step, 1)
                    v.sem_inc(dve_step, -1)
                    with v.Fori(0, steps) as it:
                        for b in range(2):
                            for k in range(CH):
                                col = digit[:, bass.ds(it * (2 * CH) + (b * CH + k), 1)]
                                v.scalar_tensor_tensor(junk[:, :], iota[:, 0:bins], col, nxt[:, :], ALU.is_equal, ALU.mult,
                                                       accum_out=rank[b][:, k:k + 1])
                                v.scalar_tensor_tensor(
                 nxt[:, :], iota[:, 0:bins], col, nxt[:, :], ALU.is_equal, ALU.add).then_inc(dve_step, 1)
                                v.wait_ge(dve_step, 1)
                                v.sem_inc(dve_step, -1)
                            v.wait_ge(sem(f"rank_free{b}"), 1)
                            v.sem_inc(sem(f"rank_free{b}"), -1)
                            v.tensor_copy(rows[b][:, :, :], payload[:, bass.ds(it * (2 * CH) + b * CH, CH), :])
                            v.tensor_copy(at[b][:, :], rank[b][:, :]).then_inc(dve_step, 1)
                            v.wait_ge(dve_step, 1)
                            v.sem_inc(dve_step, -1)
                            v.sem_inc(sem(f"ranked{b}"), 1)

                @block.tensor
                def _(pe):
                    pe.wait_ge(sem("digits_counted"), 1)
                    pe.sem_inc(sem("digits_counted"), -1)
                    pe.matmul(below[:, :], strict[:, :], nxt[:, :], start=True, stop=True)
                    pe.matmul(every[:, :], ones[:, :], nxt[:, :], start=True, stop=True).then_inc(sem("digits_summed"), 1)

                @block.gpsimd
                def _(g):
                    with g.Fori(0, steps):
                        for b in range(2):
                            g.wait_ge(sem(f"ranked{b}"), 1)
                            g.sem_inc(sem(f"ranked{b}"), -1)
                            for k in range(CH):
                                g.indirect_dma_start(out=dest, out_offset=bass.IndirectOffsetOnAxis(ap=at[b][:, k:k + 1], axis=0),
                                                     in_=rows[b][:, k, :], in_offset=None).then_inc(c[b].sem, 16)

                @block.sync
                def _(sp):
                    for b in range(2):
                        sp.sem_inc(sem(f"rank_free{b}"), 1)
                    with sp.Fori(0, steps) as it:
                        for b in range(2):
                            sp.wait_ge(c[b].sem, it * (16 * CH) + (16 * CH + base[b]))
                            sp.sem_inc(sem(f"rank_free{b}"), 1)
                    for b in range(2):
                        sp.wait_ge(sem(f"rank_free{b}"), 1)
                        sp.sem_inc(sem(f"rank_free{b}"), -1)
                for k in c:
                    k.base += 16 * CH * steps

        def sweep(gathers, ch, chunk, store, setup=None):
            steps = J // ch // 2
            with ExitStack() as st, nc.Block() as block:
                at = [[sb(st, f"at{n}{b}", [P, ch], I32) for b in range(2)] for n in range(len(gathers))]
                c = [counted(f"gathered{b}_{n_sweeps[0] // 3}") for b in range(2)]
                n_sweeps[0] += bool(gathers)
                cs = [counted(f"stored{b}") for b in range(2)]
                base = [k.base for k in c]
                sbase = [k.base for k in cs]
                per = 16 * ch * len(gathers)

                @block.scalar
                def _(a):
                    if gathers:
                        with a.Fori(0, steps) as it:
                            for b in range(2):
                                a.wait_ge(sem(f"ring_free{b}"), 1)
                                a.sem_inc(sem(f"ring_free{b}"), -1)
                                for n, (_, idx, _, _) in enumerate(gathers):
                                    last = a.copy(at[n][b][:, :], idx[:, bass.ds(it * (2 * ch) + b * ch, ch)])
                                last.then_inc(act_step, 1)
                                a.wait_ge(act_step, 1)
                                a.sem_inc(act_step, -1)
                                a.sem_inc(sem(f"indices_staged{b}"), 1)
                        for b in range(2):
                            a.wait_ge(sem(f"ring_free{b}"), 1)
                            a.sem_inc(sem(f"ring_free{b}"), -1)

                @block.gpsimd
                def _(g):
                    if gathers:
                        with g.Fori(0, steps):
                            for b in range(2):
                                g.wait_ge(sem(f"indices_staged{b}"), 1)
                                g.sem_inc(sem(f"indices_staged{b}"), -1)
                                for k in range(ch):
                                    for n, (table, _, bufs, view) in enumerate(gathers):
                                        g.indirect_dma_start(
                                            out=view(bufs[b], k), out_offset=None, in_=table,
                                            in_offset=bass.IndirectOffsetOnAxis(ap=at[n][b][:, k:k + 1], axis=0)
                                        ).then_inc(c[b].sem, 16)

                @block.vector
                def _(v):
                    if setup:
                        setup(v)
                    with v.Fori(0, steps) as it:
                        for b in range(2):
                            if gathers:
                                v.wait_ge(c[b].sem, it * per + (per + base[b]))
                                v.sem_inc(dve_step, 1)
                                v.wait_ge(dve_step, 1)
                                v.sem_inc(dve_step, -1)
                            else:
                                v.wait_ge(sem(f"ring_free{b}"), 1)
                                v.sem_inc(sem(f"ring_free{b}"), -1)
                            chunk(v, b, it * (2 * ch) + b * ch)
                            v.sem_inc(sem(f"chunk_done{b}"), 1)
                    if not gathers:
                        for b in range(2):
                            v.wait_ge(sem(f"ring_free{b}"), 1)
                            v.sem_inc(sem(f"ring_free{b}"), -1)

                @block.sync
                def _(sp):
                    for b in range(2):
                        sp.sem_inc(sem(f"ring_free{b}"), 1)
                    with sp.Fori(0, steps) as it:
                        for b in range(2):
                            sp.wait_ge(sem(f"chunk_done{b}"), 1)
                            sp.sem_inc(sem(f"chunk_done{b}"), -1)
                            if store:
                                bufs, dest = store
                                w = dest.shape[1]
                                sp.dma_start(edges_of(dest, w)[:, bass.ds(it * (2 * ch) + b * ch, ch), :],
                                             bufs[b][:, :, 0:w]).then_inc(cs[b].sem, 16)
                                sp.wait_ge(cs[b].sem, it * 16 + (16 + sbase[b]))
                            sp.sem_inc(sem(f"ring_free{b}"), 1)
                if gathers:
                    for k in c:
                        k.base += per * steps
                if store:
                    for k in cs:
                        k.base += 16 * steps

        def running_sum(v, buf, carry, keep, col, ch):
            for f in range(buf.shape[2]):
                last = v.tensor_tensor_scan(buf[:, :, f], keep[:, bass.ds(col, ch)], buf[:, :, f], carry[:, f:f + 1],
                                            ALU.mult, ALU.add)
            last.then_inc(dve_step, 1)
            v.wait_ge(dve_step, 1)
            v.sem_inc(dve_step, -1)
            v.tensor_copy(carry[:, :], buf[:, ch - 1, :]).then_inc(dve_step, 1)
            v.wait_ge(dve_step, 1)
            v.sem_inc(dve_step, -1)

        def stage_ends(run, ends_i, open_, got, tail_rhs, tails):
            F = run.shape[1]
            FT = tail_rhs.shape[1]
            stride = P if FT <= P else 2 * P
            with ExitStack() as st, nc.Block() as block:
                hot = sb(st, "hot", [P, TB * P])
                rel = sb(st, "rel", [P, 1])
                acc = ps(st, "acc", [P, TB, stride])
                c = counted("ends_gathered")

                @block.gpsimd
                def _(g):
                    for k in range(NT):
                        g.indirect_dma_start(out=got[:, k, :], out_offset=None, in_=run,
                                             in_offset=bass.IndirectOffsetOnAxis(ap=ends_i[:, k:k + 1], axis=0)).then_inc(c.sem, 16)

                @block.vector
                def _(v):
                    v.tensor_copy(rel[:, :], open_[:, :]).then_inc(dve_step, 1)
                    v.wait_ge(dve_step, 1)
                    v.sem_inc(dve_step, -1)
                    with v.Fori(0, NB) as it:
                        v.tensor_scalar(hot[:, :], iota[:, :], rel[:, 0:1], None, ALU.is_equal).then_inc(dve_step, 1)
                        v.wait_ge(dve_step, 1)
                        v.sem_inc(dve_step, -1)
                        v.sem_inc(sem("hot_ready"), 1)
                        v.tensor_scalar(rel[:, :], rel[:, :], -float(TB * P), None, ALU.add).then_inc(dve_step, 1)
                        v.wait_ge(dve_step, 1)
                        v.sem_inc(dve_step, -1)
                        v.wait_ge(sem("tails_ready"), 1)
                        v.sem_inc(sem("tails_ready"), -1)
                        v.tensor_copy(tails[:, bass.ds(it * TB, TB), :], acc[:, :, 0:FT]).then_inc(dve_step, 1)
                        v.wait_ge(dve_step, 1)
                        v.sem_inc(dve_step, -1)

                @block.tensor
                def _(pe):
                    with pe.Fori(0, NB):
                        pe.wait_ge(sem("hot_ready"), 1)
                        pe.sem_inc(sem("hot_ready"), -1)
                        for k in range(TB):
                            last = pe.matmul(acc[:, k, 0:FT], hot[:, k * P:(k + 1) * P], tail_rhs, start=True, stop=True)
                        last.then_inc(sem("tails_ready"), 1)

                @block.sync
                def _(sp):
                    sp.wait_ge(c.sem, c.base + 16 * NT)
                c.base += 16 * NT

        def stage_linear(arr, parts, width, res):
            stride = P if width <= P else 2 * P
            F = arr.shape[2]
            with ExitStack() as st, nc.Block() as block:
                rows_ = sb(st, "rows_", [P, TB, F])
                turned = [sb(st, f"turned{n}", [hi - lo, TB, P]) for n, (lo, hi, _) in enumerate(parts)]
                tp = ps(st, "tp", [P, TB, P])
                acc = ps(st, "acc", [P, TB, stride])

                @block.tensor
                def _(pe):
                    with pe.Fori(0, NB):
                        pe.wait_ge(sem("rows_staged"), 1)
                        pe.sem_inc(sem("rows_staged"), -1)
                        for lo, hi, _ in parts:
                            for k in range(TB):
                                last = pe.transpose(tp[0:hi - lo, k, :], rows_[:, k, lo:hi], ident[:, :])
                            last.then_inc(sem("turned"), 1)
                            pe.wait_ge(sem("turned_copied"), 1)
                            pe.sem_inc(sem("turned_copied"), -1)
                        for k in range(TB):
                            for n, (_, _, w) in enumerate(parts):
                                last = pe.matmul(acc[:, k, 0:width], turned[n][:, k, :], w,
                                                 start=(n == 0), stop=(n == len(parts) - 1))
                        last.then_inc(sem("product_ready"), 1)
                        pe.wait_ge(sem("product_copied"), 1)
                        pe.sem_inc(sem("product_copied"), -1)

                @block.scalar
                def _(a):
                    with a.Fori(0, NB) as it:
                        a.copy(rows_[:, :, :], arr[:, bass.ds(it * TB, TB), :]).then_inc(act_step, 1)
                        a.wait_ge(act_step, 1)
                        a.sem_inc(act_step, -1)
                        a.sem_inc(sem("rows_staged"), 1)
                        for n, (lo, hi, _) in enumerate(parts):
                            a.wait_ge(sem("turned"), 1)
                            a.sem_inc(sem("turned"), -1)
                            a.copy(turned[n][:, :, :], tp[0:hi - lo, :, :]).then_inc(act_step, 1)
                            a.wait_ge(act_step, 1)
                            a.sem_inc(act_step, -1)
                            a.sem_inc(sem("turned_copied"), 1)

                @block.vector
                def _(v):
                    with v.Fori(0, NB) as it:
                        v.wait_ge(sem("product_ready"), 1)
                        v.sem_inc(sem("product_ready"), -1)
                        v.tensor_copy(res[:, bass.ds(it * TB, TB), 0:width], acc[:, :, 0:width]).then_inc(dve_step, 1)
                        v.wait_ge(dve_step, 1)
                        v.sem_inc(dve_step, -1)
                        v.sem_inc(sem("product_copied"), 1)

        def linear(arr, k_, w, width, res):
            stage_linear(arr, [(0, k_, w)], width, res)

        to_act, from_act = sem("to_act"), sem("from_act")

        def vector_stage(f, g=None):
            with nc.Block() as block:
                @block.vector
                def _(v):
                    f(v)

                @block.scalar
                def _(a):
                    if g:
                        g(a)

        def copy_out(pairs):
            with nc.Block() as block:
                c = counted("copied_out")

                @block.sync
                def _(sp):
                    for dst, src in pairs:
                        sp.dma_start(dst, src).then_inc(c.sem, 16)
                    sp.wait_ge(c.sem, c.base + 16 * len(pairs))
                c.base += 16 * len(pairs)

        def stage_elu(x):
            with ExitStack() as st, nc.Block() as block:
                low = sb(st, "low", list(x.shape))

                @block.vector
                def _(v):
                    v.tensor_scalar(low[:, :, :], x[:, :, :], 0.0, None, ALU.min).then_inc(dve_step, 1)
                    v.wait_ge(dve_step, 1)
                    v.sem_inc(dve_step, -1)
                    v.sem_inc(to_act, 1)
                    v.tensor_scalar(x[:, :, :], x[:, :, :], 0.0, -1.0, ALU.max, ALU.add).then_inc(dve_step, 1)
                    v.wait_ge(dve_step, 1)
                    v.sem_inc(dve_step, -1)
                    v.wait_ge(from_act, 1)
                    v.sem_inc(from_act, -1)
                    v.tensor_tensor(x[:, :, :], x[:, :, :], low[:, :, :], ALU.add).then_inc(dve_step, 1)
                    v.wait_ge(dve_step, 1)
                    v.sem_inc(dve_step, -1)

                @block.scalar
                def _(a):
                    a.wait_ge(to_act, 1)
                    a.sem_inc(to_act, -1)
                    a.activation(low[:, :, :], low[:, :, :], ACT.Exp).then_inc(act_step, 1)
                    a.wait_ge(act_step, 1)
                    a.sem_inc(act_step, -1)
                    a.sem_inc(from_act, 1)

        def stage_layernorm(add):
            with ExitStack() as st:
                sq = sb(st, "sq", [P, NT, FX])
                m = sb(st, "m", [P, NT])
                s = sb(st, "s", [P, NT])

                def f(v):
                    sh = [P, NT, FX]
                    v.tensor_tensor(xcur[:, :, :], xcur[:, :, :], add[:, :, :], ALU.add).then_inc(dve_step, 1)
                    v.wait_ge(dve_step, 1)
                    v.sem_inc(dve_step, -1)
                    v.tensor_reduce(m[:, :], xcur[:, :, :], AXX, ALU.add).then_inc(dve_step, 1)
                    v.wait_ge(dve_step, 1)
                    v.sem_inc(dve_step, -1)
                    v.tensor_scalar(m[:, :], m[:, :], 1.0 / FX, None, ALU.mult).then_inc(dve_step, 1)
                    v.wait_ge(dve_step, 1)
                    v.sem_inc(dve_step, -1)
                    v.tensor_tensor(xcur[:, :, :], xcur[:, :, :], m[:, :].unsqueeze(2).to_broadcast(sh), ALU.subtract).then_inc(dve_step, 1)
                    v.wait_ge(dve_step, 1)
                    v.sem_inc(dve_step, -1)
                    v.tensor_tensor(sq[:, :, :], xcur[:, :, :], xcur[:, :, :], ALU.mult).then_inc(dve_step, 1)
                    v.wait_ge(dve_step, 1)
                    v.sem_inc(dve_step, -1)
                    v.tensor_reduce(m[:, :], sq[:, :, :], AXX, ALU.add).then_inc(dve_step, 1)
                    v.wait_ge(dve_step, 1)
                    v.sem_inc(dve_step, -1)
                    v.tensor_scalar(m[:, :], m[:, :], 1.0 / FX, 1e-5, ALU.mult, ALU.add).then_inc(dve_step, 1)
                    v.wait_ge(dve_step, 1)
                    v.sem_inc(dve_step, -1)
                    v.sem_inc(to_act, 1)
                    v.wait_ge(from_act, 1)
                    v.sem_inc(from_act, -1)
                    v.reciprocal(s[:, :], s[:, :]).then_inc(dve_step, 1)
                    v.wait_ge(dve_step, 1)
                    v.sem_inc(dve_step, -1)
                    v.tensor_tensor(xcur[:, :, :], xcur[:, :, :], s[:, :].unsqueeze(2).to_broadcast(sh), ALU.mult).then_inc(dve_step, 1)
                    v.wait_ge(dve_step, 1)
                    v.sem_inc(dve_step, -1)

                def root(a):
                    a.wait_ge(to_act, 1)
                    a.sem_inc(to_act, -1)
                    a.activation(s[:, :], m[:, :], ACT.Sqrt).then_inc(act_step, 1)
                    a.wait_ge(act_step, 1)
                    a.sem_inc(act_step, -1)
                    a.sem_inc(from_act, 1)
                vector_stage(f, root)

        def stage_expand(rows, tab, starts, start_i, keep, head, spread):
            w = tab.shape[1]
            copy_out([(nodes_of(tab), rows[:, :, :])])
            with nc.Block() as block:
                c, cl = counted("starts_sent"), counted("starts_loaded")
                base = c.base

                @block.gpsimd
                def _(g):
                    g.indirect_dma_start(out=spread[:, 0, :], out_offset=None, in_=tab,
                                         in_offset=bass.IndirectOffsetOnAxis(ap=head[:, 0:1], axis=0)).then_inc(c.sem, 16)
                    for k in range(NT):
                        g.indirect_dma_start(out=starts, out_offset=bass.IndirectOffsetOnAxis(ap=start_i[:, k:k + 1], axis=0),
                                             in_=rows[:, k, :], in_offset=None).then_inc(c.sem, 16)

                @block.sync
                def _(sp):
                    sp.wait_ge(c.sem, base + 16 * (NT + 1))
                    sp.dma_start(spread[:, 1:J + 1, :], edges_of(starts, w)).then_inc(cl.sem, 16)
                    sp.wait_ge(cl.sem, cl.base + 16)
                    sp.sem_inc(sem("starts_in"), 1)
                c.base += 16 * (NT + 1)
                cl.base += 16

                @block.vector
                def _(v):
                    v.wait_ge(sem("starts_in"), 1)
                    v.sem_inc(sem("starts_in"), -1)
                    v.tensor_copy(spread[:, 1, :], spread[:, 0, :]).then_inc(dve_step, 1)
                    v.wait_ge(dve_step, 1)
                    v.sem_inc(dve_step, -1)
                    for f in range(w):
                        last = v.tensor_tensor_scan(spread[:, 2:J + 1, f], keep[:, 1:J], spread[:, 2:J + 1, f],
                                                    spread[:, 1, f:f + 1], ALU.mult, ALU.add)
                    last.then_inc(dve_step, 1)
                    v.wait_ge(dve_step, 1)
                    v.sem_inc(dve_step, -1)

        def column(buf, k):
            return buf[:, k, :]


        def spline_setup(pseudo, w8, base_i, dst_f):
            with ExitStack() as st:
                pos = sb(st, "pos", [P, J, D3])
                cell = sb(st, "cell", [P, J, D3])
                tmp = sb(st, "tmp", [P, J, D3])
                ix = sb(st, "ix", [P, J])

                def f(v):
                    v.tensor_scalar(pos[:, :, :], pseudo[:, :, 0:D3], float(KD - 1), None, ALU.mult).then_inc(dve_step, 1)
                    v.wait_ge(dve_step, 1)
                    v.sem_inc(dve_step, -1)
                    v.tensor_scalar(cell[:, :, :], pos[:, :, :], 1.0, None, ALU.is_ge).then_inc(dve_step, 1)
                    v.wait_ge(dve_step, 1)
                    v.sem_inc(dve_step, -1)
                    for k in range(2, KD - 1):
                        v.tensor_scalar(tmp[:, :, :], pos[:, :, :], float(k), None, ALU.is_ge).then_inc(dve_step, 1)
                        v.wait_ge(dve_step, 1)
                        v.sem_inc(dve_step, -1)
                        v.tensor_tensor(cell[:, :, :], cell[:, :, :], tmp[:, :, :], ALU.add).then_inc(dve_step, 1)
                        v.wait_ge(dve_step, 1)
                        v.sem_inc(dve_step, -1)
                    v.tensor_tensor(pos[:, :, :], pos[:, :, :], cell[:, :, :], ALU.subtract).then_inc(dve_step, 1)
                    v.wait_ge(dve_step, 1)
                    v.sem_inc(dve_step, -1)
                    v.tensor_scalar(tmp[:, :, :], pos[:, :, :], -1.0, 1.0, ALU.mult, ALU.add).then_inc(dve_step, 1)
                    v.wait_ge(dve_step, 1)
                    v.sem_inc(dve_step, -1)
                    wgt = (tmp, pos)
                    for a in range(2):
                        for b in range(2):
                            n = 4 * a + 2 * b
                            v.tensor_tensor(w8[:, :, n + 1], wgt[a][:, :, 0], wgt[b][:, :, 1], ALU.mult).then_inc(dve_step, 1)
                            v.wait_ge(dve_step, 1)
                            v.sem_inc(dve_step, -1)
                            v.tensor_tensor(w8[:, :, n], w8[:, :, n + 1], tmp[:, :, 2], ALU.mult).then_inc(dve_step, 1)
                            v.wait_ge(dve_step, 1)
                            v.sem_inc(dve_step, -1)
                            v.tensor_tensor(w8[:, :, n + 1], w8[:, :, n + 1], pos[:, :, 2], ALU.mult).then_inc(dve_step, 1)
                            v.wait_ge(dve_step, 1)
                            v.sem_inc(dve_step, -1)
                    v.tensor_scalar(ix[:, :], dst_f[:, :], float(K3), None, ALU.mult).then_inc(dve_step, 1)
                    v.wait_ge(dve_step, 1)
                    v.sem_inc(dve_step, -1)
                    for d, s in enumerate((KD * KD, KD, 1)):
                        v.scalar_tensor_tensor(ix[:, :], cell[:, :, d], float(s), ix[:, :], ALU.mult, ALU.add).then_inc(dve_step, 1)
                        v.wait_ge(dve_step, 1)
                        v.sem_inc(dve_step, -1)
                    v.tensor_copy(base_i[0][:, :], ix[:, :])
                    v.tensor_scalar(base_i[1][:, :], ix[:, :], float(KD * KD), None, ALU.add).then_inc(dve_step, 1)
                    v.wait_ge(dve_step, 1)
                    v.sem_inc(dve_step, -1)
                vector_stage(f)

        def stage_z(arr, kin, w_dram, fo, z):
            cols = K3 * fo
            half = cols // 2
            wide = 500
            per = half // wide
            zv = z.rearrange("(t p k) o -> p t (k o)", p=P, k=K3)
            with ExitStack() as st, nc.Block() as block:
                wsb = sb(st, "wsb", [P, K3, fo])
                zb = [sb(st, f"zb{b}", [P, half]) for b in range(2)]
                tile_ = sb(st, "tile_", [P, kin])
                tile_t = sb(st, "tile_t", [P, P])
                acc = ps(st, "acc", [P, 8, 512])
                wf = wsb[:, :, :].rearrange("i k o -> i (k o)")
                cw, cz = counted("z_weights"), [counted(f"z_stored{b}") for b in range(2)]
                base = [k.base for k in cz]

                @block.sync
                def _(sp):
                    sp.wait_ge(sem("z_cleared"), 1)
                    sp.sem_inc(sem("z_cleared"), -1)
                    sp.dma_start(wsb[0:kin, :, :], w_dram.rearrange("k i o -> i k o")).then_inc(cw.sem, 16)
                    sp.wait_ge(cw.sem, cw.base + 16)
                    sp.sem_inc(sem("z_weights_in"), 1)
                    for b in range(2):
                        sp.sem_inc(sem(f"z_free_act{b}"), 1)
                        sp.sem_inc(sem(f"z_free_dve{b}"), 1)
                    with sp.Fori(0, NT) as it:
                        for b in range(2):
                            sp.wait_ge(sem(f"z_done{b}"), 2)
                            sp.sem_inc(sem(f"z_done{b}"), -2)
                            sp.dma_start(zv[:, bass.ds(it, 1), b * half:(b + 1) * half],
                                         zb[b][:, :].unsqueeze(1)).then_inc(cz[b].sem, 16)
                        for b in range(2):
                            sp.wait_ge(cz[b].sem, it * 16 + (16 + base[b]))
                            sp.sem_inc(sem(f"z_free_act{b}"), 1)
                            sp.wait_ge(cz[b].sem, it * 16 + (16 + base[b]))
                            sp.sem_inc(sem(f"z_free_dve{b}"), 1)
                    for b in range(2):
                        sp.wait_ge(sem(f"z_free_act{b}"), 1)
                        sp.sem_inc(sem(f"z_free_act{b}"), -1)
                        sp.wait_ge(sem(f"z_free_dve{b}"), 1)
                        sp.sem_inc(sem(f"z_free_dve{b}"), -1)

                @block.tensor
                def _(pe):
                    pe.wait_ge(sem("z_weights_in"), 1)
                    pe.sem_inc(sem("z_weights_in"), -1)
                    with pe.Fori(0, NT):
                        pe.wait_ge(sem("z_tile_in"), 1)
                        pe.sem_inc(sem("z_tile_in"), -1)
                        pe.wait_ge(sem("z_bank_free0"), 1)
                        pe.sem_inc(sem("z_bank_free0"), -1)
                        pe.transpose(acc[0:kin, 0, 0:P], tile_[:, :], ident[:, :]).then_inc(sem("z_tile_turned"), 1)
                        pe.wait_ge(sem("z_tile_ready"), 1)
                        pe.sem_inc(sem("z_tile_ready"), -1)
                        for b in range(2):
                            for n in range(per):
                                q = b * per + n
                                if q:
                                    pe.wait_ge(sem(f"z_bank_free{q % 8}"), 1)
                                    pe.sem_inc(sem(f"z_bank_free{q % 8}"), -1)
                                pe.matmul(acc[:, q % 8, 0:wide], tile_t[:, :], wf[:, q * wide:(q + 1) * wide],
                                          start=True, stop=True).then_inc(sem("z_for_act" if q % 2 else "z_for_dve"), 1)

                def drain(eng, own, parity, name, put):
                    with eng.Fori(0, NT) as it:
                        if parity:
                            put(tile_[:, :], arr[:, bass.ds(it, 1), :].rearrange("p o f -> p (o f)")).then_inc(own, 1)
                            eng.wait_ge(own, 1)
                            eng.sem_inc(own, -1)
                            eng.sem_inc(sem("z_tile_in"), 1)
                            eng.wait_ge(sem("z_tile_turned"), 1)
                            eng.sem_inc(sem("z_tile_turned"), -1)
                            put(tile_t[0:kin, :], acc[0:kin, 0, 0:P]).then_inc(own, 1)
                            eng.wait_ge(own, 1)
                            eng.sem_inc(own, -1)
                            eng.sem_inc(sem("z_tile_ready"), 1)
                        for b in range(2):
                            eng.wait_ge(sem(f"z_free_{name}{b}"), 1)
                            eng.sem_inc(sem(f"z_free_{name}{b}"), -1)
                            for n in range(per):
                                q = b * per + n
                                if q % 2 == parity:
                                    eng.wait_ge(sem(f"z_for_{name}"), 1)
                                    eng.sem_inc(sem(f"z_for_{name}"), -1)
                                    put(zb[b][:, n * wide:(n + 1) * wide], acc[:, q % 8, 0:wide]).then_inc(own, 1)
                                    eng.wait_ge(own, 1)
                                    eng.sem_inc(own, -1)
                                    eng.sem_inc(sem(f"z_bank_free{q % 8}"), 1)
                            eng.sem_inc(sem(f"z_done{b}"), 1)

                @block.vector
                def _(v):
                    v.memset(tile_t[:, :], 0.0)
                    v.memset(wsb[:, :, :], 0.0).then_inc(dve_step, 1)
                    v.wait_ge(dve_step, 1)
                    v.sem_inc(dve_step, -1)
                    v.sem_inc(sem("z_cleared"), 1)
                    v.sem_inc(sem("z_tile_cleared"), 1)
                    for q in range(8):
                        v.sem_inc(sem(f"z_bank_free{q}"), 1)
                    drain(v, dve_step, 0, "dve", v.tensor_copy)
                    for q in range(0, 8, 2):
                        v.wait_ge(sem(f"z_bank_free{q}"), 1)
                        v.sem_inc(sem(f"z_bank_free{q}"), -1)

                @block.scalar
                def _(a):
                    a.wait_ge(sem("z_tile_cleared"), 1)
                    a.sem_inc(sem("z_tile_cleared"), -1)
                    drain(a, act_step, 1, "act", a.copy)
                    for q in range(1, 8, 2):
                        a.wait_ge(sem(f"z_bank_free{q}"), 1)
                        a.sem_inc(sem(f"z_bank_free{q}"), -1)
                cw.base += 16
                for k in cz:
                    k.base += 16 * NT

        def stage_spline_sweep(z, fo, base_i, w8, keep, run, tail):
            wide = (KD + 2) * fo
            zrows = z
            with ExitStack() as st:
                ring = [sb(st, f"ring{b}", [P, CC, 2, wide]) for b in range(2)]
                msg = [sb(st, f"msg{b}", [P, CC, fo]) for b in range(2)]

                def setup(v):
                    v.memset(tail[:, :], 0.0).then_inc(dve_step, 1)
                    v.wait_ge(dve_step, 1)
                    v.sem_inc(dve_step, -1)

                def chunk(v, b, col):
                    pair = [[ring[b][:, :, n, m * KD * fo:(m * KD + 2) * fo].rearrange("p j (c o) -> p j c o", c=2)
                             for m in range(2)] for n in range(2)]
                    for n in range(2):
                        for m in range(2):
                            wgt = w8[:, bass.ds(col, CC), 4 * n + 2 * m:4 * n + 2 * m + 2]
                            last = v.tensor_tensor(pair[n][m], pair[n][m], wgt.unsqueeze(3).to_broadcast([P, CC, 2, fo]), ALU.mult)
                    last.then_inc(dve_step, 1)
                    v.wait_ge(dve_step, 1)
                    v.sem_inc(dve_step, -1)
                    v.tensor_tensor(pair[0][0], pair[0][0], pair[1][0], ALU.add)
                    v.tensor_tensor(pair[0][1], pair[0][1], pair[1][1], ALU.add).then_inc(dve_step, 1)
                    v.wait_ge(dve_step, 1)
                    v.sem_inc(dve_step, -1)
                    v.tensor_tensor(pair[0][0], pair[0][0], pair[0][1], ALU.add).then_inc(dve_step, 1)
                    v.wait_ge(dve_step, 1)
                    v.sem_inc(dve_step, -1)
                    v.tensor_tensor(msg[b][:, :, :], ring[b][:, :, 0, 0:fo], ring[b][:, :, 0, fo:2 * fo], ALU.add).then_inc(dve_step, 1)
                    v.wait_ge(dve_step, 1)
                    v.sem_inc(dve_step, -1)
                    running_sum(v, msg[b], tail, keep, col, CC)
                sweep([(zrows, base_i[n], ring, (lambda n: lambda buf, k: buf[:, k, n, :])(n)) for n in range(2)],
                      CC, chunk, (msg, run), setup)

        def node_sums(st, run, end_i, open_, tail, width):
            got = sb(st, "got", [P, NT, run.shape[1]])
            with ExitStack() as inner:
                tails = sb(inner, "tails", [P, NT, width])
                stage_ends(run, end_i, open_, got, tail[:, 0:width], tails)

                def add_tails(v):
                    v.tensor_tensor(got[:, :, 0:width], got[:, :, 0:width], tails[:, :, :], ALU.add).then_inc(dve_step, 1)
                    v.wait_ge(dve_step, 1)
                    v.sem_inc(dve_step, -1)
                vector_stage(add_tails)
            return got

        def program():
            with ExitStack() as st:
                zeros = sb(st, "zeros", [P, J * NH])
                negs = sb(st, "negs", [P, NH])
                stage_constants(zeros, negs)
            yield "constants"

            with ExitStack() as lay0:
                deg_s = sb(lay0, "deg_s", [P, NT])
                end_s = sb(lay0, "end_s", [P, NT], I32)
                start_s = sb(lay0, "start_s", [P, NT], I32)
                keep_s = sb(lay0, "keep_s", [P, J])
                open_s = sb(lay0, "open_s", [P, 1])
                head_s = sb(lay0, "head_s", [P, 1], I32)
                dst_s = sb(lay0, "dst_s", [P, J])
                pseudo = sb(lay0, "pseudo", [P, J, D3])
                with ExitStack() as srt:
                    src_f = sb(srt, "src_f", [P, J])
                    pseudo_in = sb(srt, "pseudo_in", [P, J, D3])
                    dst_i = sb(srt, "dst_i", [P, J], I32)
                    payload = sb(srt, "payload", [P, J, 8])
                    stage_load_edges(src_f, key_d, pseudo_in, src_d, dst_i)
                    stage_histogram(src_d, deg_s)
                    stage_histogram(dst_i, deg_d)
                    stage_bounds(deg_s, end_s, start_s)
                    stage_bounds(deg_d, end_d, start_d)
                    nxt = t["dst"].rearrange("(e o) -> e o", o=1)[J:E:J, :]
                    stage_order(key_d, nxt, True, keep_d, open_d, head_d)

                    def pack(v):
                        v.memset(payload[:, :, 5:8], 0.0)
                        v.tensor_copy(payload[:, :, 0], src_f[:, :])
                        v.tensor_copy(payload[:, :, 1], key_d[:, :])
                        v.tensor_copy(payload[:, :, 2:5], pseudo_in[:, :, :]).then_inc(dve_step, 1)
                        v.wait_ge(dve_step, 1)
                        v.sem_inc(dve_step, -1)
                    vector_stage(pack)
                    yield "loaded"
                    stage_radix(payload, 0, DLO, sorted1)
                    copy_out([(payload[:, :, :], edges_of(sorted1, 8))])
                    stage_radix(payload, LOB, DHI, sorted2)
                    copy_out([(payload[:, :, :], edges_of(sorted2, 8))])
                    stage_order(payload[:, :, 0], sorted2[J:EP, 0:1][0::J, :], False, keep_s, open_s, head_s)

                    def unpack(v):
                        v.tensor_copy(dst_s[:, :], payload[:, :, 1])
                        v.tensor_copy(pseudo[:, :, :], payload[:, :, 2:5]).then_inc(dve_step, 1)
                        v.wait_ge(dve_step, 1)
                        v.sem_inc(dve_step, -1)
                    vector_stage(unpack)
                yield "sorted"

                rdeg = sb(lay0, "rdeg", [P, NT])

                def inv_deg(v):
                    v.tensor_scalar(rdeg[:, :], deg_s[:, :], 1.0, None, ALU.max).then_inc(dve_step, 1)
                    v.wait_ge(dve_step, 1)
                    v.sem_inc(dve_step, -1)
                    v.reciprocal(rdeg[:, :], rdeg[:, :]).then_inc(dve_step, 1)
                    v.wait_ge(dve_step, 1)
                    v.sem_inc(dve_step, -1)
                vector_stage(inv_deg)

                def normed(v, x, bias, w):
                    sh = [P, NT, w]
                    v.tensor_tensor(x[:, :, :], x[:, :, :], rdeg[:, :].unsqueeze(2).to_broadcast(sh), ALU.mult).then_inc(dve_step, 1)
                    v.wait_ge(dve_step, 1)
                    v.sem_inc(dve_step, -1)
                    v.tensor_tensor(x[:, :, :], x[:, :, :], row(B(bias), sh), ALU.add).then_inc(dve_step, 1)
                    v.wait_ge(dve_step, 1)
                    v.sem_inc(dve_step, -1)

                h1 = sb(lay0, "h1", [P, NT, H1])
                with ExitStack() as st:
                    tail = sb(st, "tail", [P, P])
                    with ExitStack() as s2:
                        hat = sb(s2, "hat", [P, BC, D3, KD])
                        hat2 = sb(s2, "hat2", [P, BC, KD * KD])
                        pos = sb(s2, "pos", [P, BC, D3])
                        bas = [sb(s2, f"bas{b}", [P, BC, P]) for b in range(2)]

                        def setup(v):
                            v.memset(tail[:, :], 0.0)
                            v.memset(bas[0][:, :, :], 0.0)
                            v.memset(bas[1][:, :, :], 0.0).then_inc(dve_step, 1)
                            v.wait_ge(dve_step, 1)
                            v.sem_inc(dve_step, -1)

                        def chunk(v, b, col):
                            v.tensor_scalar(pos[:, :, :], pseudo[:, bass.ds(col, BC), :], float(KD - 1), None, ALU.mult).then_inc(dve_step, 1)
                            v.wait_ge(dve_step, 1)
                            v.sem_inc(dve_step, -1)
                            hatf = hat[:, :, :, :].rearrange("p c d k -> p (c d) k")
                            posf = pos[:, :, :].rearrange("p c d -> p (c d)")
                            v.tensor_tensor(hatf, posf.unsqueeze(2).to_broadcast([P, BC * D3, KD]),
                             iota[:, 0:KD].unsqueeze(1).to_broadcast([P, BC * D3, KD]), ALU.subtract).then_inc(dve_step, 1)
                            v.wait_ge(dve_step, 1)
                            v.sem_inc(dve_step, -1)
                            v.scalar_tensor_tensor(hatf, hatf, -1.0, hatf, ALU.mult, ALU.max).then_inc(dve_step, 1)
                            v.wait_ge(dve_step, 1)
                            v.sem_inc(dve_step, -1)
                            v.tensor_scalar(hatf, hatf, -1.0, 1.0, ALU.mult, ALU.add).then_inc(dve_step, 1)
                            v.wait_ge(dve_step, 1)
                            v.sem_inc(dve_step, -1)
                            v.tensor_scalar(hatf, hatf, 0.0, None, ALU.max).then_inc(dve_step, 1)
                            v.wait_ge(dve_step, 1)
                            v.sem_inc(dve_step, -1)
                            v.tensor_tensor(hat2[:, :, :].rearrange("p c (a b) -> p c a b", a=KD),
                             hat[:, :, 1, :].unsqueeze(3).to_broadcast([P, BC, KD, KD]),
                             hat[:, :, 2, :].unsqueeze(2).to_broadcast([P, BC, KD, KD]), ALU.mult).then_inc(dve_step, 1)
                            v.wait_ge(dve_step, 1)
                            v.sem_inc(dve_step, -1)
                            v.tensor_tensor(bas[b][:, :, 0:K3].rearrange("p c (a b) -> p c a b", a=KD),
                             hat[:, :, 0, :].unsqueeze(3).to_broadcast([P, BC, KD, KD * KD]),
                             hat2[:, :, :].unsqueeze(2).to_broadcast([P, BC, KD, KD * KD]), ALU.mult).then_inc(dve_step, 1)
                            v.wait_ge(dve_step, 1)
                            v.sem_inc(dve_step, -1)
                            running_sum(v, bas[b], tail, keep_s, col, BC)
                        sweep([], BC, chunk, (bas, run_basis), setup)
                    got = node_sums(st, run_basis, end_s, open_s, tail, K3)
                    yield "basis"
                    linear(got, K3, W("L0_gnn_stn1_w")[:, :], H1, h1)

                    def act1(v):
                        normed(v, h1, "L0_gnn_stn1_b", H1)
                    vector_stage(act1)
                    stage_elu(h1)
                yield "h1"
                w8 = sb(lay0, "w8", [P, J, 8])
                base_i = [sb(lay0, f"base{n}", [P, J], I32) for n in range(2)]
                stage_z(h1, H1, t["L0_gnn_stn2_w"], H1, z_stn2)
                spline_setup(pseudo, w8, base_i, dst_s)
                yield "z2"
                tt = sb(lay0, "tt", [P, NT, 4])
                with ExitStack() as st:
                    tail = sb(st, "tail", [P, H1])
                    stage_spline_sweep(z_stn2, H1, base_i, w8, keep_s, run_stn2, tail)
                    got = node_sums(st, run_stn2, end_s, open_s, tail, H1)

                    def act2(v):
                        normed(v, got, "L0_gnn_stn2_b", H1)
                    vector_stage(act2)
                    stage_elu(got)
                    linear(got, H1, W("L0_gnn_stn3_w")[:, :], H1, h1)

                    def act3(v):
                        v.tensor_tensor(h1[:, :, :], h1[:, :, :], row(B("L0_gnn_stn3_b"), [P, NT, H1]), ALU.add).then_inc(dve_step, 1)
                        v.wait_ge(dve_step, 1)
                        v.sem_inc(dve_step, -1)
                        v.memset(tt[:, :, :], 0.0).then_inc(dve_step, 1)
                        v.wait_ge(dve_step, 1)
                        v.sem_inc(dve_step, -1)
                    vector_stage(act3)
                    stage_elu(h1)
                    linear(h1, H1, W("L0_gnn_stn4_w")[:, :], D3, tt)

                    def bias4(v):
                        v.tensor_tensor(tt[:, :, 0:D3], tt[:, :, 0:D3], row(B("L0_gnn_stn4_b"), [P, NT, D3]), ALU.add).then_inc(dve_step, 1)
                        v.wait_ge(dve_step, 1)
                        v.sem_inc(dve_step, -1)
                    vector_stage(bias4)
                yield "t"
                with ExitStack() as st:
                    spread = sb(st, "spread", [P, J + 1, 4])
                    stage_expand(tt, tab_t, starts_t, start_s, keep_s, head_s, spread)
                    dst_si = sb(st, "dst_si", [P, J], I32)

                    def targets(v):
                        v.tensor_copy(dst_si[:, :], dst_s[:, :]).then_inc(dve_step, 1)
                        v.wait_ge(dve_step, 1)
                        v.sem_inc(dve_step, -1)
                    vector_stage(targets)
                    ring = [sb(st, f"ring{b}", [P, CH, 4]) for b in range(2)]

                    def chunk(v, b, col):
                        ptr = pseudo[:, bass.ds(col, CH), :]
                        v.tensor_tensor(ring[b][:, :, 0:D3], ring[b][:, :, 0:D3], ptr, ALU.add).then_inc(dve_step, 1)
                        v.wait_ge(dve_step, 1)
                        v.sem_inc(dve_step, -1)
                        v.tensor_tensor(ring[b][:, :, 0:D3], ring[b][:, :, 0:D3], spread[:, bass.ds(col + 1, CH), 0:D3], ALU.subtract).then_inc(dve_step, 1)
                        v.wait_ge(dve_step, 1)
                        v.sem_inc(dve_step, -1)
                        v.tensor_scalar(ptr, ring[b][:, :, 0:D3], 0.0, 1.0, ALU.max, ALU.min).then_inc(dve_step, 1)
                        v.wait_ge(dve_step, 1)
                        v.sem_inc(dve_step, -1)
                    sweep([(tab_t, dst_si, ring, column)], CH, chunk, None)
                stage_z(xcur, FX, t["L0_gnn_conv_w"], FX, z_conv)
                spline_setup(pseudo, w8, base_i, dst_s)
                yield "z3"
                with ExitStack() as st:
                    tail = sb(st, "tail", [P, FX])
                    stage_spline_sweep(z_conv, FX, base_i, w8, keep_s, run_conv, tail)
                    got = node_sums(st, run_conv, end_s, open_s, tail, FX)

                    def mean_bias(v):
                        normed(v, got, "L0_gnn_conv_b", FX)
                    vector_stage(mean_bias)
                    stage_layernorm(got)
            yield "layer0"

            with ExitStack() as lay1:
                neg_d = sb(lay1, "neg_d", [P, J])

                def marks(v):
                    v.tensor_scalar(neg_d[:, :], keep_d[:, :], -1.0, BIG, ALU.add, ALU.mult).then_inc(dve_step, 1)
                    v.wait_ge(dve_step, 1)
                    v.sem_inc(dve_step, -1)
                vector_stage(marks)
                h = sb(lay1, "h", [P, NT, HC])
                for layer in (1, 2, 3):
                    last = layer == 3
                    with ExitStack() as st:
                        vals = sb(st, "vals", [P, NT, HW])
                        al_d = sb(st, "al_d", [P, NT, NH])
                        mx = sb(st, "mx", [P, NT, NH])
                        e_self = sb(st, "e_self", [P, NT, NH])
                        width = NH * FX if last else HC
                        with ExitStack() as s2:
                            xw = sb(s2, "xw", [P, NT, width])
                            prod = sb(s2, "prod", [P, NT, width])
                            src_arr, k_in = (xcur, FX) if layer == 1 else (h, HC)
                            linear(src_arr, k_in, W(f"L1_gnn_W{layer}")[:, :], width, xw)

                            def terms(v):
                                sh = [P, NT, width]
                                per = width // NH
                                for name, res in (("src", vals[:, :, 0:NH]), ("dst", al_d[:, :, :])):
                                    v.tensor_tensor(prod[:, :, :], xw[:, :, :], row(B(f"L1_gnn_a_{name}{layer}"), sh), ALU.mult).then_inc(dve_step, 1)
                                    v.wait_ge(dve_step, 1)
                                    v.sem_inc(dve_step, -1)
                                    v.tensor_reduce(res, prod[:, :, :].rearrange("p t (h c) -> p t h c", h=NH), AXX, ALU.add).then_inc(dve_step, 1)
                                    v.wait_ge(dve_step, 1)
                                    v.sem_inc(dve_step, -1)
                                v.tensor_copy(vals[:, :, NH:HW], (h if last else xw)[:, :, :]).then_inc(dve_step, 1)
                                v.wait_ge(dve_step, 1)
                                v.sem_inc(dve_step, -1)
                                v.tensor_tensor(e_self[:, :, :], vals[:, :, 0:NH], al_d[:, :, :], ALU.add).then_inc(dve_step, 1)
                                v.wait_ge(dve_step, 1)
                                v.sem_inc(dve_step, -1)
                                v.scalar_tensor_tensor(e_self[:, :, :], e_self[:, :, :], 0.2, e_self[:, :, :], ALU.mult, ALU.max).then_inc(dve_step, 1)
                                v.wait_ge(dve_step, 1)
                                v.sem_inc(dve_step, -1)
                            vector_stage(terms)
                        copy_out([(nodes_of(tab_gat), vals[:, :, :])])
                        tail = sb(st, "tail", [P, HW3 if last else HW])
                        with ExitStack() as res:
                            edge = sb(res, "edge", [P, J, HW])
                            tmax = sb(res, "tmax", [P, NH])
                            per_edge = ExitStack()
                            spread = sb(per_edge, "spread", [P, J + 1, NH])
                            stage_expand(al_d, tab_h, starts_h, start_d, keep_d, head_d, spread)
                            with ExitStack() as s2:
                                ring = [sb(s2, f"ring{b}", [P, CH, HW]) for b in range(2)]
                                mxb = [sb(s2, f"mxb{b}", [P, CH, NH]) for b in range(2)]

                                def setup(v):
                                    v.memset(tmax[:, :], -BIG).then_inc(dve_step, 1)
                                    v.wait_ge(dve_step, 1)
                                    v.sem_inc(dve_step, -1)

                                def chunk(v, b, col):
                                    lg = edge[:, bass.ds(col, CH), 0:NH]
                                    v.tensor_copy(edge[:, bass.ds(col, CH), NH:HW], ring[b][:, :, NH:HW])
                                    v.tensor_tensor(ring[b][:, :, 0:NH], ring[b][:, :, 0:NH], spread[:, bass.ds(col + 1, CH), :], ALU.add).then_inc(dve_step, 1)
                                    v.wait_ge(dve_step, 1)
                                    v.sem_inc(dve_step, -1)
                                    v.scalar_tensor_tensor(lg, ring[b][:, :, 0:NH], 0.2, ring[b][:, :, 0:NH], ALU.mult, ALU.max).then_inc(dve_step, 1)
                                    v.wait_ge(dve_step, 1)
                                    v.sem_inc(dve_step, -1)
                                    for f in range(NH):
                                        scan = v.tensor_tensor_scan(mxb[b][:, :, f], neg_d[:, bass.ds(col, CH)],
                                                                    edge[:, bass.ds(col, CH), f:f + 1].rearrange("p j o -> p (j o)"),
                                                                    tmax[:, f:f + 1], ALU.add, ALU.max)
                                    scan.then_inc(dve_step, 1)
                                    v.wait_ge(dve_step, 1)
                                    v.sem_inc(dve_step, -1)
                                    v.tensor_copy(tmax[:, :], mxb[b][:, CH - 1, :]).then_inc(dve_step, 1)
                                    v.wait_ge(dve_step, 1)
                                    v.sem_inc(dve_step, -1)
                                sweep([(tab_gat, src_d, ring, column)], CH, chunk, (mxb, run_max), setup)
                            with ExitStack() as s2:
                                rhs = sb(s2, "rhs", [P, 2 * NH])
                                keys = sb(s2, "keys", [NH, P])
                                tmt = sb(s2, "tmt", [NH, P])
                                cut = sb(s2, "cut", [NH, P])
                                run2 = sb(s2, "run2", [NH, P])
                                lst = sb(s2, "lst", [NH, P])
                                with nc.Block() as block:
                                    a1 = ps(s2, "a1", [NH, P])
                                    a2 = ps(s2, "a2", [NH, P])
                                    a3 = ps(s2, "a3", [P, 2, 2 * NH])

                                    @block.tensor
                                    def _(pe):
                                        pe.transpose(a1[:, :], tmax[:, :], ident[:, :])
                                        pe.transpose(a2[:, :], open_d[:, 0:1].to_broadcast([P, NH]), ident[:, :]).then_inc(sem("tails_turned"), 1)
                                        pe.wait_ge(sem("tails_scanned"), 1)
                                        pe.sem_inc(sem("tails_scanned"), -1)
                                        pe.transpose(a3[:, 0, 0:NH], run2[:, :], ident[0:NH, 0:NH])
                                        pe.transpose(a3[:, 1, 0:NH], lst[:, :], ident[0:NH, 0:NH]).then_inc(sem("tails_back"), 1)

                                    @block.vector
                                    def _(v):
                                        v.wait_ge(sem("tails_turned"), 1)
                                        v.sem_inc(sem("tails_turned"), -1)
                                        v.tensor_copy(tmt[:, :], a1[:, :])
                                        v.memset(lst[:, :], 1.0)
                                        v.memset(cut[:, :], 0.0)
                                        v.tensor_copy(keys[:, :], a2[:, :]).then_inc(dve_step, 1)
                                        v.wait_ge(dve_step, 1)
                                        v.sem_inc(dve_step, -1)
                                        v.tensor_tensor(cut[:, 1:P], keys[:, 1:P], keys[:, 0:P - 1], ALU.is_equal)
                                        v.tensor_tensor(lst[:, 0:P - 1], keys[:, 1:P], keys[:, 0:P - 1], ALU.not_equal).then_inc(dve_step, 1)
                                        v.wait_ge(dve_step, 1)
                                        v.sem_inc(dve_step, -1)
                                        v.tensor_scalar(cut[:, :], cut[:, :], -1.0, BIG, ALU.add, ALU.mult).then_inc(dve_step, 1)
                                        v.wait_ge(dve_step, 1)
                                        v.sem_inc(dve_step, -1)
                                        v.tensor_tensor_scan(run2[:, :], cut[:, :], tmt[:, :], 0.0, ALU.add, ALU.max).then_inc(dve_step, 1)
                                        v.wait_ge(dve_step, 1)
                                        v.sem_inc(dve_step, -1)
                                        v.tensor_tensor(run2[:, :], run2[:, :], lst[:, :], ALU.mult).then_inc(dve_step, 1)
                                        v.wait_ge(dve_step, 1)
                                        v.sem_inc(dve_step, -1)
                                        v.sem_inc(sem("tails_scanned"), 1)
                                        v.wait_ge(sem("tails_back"), 1)
                                        v.sem_inc(sem("tails_back"), -1)
                                        v.tensor_copy(rhs[:, 0:NH], a3[:, 0, 0:NH])
                                        v.tensor_copy(rhs[:, NH:2 * NH], a3[:, 1, 0:NH]).then_inc(dve_step, 1)
                                        v.wait_ge(dve_step, 1)
                                        v.sem_inc(dve_step, -1)
                                tails = sb(s2, "tails", [P, NT, 2 * NH])
                                stage_ends(run_max, end_d, open_d, mx, rhs[:, :], tails)

                                def combine(v):
                                    v.tensor_scalar(tails[:, :, NH:2 * NH], tails[:, :, NH:2 * NH], -1.0, BIG, ALU.add, ALU.mult).then_inc(dve_step, 1)
                                    v.wait_ge(dve_step, 1)
                                    v.sem_inc(dve_step, -1)
                                    v.tensor_tensor(tails[:, :, 0:NH], tails[:, :, 0:NH], tails[:, :, NH:2 * NH], ALU.add).then_inc(dve_step, 1)
                                    v.wait_ge(dve_step, 1)
                                    v.sem_inc(dve_step, -1)
                                    v.tensor_tensor(mx[:, :, :], mx[:, :, :], tails[:, :, 0:NH], ALU.max).then_inc(dve_step, 1)
                                    v.wait_ge(dve_step, 1)
                                    v.sem_inc(dve_step, -1)
                                    v.tensor_tensor(mx[:, :, :], mx[:, :, :], e_self[:, :, :], ALU.max).then_inc(dve_step, 1)
                                    v.wait_ge(dve_step, 1)
                                    v.sem_inc(dve_step, -1)
                                    v.tensor_tensor(e_self[:, :, :], e_self[:, :, :], mx[:, :, :], ALU.subtract).then_inc(dve_step, 1)
                                    v.wait_ge(dve_step, 1)
                                    v.sem_inc(dve_step, -1)
                                    v.sem_inc(to_act, 1)

                                def exp_self(a):
                                    a.wait_ge(to_act, 1)
                                    a.sem_inc(to_act, -1)
                                    a.activation(e_self[:, :, :], e_self[:, :, :], ACT.Exp).then_inc(act_step, 1)
                                    a.wait_ge(act_step, 1)
                                    a.sem_inc(act_step, -1)
                                vector_stage(combine, exp_self)
                            stage_expand(mx, tab_h, starts_h, start_d, keep_d, head_d, spread)

                            def exps(v):
                                v.tensor_tensor(edge[:, :, 0:NH], edge[:, :, 0:NH], spread[:, 1:J + 1, :], ALU.subtract).then_inc(dve_step, 1)
                                v.wait_ge(dve_step, 1)
                                v.sem_inc(dve_step, -1)
                                v.sem_inc(to_act, 1)
                                v.wait_ge(from_act, 1)
                                v.sem_inc(from_act, -1)
                                if not last:
                                    ev = edge[:, :, NH:HW].rearrange("p j (h c) -> p j h c", h=NH)
                                    v.tensor_tensor(ev, ev, edge[:, :, 0:NH].unsqueeze(3).to_broadcast([P, J, NH, NC]), ALU.mult).then_inc(dve_step, 1)
                                    v.wait_ge(dve_step, 1)
                                    v.sem_inc(dve_step, -1)
                                    for f in range(HW):
                                        scan = v.tensor_tensor_scan(edge[:, :, f], keep_d[:, :], edge[:, :, f], 0.0, ALU.mult, ALU.add)
                                    scan.then_inc(dve_step, 1)
                                    v.wait_ge(dve_step, 1)
                                    v.sem_inc(dve_step, -1)
                                    v.tensor_copy(tail[:, :], edge[:, J - 1, :]).then_inc(dve_step, 1)
                                    v.wait_ge(dve_step, 1)
                                    v.sem_inc(dve_step, -1)

                            def exp_edges(a):
                                a.wait_ge(to_act, 1)
                                a.sem_inc(to_act, -1)
                                a.activation(edge[:, :, 0:NH], edge[:, :, 0:NH], ACT.Exp).then_inc(act_step, 1)
                                a.wait_ge(act_step, 1)
                                a.sem_inc(act_step, -1)
                                a.sem_inc(from_act, 1)
                            vector_stage(exps, exp_edges)
                            per_edge.close()
                            if not last:
                                copy_out([(edges_of(run_gat, HW), edge[:, :, :])])
                            else:
                                with ExitStack() as s2:
                                    halves = ((0, HW3 // 2), (HW3 // 2, HW3))
                                    half_done = [sem("half_done0"), sem("half_done1")]
                                    wv = [sb(s2, f"wv{b}", [P, 8, HW3]) for b in range(2)]

                                    def setup3(v):
                                        v.memset(tail[:, :], 0.0).then_inc(dve_step, 1)
                                        v.wait_ge(dve_step, 1)
                                        v.sem_inc(dve_step, -1)

                                    def chunk3(v, b, col):
                                        v.tensor_copy(wv[b][:, :, 0:NH], edge[:, bass.ds(col, 8), 0:NH])
                                        v.tensor_tensor(wv[b][:, :, NH:HW3].rearrange("p j (h c) -> p j h c", h=NH),
                                         edge[:, bass.ds(col, 8), 0:NH].unsqueeze(3).to_broadcast([P, 8, NH, HC]),
                                         edge[:, bass.ds(col, 8), NH:HW].unsqueeze(2).to_broadcast([P, 8, NH, HC]), ALU.mult).then_inc(dve_step, 1)
                                        v.wait_ge(dve_step, 1)
                                        v.sem_inc(dve_step, -1)
                                        for k in range(8):
                                            for n, (lo, hi) in enumerate(halves):
                                                prev = wv[b][:, k - 1, lo:hi] if k else tail[:, lo:hi]
                                                if k:
                                                    v.wait_ge(half_done[n], 1)
                                                    v.sem_inc(half_done[n], -1)
                                                v.scalar_tensor_tensor(wv[b][:, k, lo:hi], prev, keep_d[:, bass.ds(col + k, 1)],
                                                                       wv[b][:, k, lo:hi], ALU.mult, ALU.add).then_inc(half_done[n], 1)
                                        for n in range(2):
                                            v.wait_ge(half_done[n], 1)
                                            v.sem_inc(half_done[n], -1)
                                        v.tensor_copy(tail[:, :], wv[b][:, 7, :]).then_inc(dve_step, 1)
                                        v.wait_ge(dve_step, 1)
                                        v.sem_inc(dve_step, -1)
                                    sweep([], 8, chunk3, (wv, run_gat3), setup3)
                        width = HW3 if last else HW
                        got = node_sums(st, run_gat3 if last else run_gat, end_d, open_d, tail, width)
                        with ExitStack() as s2:
                            tmp = sb(s2, "tmp", [P, NT, width - NH])

                            def finish(v):
                                per = HC if last else NC
                                sh = [P, NT, NH, per]
                                tv = tmp[:, :, :].rearrange("p t (h c) -> p t h c", h=NH)
                                gv = got[:, :, NH:width].rearrange("p t (h c) -> p t h c", h=NH)
                                val = vals[:, :, NH:HW].unsqueeze(2).to_broadcast(sh) if last else \
                                    vals[:, :, NH:HW].rearrange("p t (h c) -> p t h c", h=NH)
                                v.tensor_tensor(tv, e_self[:, :, :].unsqueeze(3).to_broadcast(sh), val, ALU.mult).then_inc(dve_step, 1)
                                v.wait_ge(dve_step, 1)
                                v.sem_inc(dve_step, -1)
                                v.tensor_tensor(got[:, :, NH:width], got[:, :, NH:width], tmp[:, :, :], ALU.add).then_inc(dve_step, 1)
                                v.wait_ge(dve_step, 1)
                                v.sem_inc(dve_step, -1)
                                v.tensor_tensor(got[:, :, 0:NH], got[:, :, 0:NH], e_self[:, :, :], ALU.add).then_inc(dve_step, 1)
                                v.wait_ge(dve_step, 1)
                                v.sem_inc(dve_step, -1)
                                v.reciprocal(got[:, :, 0:NH], got[:, :, 0:NH]).then_inc(dve_step, 1)
                                v.wait_ge(dve_step, 1)
                                v.sem_inc(dve_step, -1)
                                v.tensor_tensor(gv, gv, got[:, :, 0:NH].unsqueeze(3).to_broadcast(sh), ALU.mult).then_inc(dve_step, 1)
                                v.wait_ge(dve_step, 1)
                                v.sem_inc(dve_step, -1)
                                if not last:
                                    v.tensor_tensor(h[:, :, :], got[:, :, NH:HW], row(B(f"L1_gnn_b{layer}"), [P, NT, HC]), ALU.add).then_inc(dve_step, 1)
                                    v.wait_ge(dve_step, 1)
                                    v.sem_inc(dve_step, -1)
                                    v.tensor_scalar(h[:, :, :], h[:, :, :], 0.0, None, ALU.max).then_inc(dve_step, 1)
                                    v.wait_ge(dve_step, 1)
                                    v.sem_inc(dve_step, -1)
                            vector_stage(finish)
                        if last:
                            o3 = sb(st, "o3", [P, NT, FX])
                            stage_linear(got, [(NH, NH + W3H, w3a[:, :]), (NH + W3H, HW3, w3b[:, :])], FX, o3)
                            full = N // P
                            y = sb(st, "y", [P, NT, FX])
                            m1 = sb(st, "m1", [P, FX])
                            m2 = sb(st, "m2", [P, FX])
                            with nc.Block() as block:
                                @block.vector
                                def _(v):
                                    sh = [P, NT, FX]
                                    v.tensor_scalar(o3[:, :, :], o3[:, :, :], 1.0 / NH, None, ALU.mult).then_inc(dve_step, 1)
                                    v.wait_ge(dve_step, 1)
                                    v.sem_inc(dve_step, -1)
                                    v.memset(y[:, :, :], -BIG).then_inc(dve_step, 1)
                                    v.wait_ge(dve_step, 1)
                                    v.sem_inc(dve_step, -1)
                                    v.tensor_tensor(y[:, 0:full, :], o3[:, 0:full, :], row(B("L1_gnn_b3"), [P, full, FX]), ALU.add)
                                    if N % P:
                                        q = N % P
                                        v.tensor_tensor(y[0:q, full, :], o3[0:q, full, :], B("L1_gnn_b3")[0:q, :], ALU.add)
                                    v.memset(m2[:, :], 0.0).then_inc(dve_step, 1)
                                    v.wait_ge(dve_step, 1)
                                    v.sem_inc(dve_step, -1)
                                    v.tensor_reduce(m1[:, :], y[:, :, :].rearrange("p t f -> p f t"), AXX, ALU.max).then_inc(dve_step, 1)
                                    v.wait_ge(dve_step, 1)
                                    v.sem_inc(dve_step, -1)
                                    v.sem_inc(sem("lane_max"), 1)
                                    v.wait_ge(sem("node_max"), 1)
                                    v.sem_inc(sem("node_max"), -1)
                                    v.tensor_tensor(y[:, :, :], y[:, :, :], row(m2, sh), ALU.subtract).then_inc(dve_step, 1)
                                    v.wait_ge(dve_step, 1)
                                    v.sem_inc(dve_step, -1)
                                    v.sem_inc(sem("shifted"), 1)
                                    v.wait_ge(sem("exp_done"), 1)
                                    v.sem_inc(sem("exp_done"), -1)
                                    v.tensor_reduce(m1[:, :], y[:, :, :].rearrange("p t f -> p f t"), AXX, ALU.add).then_inc(dve_step, 1)
                                    v.wait_ge(dve_step, 1)
                                    v.sem_inc(dve_step, -1)
                                    v.sem_inc(sem("lane_sum"), 1)
                                    v.wait_ge(sem("node_sum"), 1)
                                    v.sem_inc(sem("node_sum"), -1)
                                    v.reciprocal(m2[:, :], m2[:, :]).then_inc(dve_step, 1)
                                    v.wait_ge(dve_step, 1)
                                    v.sem_inc(dve_step, -1)
                                    v.tensor_tensor(y[:, :, :], y[:, :, :], row(m2, sh), ALU.mult).then_inc(dve_step, 1)
                                    v.wait_ge(dve_step, 1)
                                    v.sem_inc(dve_step, -1)

                                @block.scalar
                                def _(a):
                                    a.wait_ge(sem("shifted"), 1)
                                    a.sem_inc(sem("shifted"), -1)
                                    a.activation(y[:, :, :], y[:, :, :], ACT.Exp).then_inc(act_step, 1)
                                    a.wait_ge(act_step, 1)
                                    a.sem_inc(act_step, -1)
                                    a.sem_inc(sem("exp_done"), 1)

                                @block.gpsimd
                                def _(g):
                                    for op, need, done in ((RMAX, "lane_max", "node_max"), (RADD, "lane_sum", "node_sum")):
                                        g.wait_ge(sem(need), 1)
                                        g.sem_inc(sem(need), -1)
                                        g.partition_all_reduce(m2[:, :], m1[:, :], P, op).then_inc(pool_step, 1)
                                        g.wait_ge(pool_step, 1)
                                        g.sem_inc(pool_step, -1)
                                        g.sem_inc(sem(done), 1)
                            stage_layernorm(y)
                    yield f"gat{layer}"

            def gather_sums(st, rows, tab, run):
                w = tab.shape[1]
                copy_out([(nodes_of(tab), rows[:, :, :])])
                tail = sb(st, "tail", [P, w])
                with ExitStack() as s2:
                    ring = [sb(s2, f"ring{b}", [P, CH, w]) for b in range(2)]

                    def setup(v):
                        v.memset(tail[:, :], 0.0).then_inc(dve_step, 1)
                        v.wait_ge(dve_step, 1)
                        v.sem_inc(dve_step, -1)

                    def chunk(v, b, col):
                        running_sum(v, ring[b], tail, keep_d, col, CH)
                    sweep([(tab, src_d, ring, column)], CH, chunk, (ring, run), setup)
                return node_sums(st, run, end_d, open_d, tail, w)

            with ExitStack() as lay2:
                dinv = sb(lay2, "dinv", [P, NT])
                xn = sb(lay2, "xn", [P, NT, FG])
                g2 = sb(lay2, "g2", [P, NT, FX])
                with nc.Block() as block:
                    c = counted("vec_load")

                    @block.sync
                    def _(sp):
                        sp.wait_ge(sem("vec_zeroed"), 1)
                        sp.sem_inc(sem("vec_zeroed"), -1)
                        full = N // P
                        nv = t["node_vec1"]
                        with nc.allow_non_contiguous_dma(reason="one value per node"):
                            sp.dma_start(xn[:, 0:full, FX:FG], nv[0:full * P, :].rearrange("(t p) f -> p t f", p=P)).then_inc(c.sem, 16)
                            if N % P:
                                sp.dma_start(xn[0:N % P, full, FX:FG], nv[full * P:N, :]).then_inc(c.sem, 16)
                                c.base += 16
                        c.base += 16
                        sp.wait_ge(c.sem, c.base)

                    @block.vector
                    def _(v):
                        v.memset(xn[:, :, :], 0.0).then_inc(dve_step, 1)
                        v.wait_ge(dve_step, 1)
                        v.sem_inc(dve_step, -1)
                        v.sem_inc(sem("vec_zeroed"), 1)

                def scale_in(v):
                    v.tensor_copy(xn[:, :, 0:FX], xcur[:, :, :]).then_inc(dve_step, 1)
                    v.wait_ge(dve_step, 1)
                    v.sem_inc(dve_step, -1)
                    v.tensor_scalar(dinv[:, :], deg_d[:, :], 1.0, None, ALU.add).then_inc(dve_step, 1)
                    v.wait_ge(dve_step, 1)
                    v.sem_inc(dve_step, -1)
                    v.sem_inc(to_act, 1)
                    v.wait_ge(from_act, 1)
                    v.sem_inc(from_act, -1)
                    v.reciprocal(dinv[:, :], dinv[:, :]).then_inc(dve_step, 1)
                    v.wait_ge(dve_step, 1)
                    v.sem_inc(dve_step, -1)
                    v.tensor_tensor(xn[:, :, :], xn[:, :, :], dinv[:, :].unsqueeze(2).to_broadcast([P, NT, FG]), ALU.mult).then_inc(dve_step, 1)
                    v.wait_ge(dve_step, 1)
                    v.sem_inc(dve_step, -1)

                def root(a):
                    a.wait_ge(to_act, 1)
                    a.sem_inc(to_act, -1)
                    a.activation(dinv[:, :], dinv[:, :], ACT.Sqrt).then_inc(act_step, 1)
                    a.wait_ge(act_step, 1)
                    a.sem_inc(act_step, -1)
                    a.sem_inc(from_act, 1)
                vector_stage(scale_in, root)
                with ExitStack() as st:
                    got = gather_sums(st, xn, tab_gcn1, run_gcn)
                    hid = sb(st, "hid", [P, NT, HID])

                    def own(v):
                        v.tensor_tensor(got[:, :, :], got[:, :, :], xn[:, :, :], ALU.add).then_inc(dve_step, 1)
                        v.wait_ge(dve_step, 1)
                        v.sem_inc(dve_step, -1)
                        v.tensor_tensor(got[:, :, :], got[:, :, :], dinv[:, :].unsqueeze(2).to_broadcast([P, NT, FG]), ALU.mult).then_inc(dve_step, 1)
                        v.wait_ge(dve_step, 1)
                        v.sem_inc(dve_step, -1)
                    vector_stage(own)
                    linear(got, FG, W("L2_gnn_W1")[:, :], HID, hid)

                    def relu(v):
                        v.tensor_tensor(hid[:, :, :], hid[:, :, :], row(B("L2_gnn_b1"), [P, NT, HID]), ALU.add).then_inc(dve_step, 1)
                        v.wait_ge(dve_step, 1)
                        v.sem_inc(dve_step, -1)
                        v.tensor_scalar(hid[:, :, :], hid[:, :, :], 0.0, None, ALU.max).then_inc(dve_step, 1)
                        v.wait_ge(dve_step, 1)
                        v.sem_inc(dve_step, -1)
                    vector_stage(relu)
                    linear(hid, HID, W("L2_gnn_W2")[:, :], FX, g2)

                    def scale2(v):
                        v.tensor_tensor(g2[:, :, :], g2[:, :, :], dinv[:, :].unsqueeze(2).to_broadcast([P, NT, FX]), ALU.mult).then_inc(dve_step, 1)
                        v.wait_ge(dve_step, 1)
                        v.sem_inc(dve_step, -1)
                    vector_stage(scale2)
                with ExitStack() as st:
                    got = gather_sums(st, g2, tab_gcn2, run_conv)

                    def own2(v):
                        v.tensor_tensor(got[:, :, :], got[:, :, :], g2[:, :, :], ALU.add).then_inc(dve_step, 1)
                        v.wait_ge(dve_step, 1)
                        v.sem_inc(dve_step, -1)
                        v.tensor_tensor(got[:, :, :], got[:, :, :], dinv[:, :].unsqueeze(2).to_broadcast([P, NT, FX]), ALU.mult).then_inc(dve_step, 1)
                        v.wait_ge(dve_step, 1)
                        v.sem_inc(dve_step, -1)
                        v.tensor_tensor(got[:, :, :], got[:, :, :], row(B("L2_gnn_b2"), [P, NT, FX]), ALU.add).then_inc(dve_step, 1)
                        v.wait_ge(dve_step, 1)
                        v.sem_inc(dve_step, -1)
                    vector_stage(own2)
                    stage_layernorm(got)
            yield "gcn"

            with ExitStack() as lay3:
                rdeg = sb(lay3, "rdeg", [P, NT])
                hop = sb(lay3, "hop", [P, NT, FX])
                total = sb(lay3, "total", [P, NT, FX])

                def begin(v):
                    v.tensor_scalar(rdeg[:, :], deg_d[:, :], 1.0, None, ALU.max).then_inc(dve_step, 1)
                    v.wait_ge(dve_step, 1)
                    v.sem_inc(dve_step, -1)
                    v.reciprocal(rdeg[:, :], rdeg[:, :]).then_inc(dve_step, 1)
                    v.wait_ge(dve_step, 1)
                    v.sem_inc(dve_step, -1)
                    v.tensor_copy(hop[:, :, :], xcur[:, :, :])
                    v.tensor_scalar(total[:, :, :], xcur[:, :, :], 0.25, None, ALU.mult).then_inc(dve_step, 1)
                    v.wait_ge(dve_step, 1)
                    v.sem_inc(dve_step, -1)
                vector_stage(begin)
                for k in range(3):
                    with ExitStack() as st:
                        got = gather_sums(st, hop, tab_gcn2, run_conv)

                        def mean(v):
                            v.tensor_tensor(hop[:, :, :], got[:, :, :], rdeg[:, :].unsqueeze(2).to_broadcast([P, NT, FX]), ALU.mult).then_inc(dve_step, 1)
                            v.wait_ge(dve_step, 1)
                            v.sem_inc(dve_step, -1)
                            v.scalar_tensor_tensor(total[:, :, :], hop[:, :, :], 0.25, total[:, :, :], ALU.mult, ALU.add).then_inc(dve_step, 1)
                            v.wait_ge(dve_step, 1)
                            v.sem_inc(dve_step, -1)
                        vector_stage(mean)
                stage_layernorm(total)
            full = N // P
            pairs = [(out[0:full * P, :].rearrange("(t p) f -> p t f", p=P), xcur[:, 0:full, :])]
            if N % P:
                pairs.append((out[full * P:N, :], xcur[0:N % P, full, :]))
            copy_out(pairs)
            yield "out"

        steps = program()
        for name in steps:
            if name == stop:
                steps.close()
                break


_INS = ["x", "src", "dst", "edge_attr_3", "node_vec1",
        "L0_gnn_stn1_w", "L0_gnn_stn1_b", "L0_gnn_stn2_w", "L0_gnn_stn2_b", "L0_gnn_stn3_w", "L0_gnn_stn3_b",
        "L0_gnn_stn4_w", "L0_gnn_stn4_b", "L0_gnn_conv_w", "L0_gnn_conv_b",
        "L1_gnn_W1", "L1_gnn_a_src1", "L1_gnn_a_dst1", "L1_gnn_b1", "L1_gnn_W2", "L1_gnn_a_src2", "L1_gnn_a_dst2",
        "L1_gnn_b2", "L1_gnn_W3", "L1_gnn_a_src3", "L1_gnn_a_dst3", "L1_gnn_b3",
        "L2_gnn_W1", "L2_gnn_b1", "L2_gnn_W2", "L2_gnn_b2"]


def kernel(**inputs):
    import numpy as _np
    import concourse.bacc as _bacc
    from concourse import mybir as _mybir
    from concourse.bass_utils import run_bass_kernel_spmd as _run

    nc = _bacc.Bacc("TRN2", target_bir_lowering=False, num_devices=1)
    arrays, args = {}, {}
    for name in _INS:
        a = _np.ascontiguousarray(inputs[name])
        arrays[f"in_{name}"] = a
        args[name] = nc.dram_tensor(f"in_{name}", a.shape, _mybir.dt.from_np(a.dtype), kind="ExternalInput").ap()
    out = nc.dram_tensor("out_0", inputs["x"].shape, _mybir.dt.float32, kind="ExternalOutput").ap()
    gnn_stack_kernel(nc, args, out)
    r = _run(nc, [arrays], core_ids=[0])
    return r.results[0]["out_0"]
```

```python
import concourse.bass as bass
from concourse import mybir
from contextlib import ExitStack

F32 = mybir.dt.float32
I32 = mybir.dt.int32
BF16 = mybir.dt.bfloat16
ALU = mybir.AluOpType
ACT = mybir.ActivationFunctionType
AXX = mybir.AxisListType.X
RMAX = bass.bass_isa.ReduceOp.max
RADD = bass.bass_isa.ReduceOp.add
BIG = 3.0e38
P = 128


def gnn_stack_kernel(nc, t, out, stop=None):
    N, FX = t["x"].shape
    E = t["src"].shape[0]
    NT = 7 * -(-N // (7 * P))
    TB = 7
    NB = NT // TB
    NP = NT * P
    PAD = NP - 1
    J = 56 * -(-E // (56 * P))
    EP = J * P
    LASTP, LASTC = E // J, E % J
    CH = 28
    CC = 14
    BC = 56
    KD, D3 = 5, 3
    K3 = KD ** D3
    K3P = (KD - 1) * KD * KD
    H1 = t["L0_gnn_stn1_w"].shape[2]
    NH, NC = t["L1_gnn_a_src1"].shape
    HC = NH * NC
    HW = NH + HC
    HW3 = NH + NH * HC
    HID = t["L2_gnn_W1"].shape[1]
    FG = FX + 1
    LOB = 6
    DLO = 1 << LOB
    DHI = NP // DLO
    DMP = EP + 1

    ctx = ExitStack()
    sems, counts = {}, {}

    def sem(name):
        if name not in sems:
            sems[name] = ctx.enter_context(nc.semaphore(name))
        return sems[name]

    class Counted:

        def __init__(self, name):
            self.sem, self.base = sem(name), 0

    def counted(name):
        if name not in counts:
            counts[name] = Counted(name)
        return counts[name]

    uid, n_sweeps = [0], [0]

    def sb(st, name, shape, dt=F32):
        uid[0] += 1
        return st.enter_context(nc.sbuf_tensor(f"{name}_{uid[0]}", shape, dt))

    def ps(st, name, shape, dt=F32):
        uid[0] += 1
        return st.enter_context(nc.psum_tensor(f"{name}_{uid[0]}", shape, dt))

    def dram(name, shape):
        return nc.dram_tensor(name, shape, F32, kind="Internal").ap()

    def edges_of(d, w):
        return d[0:EP, :].rearrange("(p j) w -> p j w", p=P)

    def nodes_of(d):
        return d.rearrange("(t p) w -> p t w", p=P)

    with ctx:
        sorted1 = dram("sorted1", [EP, 8])
        sorted2 = dram("sorted2", [EP, 8])
        run_basis = dram("run_basis", [EP + 1, P])
        run_stn2 = dram("run_stn2", [EP + 1, H1])
        run_conv = dram("run_conv", [EP + 1, FX])
        run_max = dram("run_max", [EP + 1, NH])
        run_gat = dram("run_gat", [EP + 1, HW])
        run_gat3 = dram("run_gat3", [EP + 1, HW3])
        run_gcn = dram("run_gcn", [EP + 1, FG])
        starts_t = dram("starts_t", [DMP + NP, 4])
        starts_h = dram("starts_h", [DMP + NP, NH])
        z_stn2 = dram("z_stn2", [NP * K3, H1])
        z_conv = dram("z_conv", [NP * K3P, 2 * FX])
        tab_t = dram("tab_t", [NP, 4])
        tab_gat = dram("tab_gat", [NP, HW])
        tab_h = dram("tab_h", [NP, NH])
        tab_gcn1 = dram("tab_gcn1", [NP, FG])
        tab_gcn2 = dram("tab_gcn2", [NP, FX])

        dve_step, act_step, pe_step, pool_step = (sem(n) for n in ("dve_step", "act_step", "pe_step", "pool_step"))

        keep_all = ctx
        ident = sb(keep_all, "ident", [P, P])
        upper = sb(keep_all, "upper", [P, P])
        strict = sb(keep_all, "strict", [P, P])
        ones = sb(keep_all, "ones", [P, P])
        lane = sb(keep_all, "lane", [P, 1])
        iota = sb(keep_all, "iota", [P, TB * P])
        xcur = sb(keep_all, "xcur", [P, NT, FX])
        deg_d = sb(keep_all, "deg_d", [P, NT])
        end_d = sb(keep_all, "end_d", [P, NT], I32)
        start_d = sb(keep_all, "start_d", [P, NT], I32)
        src_d = sb(keep_all, "src_d", [P, J], I32)
        key_d = sb(keep_all, "key_d", [P, J])
        keep_d = sb(keep_all, "keep_d", [P, J])
        open_d = sb(keep_all, "open_d", [P, 1])
        head_d = sb(keep_all, "head_d", [P, 1], I32)

        weights = {}
        for name in ("L0_gnn_stn3_w", "L0_gnn_stn4_w", "L1_gnn_W1", "L1_gnn_W2", "L1_gnn_W3", "L2_gnn_W1", "L2_gnn_W2"):
            weights[name] = (t[name], sb(keep_all, name, list(t[name].shape)))
        w1 = t["L0_gnn_stn1_w"].rearrange("k i o -> k (i o)")
        weights["L0_gnn_stn1_w"] = (w1, sb(keep_all, "stn1_w", [K3, H1]))
        W3H = NH // 2 * HC
        w3rows = t["L1_gnn_W3"].rearrange("i (h o) -> h i o", h=NH)
        w3a = sb(keep_all, "w3a", [W3H, FX])
        w3b = sb(keep_all, "w3b", [W3H, FX])
        bcast = {}
        for name in ("L0_gnn_stn1_b", "L0_gnn_stn2_b", "L0_gnn_stn3_b", "L0_gnn_stn4_b", "L0_gnn_conv_b",
                     "L1_gnn_b1", "L1_gnn_b2", "L1_gnn_b3", "L2_gnn_b1", "L2_gnn_b2",
                     "L1_gnn_a_src1", "L1_gnn_a_dst1", "L1_gnn_a_src2", "L1_gnn_a_dst2", "L1_gnn_a_src3", "L1_gnn_a_dst3"):
            a = t[name]
            if len(a.shape) == 2:
                a = a.rearrange("h c -> (h c)")
            bcast[name] = (a, sb(keep_all, name, [P, a.shape[0]]))

        def W(name):
            return weights[name][1]

        def B(name):
            return bcast[name][1]

        def row(ap, shape):
            return ap[:, :].unsqueeze(1).to_broadcast(shape)


        def stage_constants(zeros, negs):
            with nc.Block() as block:
                c = counted("const_load")
                n_load = [0]

                @block.sync
                def _(sp):
                    def load(dst, src):
                        sp.dma_start(dst, src).then_inc(c.sem, 16)
                        n_load[0] += 1
                    for src, dst in weights.values():
                        load(dst[:, :], src)
                    for h in range(NH):
                        dst = w3a if h < NH // 2 else w3b
                        h0 = h % (NH // 2)
                        load(dst[h0 * HC:(h0 + 1) * HC, :], w3rows[h])
                    for src, dst in bcast.values():
                        load(dst[:, :], src.partition_broadcast(P))
                    sp.wait_ge(sem("x_zeroed"), 1)
                    sp.sem_inc(sem("x_zeroed"), -1)
                    full = N // P
                    load(xcur[:, 0:full, :], t["x"][0:full * P, :].rearrange("(t p) f -> p t f", p=P))
                    if N % P:
                        load(xcur[0:N % P, full, :], t["x"][full * P:N, :])
                    sp.wait_ge(sem("zeros_set"), 1)
                    sp.sem_inc(sem("zeros_set"), -1)
                    for d in (starts_t, starts_h):
                        w = d.shape[1]
                        load(edges_of(d, w).rearrange("p j w -> p (j w)"), zeros[:, 0:J * w])
                    for d in (run_basis, run_stn2, run_conv, run_gat, run_gat3, run_gcn):
                        load(d[EP:EP + 1, :], zeros[0:1, 0:d.shape[1]])
                    load(run_max[EP:EP + 1, :], negs[0:1, :])
                    sp.wait_ge(c.sem, 16 * n_load[0])
                    c.base += 16 * n_load[0]

                @block.vector
                def _(v):
                    v.memset(xcur[:, :, :], 0.0).then_inc(dve_step, 1)
                    v.wait_ge(dve_step, 1)
                    v.sem_inc(dve_step, -1)
                    v.sem_inc(sem("x_zeroed"), 1)
                    v.memset(negs[:, :], -BIG)
                    v.memset(zeros[:, :], 0.0).then_inc(dve_step, 1)
                    v.wait_ge(dve_step, 1)
                    v.sem_inc(dve_step, -1)
                    v.sem_inc(sem("zeros_set"), 1)

                @block.gpsimd
                def _(g):
                    g.iota(iota[:, :], pattern=[[1, TB * P]], base=0, channel_multiplier=0,
                           allow_small_or_imprecise_dtypes=True)
                    g.iota(lane[:, :], pattern=[[0, 1]], base=0, channel_multiplier=1,
                           allow_small_or_imprecise_dtypes=True)
                    g.memset(ones[:, :], 1.0).then_inc(pool_step, 1)
                    g.wait_ge(pool_step, 1)
                    g.sem_inc(pool_step, -1)
                    g.affine_select(out=upper[:, :], in_=ones[:, :], compare_op=ALU.is_ge, fill=0.0,
                                    base=0, pattern=[[1, P]], channel_multiplier=-1)
                    g.affine_select(out=strict[:, :], in_=ones[:, :], compare_op=ALU.is_gt, fill=0.0,
                                    base=0, pattern=[[1, P]], channel_multiplier=-1)
                    g.affine_select(out=ident[:, :], in_=ones[:, :], compare_op=ALU.is_equal,
                                    fill=0.0, base=0, pattern=[[1, P]], channel_multiplier=-1).then_inc(pool_step, 1)
                    g.wait_ge(pool_step, 1)
                    g.sem_inc(pool_step, -1)

        def stage_load_edges(src_f, dst_f, pseudo, src_i, dst_i):
            with nc.Block() as block:
                c = counted("edge_load")

                @block.sync
                def _(sp):
                    sp.wait_ge(sem("edges_padded"), 1)
                    sp.sem_inc(sem("edges_padded"), -1)
                    k = 0
                    for dst, s in ((src_i, t["src"]), (dst_i, t["dst"])):
                        sp.dma_start(dst[0:LASTP, :], s[0:LASTP * J].rearrange("(p j) -> p j", j=J)).then_inc(c.sem, 16)
                        sp.dma_start(dst[LASTP:LASTP + 1, 0:LASTC],
                                     s[LASTP * J:E].rearrange("(p j) -> p j", p=1)).then_inc(c.sem, 16)
                        k += 2
                    a = t["edge_attr_3"]
                    sp.dma_start(pseudo[0:LASTP, :, :], a[0:LASTP * J, :].rearrange("(p j) w -> p j w", j=J)).then_inc(c.sem, 16)
                    sp.dma_start(pseudo[LASTP:LASTP + 1, 0:LASTC, :],
                                 a[LASTP * J:E, :].rearrange("(p j) w -> p j w", p=1)).then_inc(c.sem, 16)
                    sp.wait_ge(c.sem, 16 * (k + 2))
                    sp.sem_inc(sem("edges_in"), 1)

                @block.vector
                def _(v):
                    v.memset(src_i[:, :], PAD)
                    v.memset(dst_i[:, :], PAD)
                    v.memset(pseudo[:, :, :], 0.0).then_inc(dve_step, 1)
                    v.wait_ge(dve_step, 1)
                    v.sem_inc(dve_step, -1)
                    v.sem_inc(sem("edges_padded"), 1)
                    v.wait_ge(sem("edges_in"), 1)
                    v.sem_inc(sem("edges_in"), -1)
                    v.tensor_copy(src_f[:, :], src_i[:, :])
                    v.tensor_copy(dst_f[:, :], dst_i[:, :]).then_inc(dve_step, 1)
                    v.wait_ge(dve_step, 1)
                    v.sem_inc(dve_step, -1)

        class Histogram:

            def __init__(self, st, key, deg):
                self.key, self.deg = key, deg
                self.key_i = sb(st, "key_i", [P, J], I32)
                self.digit_i = sb(st, "digit_i", [P, J], I32)
                self.lo = sb(st, "lo", [P, J])
                self.hi = sb(st, "hi", [P, J])
                self.hot_lo = sb(st, "hot_lo", [P, CH, P], BF16)
                self.hot_hi = sb(st, "hot_hi", [P, CH, NT], BF16)
                self.part = ps(st, "part", [P, NT])

            def setup(self, v):
                v.memset(self.deg[:, :], 0.0)
                v.tensor_copy(self.key_i[:, :], self.key).then_inc(dve_step, 1)
                v.wait_ge(dve_step, 1)
                v.sem_inc(dve_step, -1)
                v.tensor_scalar(self.digit_i[:, :], self.key_i[:, :], P - 1, None, ALU.bitwise_and).then_inc(dve_step, 1)
                v.wait_ge(dve_step, 1)
                v.sem_inc(dve_step, -1)
                v.tensor_copy(self.lo[:, :], self.digit_i[:, :]).then_inc(dve_step, 1)
                v.wait_ge(dve_step, 1)
                v.sem_inc(dve_step, -1)
                v.tensor_scalar(self.digit_i[:, :], self.key_i[:, :], 7, None, ALU.logical_shift_right).then_inc(dve_step, 1)
                v.wait_ge(dve_step, 1)
                v.sem_inc(dve_step, -1)
                v.tensor_copy(self.hi[:, :], self.digit_i[:, :]).then_inc(dve_step, 1)
                v.wait_ge(dve_step, 1)
                v.sem_inc(dve_step, -1)

            def make(self, v, col):
                v.tensor_tensor(self.hot_lo[:, :, :], self.lo[:, bass.ds(col, CH)].unsqueeze(2).to_broadcast([P, CH, P]),
                                iota[:, 0:P].unsqueeze(1).to_broadcast([P, CH, P]), ALU.is_equal)
                v.tensor_tensor(
 self.hot_hi[:, :, :], self.hi[:, bass.ds(col, CH)].unsqueeze(2).to_broadcast([P, CH, NT]),
 iota[:, 0:NT].unsqueeze(1).to_broadcast([P, CH, NT]), ALU.is_equal).then_inc(dve_step, 1)
                v.wait_ge(dve_step, 1)
                v.sem_inc(dve_step, -1)
                v.sem_inc(sem("hot_made"), 1)

            def add(self, v):
                v.wait_ge(sem("hot_counted"), 1)
                v.sem_inc(sem("hot_counted"), -1)
                v.tensor_tensor(self.deg[:, :], self.deg[:, :], self.part[:, :], ALU.add).then_inc(dve_step, 1)
                v.wait_ge(dve_step, 1)
                v.sem_inc(dve_step, -1)

            def tensor(self, pe):
                with pe.Fori(0, J // CH):
                    pe.wait_ge(sem("hot_made"), 1)
                    pe.sem_inc(sem("hot_made"), -1)
                    for c in range(CH):
                        last = pe.matmul(self.part[:, :], self.hot_lo[:, c, :], self.hot_hi[:, c, :], start=(c == 0), stop=(c == CH - 1))
                    last.then_inc(sem("hot_counted"), 1)

        def stage_bounds(deg, end_i, start_i):
            with ExitStack() as st, nc.Block() as block:
                within = ps(st, "within", [P, NT])
                total = ps(st, "total", [P, NT])
                run = sb(st, "run", [P, NT])
                tot = sb(st, "tot", [P, NT])
                has = sb(st, "has", [P, NT])
                fin = sb(st, "fin", [P, NT])
                beg = sb(st, "beg", [P, NT])
                zero = sb(st, "zero", [P, NT])
                dump = sb(st, "dump", [P, NT])
                summed = sem("bounds_summed")

                @block.tensor
                def _(pe):
                    pe.matmul(within[:, :], upper[:, :], deg[:, :], start=True, stop=True)
                    pe.matmul(total[:, :], ones[:, :], deg[:, :], start=True, stop=True).then_inc(summed, 1)

                @block.vector
                def _(v):
                    v.memset(zero[:, :], 0.0)
                    v.tensor_scalar(dump[:, :], iota[:, 0:NT], float(P), float(DMP), ALU.mult, ALU.add).then_inc(dve_step, 1)
                    v.wait_ge(dve_step, 1)
                    v.sem_inc(dve_step, -1)
                    v.tensor_scalar(dump[:, :], dump[:, :], lane[:, 0:1], None, ALU.add)
                    v.tensor_scalar(has[:, :], deg[:, :], 0.5, None, ALU.is_gt).then_inc(dve_step, 1)
                    v.wait_ge(dve_step, 1)
                    v.sem_inc(dve_step, -1)
                    v.wait_ge(summed, 1)
                    v.sem_inc(summed, -1)
                    v.tensor_copy(tot[:, :], total[:, :]).then_inc(dve_step, 1)
                    v.wait_ge(dve_step, 1)
                    v.sem_inc(dve_step, -1)
                    v.tensor_tensor_scan(run[:, :], tot[:, :], zero[:, :], 0.0, ALU.add, ALU.add).then_inc(dve_step, 1)
                    v.wait_ge(dve_step, 1)
                    v.sem_inc(dve_step, -1)
                    v.tensor_tensor(run[:, :], run[:, :], tot[:, :], ALU.subtract).then_inc(dve_step, 1)
                    v.wait_ge(dve_step, 1)
                    v.sem_inc(dve_step, -1)
                    v.tensor_tensor(fin[:, :], run[:, :], within[:, :], ALU.add).then_inc(dve_step, 1)
                    v.wait_ge(dve_step, 1)
                    v.sem_inc(dve_step, -1)
                    v.tensor_tensor(beg[:, :], fin[:, :], deg[:, :], ALU.subtract).then_inc(dve_step, 1)
                    v.wait_ge(dve_step, 1)
                    v.sem_inc(dve_step, -1)
                    v.tensor_scalar(fin[:, :], fin[:, :], -1.0 - EP, None, ALU.add)
                    v.tensor_tensor(beg[:, :], beg[:, :], dump[:, :], ALU.subtract).then_inc(dve_step, 1)
                    v.wait_ge(dve_step, 1)
                    v.sem_inc(dve_step, -1)
                    v.tensor_tensor(fin[:, :], fin[:, :], has[:, :], ALU.mult)
                    v.tensor_tensor(beg[:, :], beg[:, :], has[:, :], ALU.mult).then_inc(dve_step, 1)
                    v.wait_ge(dve_step, 1)
                    v.sem_inc(dve_step, -1)
                    v.tensor_scalar(end_i[:, :], fin[:, :], float(EP), None, ALU.add)
                    v.tensor_tensor(start_i[:, :], beg[:, :], dump[:, :], ALU.add).then_inc(dve_step, 1)
                    v.wait_ge(dve_step, 1)
                    v.sem_inc(dve_step, -1)

        def stage_order(key, next_head_src, next_is_int, keep, open_, head):
            with ExitStack() as st, nc.Block() as block:
                nxt_raw = sb(st, "nxt_raw", [P, 1], I32 if next_is_int else F32)
                nxt = sb(st, "nxt", [P, 1])
                same = sb(st, "same", [P, 1])
                c = counted("order_load")

                @block.sync
                def _(sp):
                    sp.wait_ge(sem("next_cleared"), 1)
                    sp.sem_inc(sem("next_cleared"), -1)
                    with nc.allow_non_contiguous_dma(reason="one value per partition"):
                        sp.dma_start(nxt_raw[0:P - 1, :], next_head_src).then_inc(c.sem, 16)
                    sp.wait_ge(c.sem, c.base + 16)
                    sp.sem_inc(sem("next_in"), 1)
                c.base += 16

                @block.vector
                def _(v):
                    v.memset(nxt_raw[:, :], -1).then_inc(dve_step, 1)
                    v.wait_ge(dve_step, 1)
                    v.sem_inc(dve_step, -1)
                    v.sem_inc(sem("next_cleared"), 1)
                    v.memset(keep[:, 0:1], 0.0)
                    v.tensor_copy(head[:, :], key[:, 0:1])
                    v.tensor_tensor(keep[:, 1:J], key[:, 1:J], key[:, 0:J - 1], ALU.is_equal)
                    v.wait_ge(sem("next_in"), 1)
                    v.sem_inc(sem("next_in"), -1)
                    v.tensor_copy(nxt[:, :], nxt_raw[:, :]).then_inc(dve_step, 1)
                    v.wait_ge(dve_step, 1)
                    v.sem_inc(dve_step, -1)
                    v.tensor_tensor(same[:, :], nxt[:, :], key[:, J - 1:J], ALU.is_equal).then_inc(dve_step, 1)
                    v.wait_ge(dve_step, 1)
                    v.sem_inc(dve_step, -1)
                    v.scalar_tensor_tensor(open_[:, :], key[:, J - 1:J], 1.0, same[:, :], ALU.add, ALU.mult).then_inc(dve_step, 1)
                    v.wait_ge(dve_step, 1)
                    v.sem_inc(dve_step, -1)
                    v.tensor_scalar(open_[:, :], open_[:, :], -1.0, None, ALU.add).then_inc(dve_step, 1)
                    v.wait_ge(dve_step, 1)
                    v.sem_inc(dve_step, -1)

        def stage_radix(payload, shift, bins, dest, deg, spline):
            with ExitStack() as st, nc.Block() as block:
                hist = Histogram(st, payload[:, :, 0], deg) if deg is not None else None
                table = SplineTable(st, *spline, True) if spline is not None else None
                key_i = sb(st, "key_i", [P, J], I32)
                digit = sb(st, "digit", [P, J])
                nxt = sb(st, "nxt", [P, bins])
                total = sb(st, "total", [P, bins])
                zero = sb(st, "zero", [P, bins])
                junk = sb(st, "junk", [P, bins])
                hot = sb(st, "hot", [P, CH, bins])
                rank = [sb(st, f"rank{b}", [P, CH]) for b in range(2)]
                at = [sb(st, f"at{b}", [P, CH], I32) for b in range(2)]
                rows = [sb(st, f"rows{b}", [P, CH, 8]) for b in range(2)]
                below = ps(st, "below", [P, bins])
                every = ps(st, "every", [P, bins])
                c = [counted(f"scattered{b}") for b in range(2)]
                base = [k.base for k in c]
                steps = J // CH // 2

                @block.vector
                def _(v):
                    if table:
                        table.clear(v)
                    if hist:
                        hist.setup(v)
                    v.memset(nxt[:, :], 0.0)
                    v.memset(zero[:, :], 0.0)
                    v.tensor_copy(key_i[:, :], payload[:, :, 0]).then_inc(dve_step, 1)
                    v.wait_ge(dve_step, 1)
                    v.sem_inc(dve_step, -1)
                    if shift:
                        v.tensor_scalar(key_i[:, :], key_i[:, :], shift, None, ALU.logical_shift_right).then_inc(dve_step, 1)
                        v.wait_ge(dve_step, 1)
                        v.sem_inc(dve_step, -1)
                    else:
                        v.tensor_scalar(key_i[:, :], key_i[:, :], bins - 1, None, ALU.bitwise_and).then_inc(dve_step, 1)
                        v.wait_ge(dve_step, 1)
                        v.sem_inc(dve_step, -1)
                    v.tensor_copy(digit[:, :], key_i[:, :]).then_inc(dve_step, 1)
                    v.wait_ge(dve_step, 1)
                    v.sem_inc(dve_step, -1)
                    with v.Fori(0, J // CH) as it:
                        sh = [P, CH, bins]
                        v.tensor_tensor(hot[:, :, :], digit[:, bass.ds(it * CH, CH)].unsqueeze(2).to_broadcast(sh),
                                        iota[:, 0:bins].unsqueeze(1).to_broadcast(sh), ALU.is_equal).then_inc(dve_step, 1)
                        v.wait_ge(dve_step, 1)
                        v.sem_inc(dve_step, -1)
                        v.tensor_reduce(junk[:, :], hot[:, :, :].rearrange("p c k -> p k c"), AXX, ALU.add).then_inc(dve_step, 1)
                        v.wait_ge(dve_step, 1)
                        v.sem_inc(dve_step, -1)
                        v.tensor_tensor(nxt[:, :], nxt[:, :], junk[:, :], ALU.add).then_inc(dve_step, 1)
                        v.wait_ge(dve_step, 1)
                        v.sem_inc(dve_step, -1)
                    v.sem_inc(sem("digits_counted"), 1)
                    v.wait_ge(sem("digits_summed"), 1)
                    v.sem_inc(sem("digits_summed"), -1)
                    v.tensor_copy(total[:, :], every[:, :])
                    v.tensor_copy(nxt[:, :], below[:, :]).then_inc(dve_step, 1)
                    v.wait_ge(dve_step, 1)
                    v.sem_inc(dve_step, -1)
                    v.tensor_tensor_scan(junk[:, :], total[:, :], zero[:, :], 0.0, ALU.add, ALU.add).then_inc(dve_step, 1)
                    v.wait_ge(dve_step, 1)
                    v.sem_inc(dve_step, -1)
                    v.tensor_tensor(junk[:, :], junk[:, :], total[:, :], ALU.subtract).then_inc(dve_step, 1)
                    v.wait_ge(dve_step, 1)
                    v.sem_inc(dve_step, -1)
                    v.tensor_tensor(nxt[:, :], nxt[:, :], junk[:, :], ALU.add).then_inc(dve_step, 1)
                    v.wait_ge(dve_step, 1)
                    v.sem_inc(dve_step, -1)
                    with v.Fori(0, steps) as it:
                        for b in range(2):
                            if hist:
                                hist.make(v, it * (2 * CH) + b * CH)
                            for k in range(CH):
                                col = digit[:, bass.ds(it * (2 * CH) + (b * CH + k), 1)]
                                v.scalar_tensor_tensor(junk[:, :], iota[:, 0:bins], col, nxt[:, :], ALU.is_equal, ALU.mult,
                                                       accum_out=rank[b][:, k:k + 1])
                                v.scalar_tensor_tensor(
                 nxt[:, :], iota[:, 0:bins], col, nxt[:, :], ALU.is_equal, ALU.add).then_inc(dve_step, 1)
                                v.wait_ge(dve_step, 1)
                                v.sem_inc(dve_step, -1)
                            v.wait_ge(sem(f"rank_free{b}"), 1)
                            v.sem_inc(sem(f"rank_free{b}"), -1)
                            v.tensor_copy(rows[b][:, :, :], payload[:, bass.ds(it * (2 * CH) + b * CH, CH), :])
                            v.tensor_copy(at[b][:, :], rank[b][:, :]).then_inc(dve_step, 1)
                            v.wait_ge(dve_step, 1)
                            v.sem_inc(dve_step, -1)
                            v.sem_inc(sem(f"ranked{b}"), 1)
                            if hist:
                                hist.add(v)

                @block.tensor
                def _(pe):
                    pe.wait_ge(sem("digits_counted"), 1)
                    pe.sem_inc(sem("digits_counted"), -1)
                    pe.matmul(below[:, :], strict[:, :], nxt[:, :], start=True, stop=True)
                    pe.matmul(every[:, :], ones[:, :], nxt[:, :], start=True, stop=True).then_inc(sem("digits_summed"), 1)
                    if hist:
                        hist.tensor(pe)
                    if table:
                        table.tensor(pe)

                @block.scalar
                def _(a):
                    if table:
                        table.scalar(a)

                @block.gpsimd
                def _(g):
                    with g.Fori(0, steps):
                        for b in range(2):
                            g.wait_ge(sem(f"ranked{b}"), 1)
                            g.sem_inc(sem(f"ranked{b}"), -1)
                            for k in range(CH):
                                g.indirect_dma_start(out=dest, out_offset=bass.IndirectOffsetOnAxis(ap=at[b][:, k:k + 1], axis=0),
                                                     in_=rows[b][:, k, :], in_offset=None).then_inc(c[b].sem, 16)

                @block.sync
                def _(sp):
                    if table:
                        table.sync(sp)
                    for b in range(2):
                        sp.sem_inc(sem(f"rank_free{b}"), 1)
                    with sp.Fori(0, steps) as it:
                        for b in range(2):
                            sp.wait_ge(c[b].sem, it * (16 * CH) + (16 * CH + base[b]))
                            sp.sem_inc(sem(f"rank_free{b}"), 1)
                    for b in range(2):
                        sp.wait_ge(sem(f"rank_free{b}"), 1)
                        sp.sem_inc(sem(f"rank_free{b}"), -1)
                for k in c:
                    k.base += 16 * CH * steps

        def sweep(gathers, ch, chunk, store, setup=None, tensor=None, apart=False, prepare=None):
            steps = J // ch // 2
            with ExitStack() as st, nc.Block() as block:
                at = [[sb(st, f"at{n}{b}", [P, ch], I32) for b in range(2)] for n in range(len(gathers))]
                c = [counted(f"gathered{b}_{n_sweeps[0] // 3}") for b in range(2)]
                n_sweeps[0] += bool(gathers)
                cs = [counted(f"stored{b}") for b in range(2)]
                base = [k.base for k in c]
                sbase = [k.base for k in cs]
                per = 16 * ch * len(gathers)

                @block.scalar
                def _(a):
                    if gathers:
                        with a.Fori(0, steps) as it:
                            for b in range(2):
                                a.wait_ge(sem(f"ring_free{b}"), 1)
                                a.sem_inc(sem(f"ring_free{b}"), -1)
                                for n, (_, idx, _, _) in enumerate(gathers):
                                    last = a.copy(at[n][b][:, :], idx[:, bass.ds(it * (2 * ch) + b * ch, ch)])
                                last.then_inc(act_step, 1)
                                a.wait_ge(act_step, 1)
                                a.sem_inc(act_step, -1)
                                a.sem_inc(sem(f"indices_staged{b}"), 1)
                        for b in range(2):
                            a.wait_ge(sem(f"ring_free{b}"), 1)
                            a.sem_inc(sem(f"ring_free{b}"), -1)

                @block.gpsimd
                def _(g):
                    if gathers:
                        with g.Fori(0, steps):
                            for b in range(2):
                                g.wait_ge(sem(f"indices_staged{b}"), 1)
                                g.sem_inc(sem(f"indices_staged{b}"), -1)
                                for k in range(ch):
                                    for n, (table, _, bufs, view) in enumerate(gathers):
                                        g.indirect_dma_start(
                                            out=view(bufs[b], k), out_offset=None, in_=table,
                                            in_offset=bass.IndirectOffsetOnAxis(ap=at[n][b][:, k:k + 1], axis=0)
                                        ).then_inc(c[b].sem, 16)
                    if prepare:
                        with g.Fori(0, steps) as it:
                            for b in range(2):
                                g.wait_ge(sem(f"ring_free{b}"), 1)
                                g.sem_inc(sem(f"ring_free{b}"), -1)
                                prepare(g, b, it * (2 * ch) + b * ch)
                                g.sem_inc(sem(f"prepared{b}"), 1)
                        for b in range(2):
                            g.wait_ge(sem(f"ring_free{b}"), 1)
                            g.sem_inc(sem(f"ring_free{b}"), -1)

                @block.tensor
                def _(pe):
                    if tensor:
                        tensor(pe)

                @block.vector
                def _(v):
                    if setup:
                        setup(v)
                    with v.Fori(0, steps) as it:
                        for b in range(2):
                            if gathers:
                                v.wait_ge(c[b].sem, it * per + (per + base[b]))
                                v.sem_inc(dve_step, 1)
                                v.wait_ge(dve_step, 1)
                                v.sem_inc(dve_step, -1)
                            elif prepare:
                                v.wait_ge(sem(f"prepared{b}"), 1)
                                v.sem_inc(sem(f"prepared{b}"), -1)
                            else:
                                v.wait_ge(sem(f"ring_free{b}"), 1)
                                v.sem_inc(sem(f"ring_free{b}"), -1)
                            chunk(v, b, it * (2 * ch) + b * ch)
                            v.sem_inc(sem(f"chunk_done{b}"), 1)
                    if not gathers and not prepare:
                        for b in range(2):
                            v.wait_ge(sem(f"ring_free{b}"), 1)
                            v.sem_inc(sem(f"ring_free{b}"), -1)

                @block.sync
                def _(sp):
                    for b in range(2):
                        sp.sem_inc(sem(f"ring_free{b}"), 1)
                        if apart:
                            sp.sem_inc(sem(f"out_free{b}"), 1)
                    with sp.Fori(0, steps) as it:
                        for b in range(2):
                            sp.wait_ge(sem(f"chunk_done{b}"), 1)
                            sp.sem_inc(sem(f"chunk_done{b}"), -1)
                            if store:
                                bufs, dest = store
                                w = dest.shape[1]
                                sp.dma_start(edges_of(dest, w)[:, bass.ds(it * (2 * ch) + b * ch, ch), :],
                                             bufs[b][:, :, 0:w]).then_inc(cs[b].sem, 16)
                                sp.wait_ge(cs[b].sem, it * 16 + (16 + sbase[b]))
                            sp.sem_inc(sem(f"out_free{b}" if apart else f"ring_free{b}"), 1)
                    if apart:
                        for b in range(2):
                            sp.wait_ge(sem(f"out_free{b}"), 1)
                            sp.sem_inc(sem(f"out_free{b}"), -1)
                if gathers:
                    for k in c:
                        k.base += per * steps
                if store:
                    for k in cs:
                        k.base += 16 * steps

        def running_sum(v, buf, carry, keep, col, ch):
            for f in range(buf.shape[2]):
                last = v.tensor_tensor_scan(buf[:, :, f], keep[:, bass.ds(col, ch)], buf[:, :, f], carry[:, f:f + 1],
                                            ALU.mult, ALU.add)
            last.then_inc(dve_step, 1)
            v.wait_ge(dve_step, 1)
            v.sem_inc(dve_step, -1)
            v.tensor_copy(carry[:, :], buf[:, ch - 1, :]).then_inc(dve_step, 1)
            v.wait_ge(dve_step, 1)
            v.sem_inc(dve_step, -1)

        def stage_ends(run, ends_i, open_, got, tail_rhs, tails):
            F = run.shape[1]
            FT = tail_rhs.shape[1]
            stride = P if FT <= P else 2 * P
            with ExitStack() as st, nc.Block() as block:
                hot = sb(st, "hot", [P, TB * P])
                rel = sb(st, "rel", [P, 1])
                acc = ps(st, "acc", [P, TB, stride])
                c = counted("ends_gathered")

                @block.gpsimd
                def _(g):
                    for k in range(NT):
                        g.indirect_dma_start(out=got[:, k, :], out_offset=None, in_=run,
                                             in_offset=bass.IndirectOffsetOnAxis(ap=ends_i[:, k:k + 1], axis=0)).then_inc(c.sem, 16)

                @block.vector
                def _(v):
                    v.tensor_copy(rel[:, :], open_[:, :]).then_inc(dve_step, 1)
                    v.wait_ge(dve_step, 1)
                    v.sem_inc(dve_step, -1)
                    with v.Fori(0, NB) as it:
                        v.tensor_scalar(hot[:, :], iota[:, :], rel[:, 0:1], None, ALU.is_equal).then_inc(dve_step, 1)
                        v.wait_ge(dve_step, 1)
                        v.sem_inc(dve_step, -1)
                        v.sem_inc(sem("hot_ready"), 1)
                        v.tensor_scalar(rel[:, :], rel[:, :], -float(TB * P), None, ALU.add).then_inc(dve_step, 1)
                        v.wait_ge(dve_step, 1)
                        v.sem_inc(dve_step, -1)
                        v.wait_ge(sem("tails_ready"), 1)
                        v.sem_inc(sem("tails_ready"), -1)
                        v.tensor_copy(tails[:, bass.ds(it * TB, TB), :], acc[:, :, 0:FT]).then_inc(dve_step, 1)
                        v.wait_ge(dve_step, 1)
                        v.sem_inc(dve_step, -1)

                @block.tensor
                def _(pe):
                    with pe.Fori(0, NB):
                        pe.wait_ge(sem("hot_ready"), 1)
                        pe.sem_inc(sem("hot_ready"), -1)
                        for k in range(TB):
                            last = pe.matmul(acc[:, k, 0:FT], hot[:, k * P:(k + 1) * P], tail_rhs, start=True, stop=True)
                        last.then_inc(sem("tails_ready"), 1)

                @block.sync
                def _(sp):
                    sp.wait_ge(c.sem, c.base + 16 * NT)
                c.base += 16 * NT

        def stage_linear(arr, parts, width, res):
            stride = P if width <= P else 2 * P
            n_acc = 2 if width <= P else 1
            with ExitStack() as st, nc.Block() as block:
                turned = [[sb(st, f"turned{n}{b}", [hi - lo, TB, P]) for b in range(2)] for n, (lo, hi, _) in enumerate(parts)]
                tp = [ps(st, f"tp{b}", [P, TB, P]) for b in range(2)]
                acc = [ps(st, f"acc{b}", [P, TB, stride]) for b in range(n_acc)]
                items = [(it, n) for it in range(NB) for n in range(len(parts))]

                @block.tensor
                def _(pe):
                    def product(it):
                        pe.wait_ge(sem("turned_copied"), len(parts))
                        pe.sem_inc(sem("turned_copied"), -len(parts))
                        if it >= n_acc:
                            pe.wait_ge(sem(f"product_copied{it % n_acc}"), 1)
                            pe.sem_inc(sem(f"product_copied{it % n_acc}"), -1)
                        for k in range(TB):
                            for n, (_, _, w) in enumerate(parts):
                                last = pe.matmul(acc[it % n_acc][:, k, 0:width], turned[n][it % 2][:, k, :], w,
                                                 start=(n == 0), stop=(n == len(parts) - 1))
                        last.then_inc(sem("product_ready"), 1)
                    for i, (it, n) in enumerate(items):
                        lo, hi, _ = parts[n]
                        if i >= 2:
                            pe.wait_ge(sem(f"turned_free{i % 2}"), 1)
                            pe.sem_inc(sem(f"turned_free{i % 2}"), -1)
                        for k in range(TB):
                            last = pe.transpose(tp[i % 2][0:hi - lo, k, :], arr[:, it * TB + k, lo:hi], ident[:, :])
                        last.then_inc(sem("turned"), 1)
                        if it and n == 0:
                            product(it - 1)
                    product(NB - 1)

                @block.scalar
                def _(a):
                    for i, (it, n) in enumerate(items):
                        lo, hi, _ = parts[n]
                        a.wait_ge(sem("turned"), 1)
                        a.sem_inc(sem("turned"), -1)
                        a.copy(turned[n][it % 2][:, :, :], tp[i % 2][0:hi - lo, :, :]).then_inc(act_step, 1)
                        a.wait_ge(act_step, 1)
                        a.sem_inc(act_step, -1)
                        a.sem_inc(sem("turned_copied"), 1)
                        if i + 2 < len(items):
                            a.sem_inc(sem(f"turned_free{i % 2}"), 1)

                @block.vector
                def _(v):
                    for it in range(NB):
                        v.wait_ge(sem("product_ready"), 1)
                        v.sem_inc(sem("product_ready"), -1)
                        v.tensor_copy(res[:, it * TB:(it + 1) * TB, 0:width], acc[it % n_acc][:, :, 0:width]).then_inc(dve_step, 1)
                        v.wait_ge(dve_step, 1)
                        v.sem_inc(dve_step, -1)
                        if it + n_acc < NB:
                            v.sem_inc(sem(f"product_copied{it % n_acc}"), 1)

        def linear(arr, k_, w, width, res):
            stage_linear(arr, [(0, k_, w)], width, res)

        to_act, from_act = sem("to_act"), sem("from_act")

        def vector_stage(f, g=None):
            with nc.Block() as block:
                @block.vector
                def _(v):
                    f(v)

                @block.scalar
                def _(a):
                    if g:
                        g(a)

        def copy_out(pairs):
            with nc.Block() as block:
                c = counted("copied_out")

                @block.sync
                def _(sp):
                    for dst, src in pairs:
                        sp.dma_start(dst, src).then_inc(c.sem, 16)
                    sp.wait_ge(c.sem, c.base + 16 * len(pairs))
                c.base += 16 * len(pairs)

        def stage_elu(x):
            with ExitStack() as st, nc.Block() as block:
                low = sb(st, "low", list(x.shape))

                @block.vector
                def _(v):
                    v.tensor_scalar(low[:, :, :], x[:, :, :], 0.0, None, ALU.min).then_inc(dve_step, 1)
                    v.wait_ge(dve_step, 1)
                    v.sem_inc(dve_step, -1)
                    v.sem_inc(to_act, 1)
                    v.tensor_scalar(x[:, :, :], x[:, :, :], 0.0, -1.0, ALU.max, ALU.add).then_inc(dve_step, 1)
                    v.wait_ge(dve_step, 1)
                    v.sem_inc(dve_step, -1)
                    v.wait_ge(from_act, 1)
                    v.sem_inc(from_act, -1)
                    v.tensor_tensor(x[:, :, :], x[:, :, :], low[:, :, :], ALU.add).then_inc(dve_step, 1)
                    v.wait_ge(dve_step, 1)
                    v.sem_inc(dve_step, -1)

                @block.scalar
                def _(a):
                    a.wait_ge(to_act, 1)
                    a.sem_inc(to_act, -1)
                    a.activation(low[:, :, :], low[:, :, :], ACT.Exp).then_inc(act_step, 1)
                    a.wait_ge(act_step, 1)
                    a.sem_inc(act_step, -1)
                    a.sem_inc(from_act, 1)

        def stage_layernorm(add):
            with ExitStack() as st:
                sq = sb(st, "sq", [P, NT, FX])
                m = sb(st, "m", [P, NT])
                s = sb(st, "s", [P, NT])

                def f(v):
                    sh = [P, NT, FX]
                    v.tensor_tensor(xcur[:, :, :], xcur[:, :, :], add[:, :, :], ALU.add).then_inc(dve_step, 1)
                    v.wait_ge(dve_step, 1)
                    v.sem_inc(dve_step, -1)
                    v.tensor_reduce(m[:, :], xcur[:, :, :], AXX, ALU.add).then_inc(dve_step, 1)
                    v.wait_ge(dve_step, 1)
                    v.sem_inc(dve_step, -1)
                    v.tensor_scalar(m[:, :], m[:, :], 1.0 / FX, None, ALU.mult).then_inc(dve_step, 1)
                    v.wait_ge(dve_step, 1)
                    v.sem_inc(dve_step, -1)
                    v.tensor_tensor(xcur[:, :, :], xcur[:, :, :], m[:, :].unsqueeze(2).to_broadcast(sh), ALU.subtract).then_inc(dve_step, 1)
                    v.wait_ge(dve_step, 1)
                    v.sem_inc(dve_step, -1)
                    v.tensor_tensor(sq[:, :, :], xcur[:, :, :], xcur[:, :, :], ALU.mult).then_inc(dve_step, 1)
                    v.wait_ge(dve_step, 1)
                    v.sem_inc(dve_step, -1)
                    v.tensor_reduce(m[:, :], sq[:, :, :], AXX, ALU.add).then_inc(dve_step, 1)
                    v.wait_ge(dve_step, 1)
                    v.sem_inc(dve_step, -1)
                    v.tensor_scalar(m[:, :], m[:, :], 1.0 / FX, 1e-5, ALU.mult, ALU.add).then_inc(dve_step, 1)
                    v.wait_ge(dve_step, 1)
                    v.sem_inc(dve_step, -1)
                    v.sem_inc(to_act, 1)
                    v.wait_ge(from_act, 1)
                    v.sem_inc(from_act, -1)
                    v.reciprocal(s[:, :], s[:, :]).then_inc(dve_step, 1)
                    v.wait_ge(dve_step, 1)
                    v.sem_inc(dve_step, -1)
                    v.tensor_tensor(xcur[:, :, :], xcur[:, :, :], s[:, :].unsqueeze(2).to_broadcast(sh), ALU.mult).then_inc(dve_step, 1)
                    v.wait_ge(dve_step, 1)
                    v.sem_inc(dve_step, -1)

                def root(a):
                    a.wait_ge(to_act, 1)
                    a.sem_inc(to_act, -1)
                    a.activation(s[:, :], m[:, :], ACT.Sqrt).then_inc(act_step, 1)
                    a.wait_ge(act_step, 1)
                    a.sem_inc(act_step, -1)
                    a.sem_inc(from_act, 1)
                vector_stage(f, root)

        def stage_expand(rows, tab, starts, start_i, keep, head, spread):
            w = tab.shape[1]
            copy_out([(nodes_of(tab), rows[:, :, :])])
            with nc.Block() as block:
                c, cl = counted("starts_sent"), counted("starts_loaded")
                base = c.base

                @block.gpsimd
                def _(g):
                    g.indirect_dma_start(out=spread[:, 0, :], out_offset=None, in_=tab,
                                         in_offset=bass.IndirectOffsetOnAxis(ap=head[:, 0:1], axis=0)).then_inc(c.sem, 16)
                    for k in range(NT):
                        g.indirect_dma_start(out=starts, out_offset=bass.IndirectOffsetOnAxis(ap=start_i[:, k:k + 1], axis=0),
                                             in_=rows[:, k, :], in_offset=None).then_inc(c.sem, 16)

                @block.sync
                def _(sp):
                    sp.wait_ge(c.sem, base + 16 * (NT + 1))
                    sp.dma_start(spread[:, 1:J + 1, :], edges_of(starts, w)).then_inc(cl.sem, 16)
                    sp.wait_ge(cl.sem, cl.base + 16)
                    sp.sem_inc(sem("starts_in"), 1)
                c.base += 16 * (NT + 1)
                cl.base += 16

                @block.vector
                def _(v):
                    v.wait_ge(sem("starts_in"), 1)
                    v.sem_inc(sem("starts_in"), -1)
                    v.tensor_copy(spread[:, 1, :], spread[:, 0, :]).then_inc(dve_step, 1)
                    v.wait_ge(dve_step, 1)
                    v.sem_inc(dve_step, -1)
                    for f in range(w):
                        last = v.tensor_tensor_scan(spread[:, 2:J + 1, f], keep[:, 1:J], spread[:, 2:J + 1, f],
                                                    spread[:, 1, f:f + 1], ALU.mult, ALU.add)
                    last.then_inc(dve_step, 1)
                    v.wait_ge(dve_step, 1)
                    v.sem_inc(dve_step, -1)

        def column(buf, k):
            return buf[:, k, :]


        def spline_setup(pseudo, w8, units, starts, dst_f):
            with ExitStack() as st:
                pos = sb(st, "pos", [P, J, D3])
                cell = sb(st, "cell", [P, J, D3])
                tmp = sb(st, "tmp", [P, J, D3])
                ix = sb(st, "ix", [P, J])

                def f(v):
                    v.tensor_scalar(pos[:, :, :], pseudo[:, :, 0:D3], float(KD - 1), None, ALU.mult).then_inc(dve_step, 1)
                    v.wait_ge(dve_step, 1)
                    v.sem_inc(dve_step, -1)
                    v.tensor_scalar(cell[:, :, :], pos[:, :, :], 1.0, None, ALU.is_ge).then_inc(dve_step, 1)
                    v.wait_ge(dve_step, 1)
                    v.sem_inc(dve_step, -1)
                    for k in range(2, KD - 1):
                        v.tensor_scalar(tmp[:, :, :], pos[:, :, :], float(k), None, ALU.is_ge).then_inc(dve_step, 1)
                        v.wait_ge(dve_step, 1)
                        v.sem_inc(dve_step, -1)
                        v.tensor_tensor(cell[:, :, :], cell[:, :, :], tmp[:, :, :], ALU.add).then_inc(dve_step, 1)
                        v.wait_ge(dve_step, 1)
                        v.sem_inc(dve_step, -1)
                    v.tensor_tensor(pos[:, :, :], pos[:, :, :], cell[:, :, :], ALU.subtract).then_inc(dve_step, 1)
                    v.wait_ge(dve_step, 1)
                    v.sem_inc(dve_step, -1)
                    v.tensor_scalar(tmp[:, :, :], pos[:, :, :], -1.0, 1.0, ALU.mult, ALU.add).then_inc(dve_step, 1)
                    v.wait_ge(dve_step, 1)
                    v.sem_inc(dve_step, -1)
                    wgt = (tmp, pos)
                    for b in range(2):
                        for c in range(2):
                            n = 4 * b + 2 * c
                            v.tensor_tensor(w8[:, :, n + 1], wgt[b][:, :, 1], wgt[c][:, :, 2], ALU.mult).then_inc(dve_step, 1)
                            v.wait_ge(dve_step, 1)
                            v.sem_inc(dve_step, -1)
                            v.tensor_tensor(w8[:, :, n], w8[:, :, n + 1], tmp[:, :, 0], ALU.mult).then_inc(dve_step, 1)
                            v.wait_ge(dve_step, 1)
                            v.sem_inc(dve_step, -1)
                            v.tensor_tensor(w8[:, :, n + 1], w8[:, :, n + 1], pos[:, :, 0], ALU.mult).then_inc(dve_step, 1)
                            v.wait_ge(dve_step, 1)
                            v.sem_inc(dve_step, -1)
                    v.tensor_scalar(ix[:, :], dst_f[:, :], float(units), None, ALU.mult).then_inc(dve_step, 1)
                    v.wait_ge(dve_step, 1)
                    v.sem_inc(dve_step, -1)
                    for d, s in enumerate((KD * KD, KD, 1)):
                        v.scalar_tensor_tensor(ix[:, :], cell[:, :, d], float(s), ix[:, :], ALU.mult, ALU.add).then_inc(dve_step, 1)
                        v.wait_ge(dve_step, 1)
                        v.sem_inc(dve_step, -1)
                    v.tensor_copy(starts[0][:, :], ix[:, :]).then_inc(dve_step, 1)
                    v.wait_ge(dve_step, 1)
                    v.sem_inc(dve_step, -1)
                    if len(starts) == 2:
                        v.tensor_scalar(starts[1][:, :], ix[:, :], float(KD * KD), None, ALU.add).then_inc(dve_step, 1)
                        v.wait_ge(dve_step, 1)
                        v.sem_inc(dve_step, -1)
                vector_stage(f)

        class SplineTable:

            def __init__(self, st, arr, kin, w_dram, fo, z, paired):
                self.arr, self.kin, self.fo, self.paired, self.w_dram = arr, kin, fo, paired, w_dram
                self.slots = 2 if paired else 1
                self.n_blocks = KD + 1 - self.slots
                self.zv = z.rearrange("(t p u) o -> p t u o", p=P, u=self.n_blocks * KD * KD)
                self.wsb = sb(st, "wsb", [P, K3, fo])
                self.tiles = sb(st, "tiles", [P, TB, kin])
                self.turned = sb(st, "turned", [P, TB, P])
                self.blocks = [sb(st, f"block{a}", [P, KD * KD, self.slots, fo]) for a in range(self.n_blocks)]
                banks = -(-KD * KD * fo // 512)
                cuts = [KD * KD * n // banks for n in range(banks + 1)]
                self.pieces = list(zip(cuts[:-1], cuts[1:]))
                self.acc = [ps(st, f"planes{n}", [P, banks, 512]) for n in range(2)]
                self.drains = 1 if paired else 2
                self.stored = [counted(f"z_stored{a}") for a in range(self.n_blocks)]
                self.base = [k.base for k in self.stored]
                for k in self.stored:
                    k.base += 16 * (NT + 1)

            def sync(self, sp):
                sp.wait_ge(sem("z_cleared"), 1)
                sp.sem_inc(sem("z_cleared"), -1)
                cut = [K3 * n // self.n_blocks for n in range(self.n_blocks + 1)]
                for a in range(self.n_blocks):
                    sp.dma_start(self.wsb[0:self.kin, cut[a]:cut[a + 1], :],
                                 self.w_dram.rearrange("k i o -> i k o")[:, cut[a]:cut[a + 1], :]).then_inc(self.stored[a].sem, 16)
                for a in range(self.n_blocks):
                    sp.wait_ge(self.stored[a].sem, self.base[a] + 16)
                sp.sem_inc(sem("z_weights_in"), 1)

            def tensor(self, pe):
                pe.wait_ge(sem("z_weights_in"), 1)
                pe.sem_inc(sem("z_weights_in"), -1)
                for g in range(2):
                    pe.sem_inc(sem(f"planes_free{g}"), self.drains)
                with pe.Fori(0, NB):
                    pe.wait_ge(sem("z_tiles_in"), 1)
                    pe.sem_inc(sem("z_tiles_in"), -1)
                    pe.wait_ge(sem("planes_free1"), self.drains)
                    pe.sem_inc(sem("planes_free1"), -self.drains)
                    for k in range(TB):
                        last = pe.transpose(self.acc[1][0:self.kin, k // 4, k % 4 * P:(k % 4 + 1) * P], self.tiles[:, k, :], ident[:, :])
                    last.then_inc(sem("z_tiles_turned"), 1)
                    pe.wait_ge(sem("z_tiles_ready"), 1)
                    pe.sem_inc(sem("z_tiles_ready"), -1)
                    for k in range(TB):
                        for plane in range(KD):
                            g = (k * KD + plane) % 2
                            pe.wait_ge(sem(f"planes_free{g}"), self.drains)
                            pe.sem_inc(sem(f"planes_free{g}"), -self.drains)
                            for n, (lo, hi) in enumerate(self.pieces):
                                cols = self.wsb[:, plane * KD * KD + lo:plane * KD * KD + hi, :].rearrange("i k o -> i (k o)")
                                ins = pe.matmul(self.acc[g][:, n, 0:(hi - lo) * self.fo], self.turned[:, k, :], cols, start=True, stop=True)
                                if n == len(self.pieces) - 1:
                                    ins.then_inc(sem("plane_for_act"), 1)
                                elif n == len(self.pieces) - 2 and not self.paired:
                                    ins.then_inc(sem("plane_for_dve"), 1)
                for g in range(2):
                    pe.wait_ge(sem(f"planes_free{g}"), self.drains)
                    pe.sem_inc(sem(f"planes_free{g}"), -self.drains)

            def drain(self, put, k, plane, slot, first, step):
                for n, (lo, hi) in list(enumerate(self.pieces))[first::step]:
                    last = put(self.blocks[plane - slot][:, lo:hi, slot, :],
                               self.acc[(k * KD + plane) % 2][:, n, 0:(hi - lo) * self.fo].rearrange("p (u o) -> p u o", o=self.fo))
                return last

            def clear(self, v):
                v.memset(self.turned[:, :, :], 0.0)
                v.memset(self.wsb[:, :, :], 0.0).then_inc(dve_step, 1)
                v.wait_ge(dve_step, 1)
                v.sem_inc(dve_step, -1)
                v.sem_inc(sem("z_cleared"), 1)
                v.sem_inc(sem("z_tile_cleared"), 1)

            def vector(self, v):
                with v.Fori(0, NB) as it:
                    for k in range(TB):
                        for plane in range(KD):
                            v.wait_ge(self.stored[plane].sem, it * (16 * TB) + (16 * k + 16 + self.base[plane]))
                            v.sem_inc(dve_step, 1)
                            v.wait_ge(dve_step, 1)
                            v.sem_inc(dve_step, -1)
                            v.wait_ge(sem("plane_for_dve"), 1)
                            v.sem_inc(sem("plane_for_dve"), -1)
                            self.drain(v.tensor_copy, k, plane, 0, 0, 2).then_inc(dve_step, 1)
                            v.wait_ge(dve_step, 1)
                            v.sem_inc(dve_step, -1)
                            v.sem_inc(sem(f"planes_free{(k * KD + plane) % 2}"), 1)
                            v.sem_inc(sem("dve_part_done"), 1)

            def scalar(self, a):
                a.wait_ge(sem("z_tile_cleared"), 1)
                a.sem_inc(sem("z_tile_cleared"), -1)
                with a.Fori(0, NB) as it:
                    a.copy(self.tiles[:, :, :], self.arr[:, bass.ds(it * TB, TB), :]).then_inc(act_step, 1)
                    a.wait_ge(act_step, 1)
                    a.sem_inc(act_step, -1)
                    a.sem_inc(sem("z_tiles_in"), 1)
                    a.wait_ge(sem("z_tiles_turned"), 1)
                    a.sem_inc(sem("z_tiles_turned"), -1)
                    a.copy(self.turned[0:self.kin, 0:4, :].rearrange("i k n -> i (k n)"), self.acc[1][0:self.kin, 0, :])
                    a.copy(self.turned[0:self.kin, 4:TB, :].rearrange("i k n -> i (k n)"),
                           self.acc[1][0:self.kin, 1, 0:(TB - 4) * P]).then_inc(act_step, 1)
                    a.wait_ge(act_step, 1)
                    a.sem_inc(act_step, -1)
                    a.sem_inc(sem("z_tiles_ready"), 1)
                    a.sem_inc(sem("planes_free1"), self.drains)
                    for k in range(TB):
                        for plane in range(KD):
                            if plane < self.n_blocks:
                                a.wait_ge(self.stored[plane].sem, it * (16 * TB) + (16 * k + 16 + self.base[plane]))
                                a.sem_inc(act_step, 1)
                                a.wait_ge(act_step, 1)
                                a.sem_inc(act_step, -1)
                            a.wait_ge(sem("plane_for_act"), 1)
                            a.sem_inc(sem("plane_for_act"), -1)
                            if not self.paired:
                                last = self.drain(a.copy, k, plane, 0, 1, 2)
                            else:
                                if plane < self.n_blocks:
                                    last = self.drain(a.copy, k, plane, 0, 0, 1)
                                if plane > 0:
                                    last = self.drain(a.copy, k, plane, 1, 0, 1)
                            last.then_inc(act_step, 1)
                            a.wait_ge(act_step, 1)
                            a.sem_inc(act_step, -1)
                            a.sem_inc(sem(f"planes_free{(k * KD + plane) % 2}"), 1)
                            full = plane - (self.slots - 1)
                            if full >= 0:
                                if not self.paired:
                                    a.wait_ge(sem("dve_part_done"), 1)
                                    a.sem_inc(sem("dve_part_done"), -1)
                                first = full * KD * KD
                                a.dma_start(self.zv[:, bass.ds(it * TB + k, 1), first:first + KD * KD, :],
                                            self.blocks[full][:, :, :, :].rearrange("p u s o -> p u (s o)").unsqueeze(1)
                                            ).then_inc(self.stored[full].sem, 16)
                for n in range(self.n_blocks):
                    a.wait_ge(self.stored[n].sem, self.base[n] + 16 * (NT + 1))

        def stage_z(arr, kin, w_dram, fo, z):
            with ExitStack() as st, nc.Block() as block:
                table = SplineTable(st, arr, kin, w_dram, fo, z, False)

                @block.sync
                def _(sp):
                    table.sync(sp)

                @block.tensor
                def _(pe):
                    table.tensor(pe)

                @block.vector
                def _(v):
                    table.clear(v)
                    table.vector(v)

                @block.scalar
                def _(a):
                    table.scalar(a)

        def stage_spline_sweep(z, fo, starts, w8, keep, run, tail, ch):
            with ExitStack() as st:
                paired = len(starts) == 1
                shape = [KD + 2, 2, fo] if paired else [2, KD + 2, fo]
                ring = [sb(st, f"ring{b}", [P, ch] + shape) for b in range(2)]
                msg = [sb(st, f"msg{b}", [P, ch, fo]) for b in range(2)]

                def setup(v):
                    v.memset(tail[:, :], 0.0).then_inc(dve_step, 1)
                    v.wait_ge(dve_step, 1)
                    v.sem_inc(dve_step, -1)

                def chunk(v, b, col):
                    if paired:
                        pair = [ring[b][:, :, u, :, :] for u in (0, 1, KD, KD + 1)]
                        first = [(n, 1) for n in (0, 2, 4, 6)]
                    else:
                        pair = [ring[b][:, :, n, m * KD:m * KD + 2, :] for n in range(2) for m in range(2)]
                        first = [(n + 4 * m, 2) for n in range(2) for m in range(2)]
                    for n, (w0, step) in enumerate(first):
                        wgt = w8[:, bass.ds(col, ch), w0:w0 + step + 1:step].unsqueeze(3).to_broadcast([P, ch, 2, fo])
                        last = v.tensor_tensor(pair[n], pair[n], wgt, ALU.mult)
                    last.then_inc(dve_step, 1)
                    v.wait_ge(dve_step, 1)
                    v.sem_inc(dve_step, -1)
                    v.tensor_tensor(pair[0], pair[0], pair[2], ALU.add)
                    v.tensor_tensor(pair[1], pair[1], pair[3], ALU.add).then_inc(dve_step, 1)
                    v.wait_ge(dve_step, 1)
                    v.sem_inc(dve_step, -1)
                    v.tensor_tensor(pair[0], pair[0], pair[1], ALU.add).then_inc(dve_step, 1)
                    v.wait_ge(dve_step, 1)
                    v.sem_inc(dve_step, -1)
                    v.wait_ge(sem(f"out_free{b}"), 1)
                    v.sem_inc(sem(f"out_free{b}"), -1)
                    v.tensor_tensor(msg[b][:, :, :], pair[0][:, :, 0, :], pair[0][:, :, 1, :], ALU.add).then_inc(dve_step, 1)
                    v.wait_ge(dve_step, 1)
                    v.sem_inc(dve_step, -1)
                    v.sem_inc(sem(f"ring_free{b}"), 1)
                    running_sum(v, msg[b], tail, keep, col, ch)
                def whole(buf, k):
                    return buf[:, k, :, :, :].rearrange("p u s o -> p (u s o)")

                def plane(n):
                    return lambda buf, k: buf[:, k, n, :, :].rearrange("p u o -> p (u o)")
                views = [whole] if paired else [plane(0), plane(1)]
                sweep([(z, at, ring, view) for at, view in zip(starts, views)], ch, chunk, (msg, run), setup, apart=True)

        def node_sums(st, run, end_i, open_, tail, width):
            got = sb(st, "got", [P, NT, run.shape[1]])
            with ExitStack() as inner:
                tails = sb(inner, "tails", [P, NT, width])
                stage_ends(run, end_i, open_, got, tail[:, 0:width], tails)

                def add_tails(v):
                    v.tensor_tensor(got[:, :, 0:width], got[:, :, 0:width], tails[:, :, :], ALU.add).then_inc(dve_step, 1)
                    v.wait_ge(dve_step, 1)
                    v.sem_inc(dve_step, -1)
                vector_stage(add_tails)
            return got

        def program():
            with ExitStack() as st:
                zeros = sb(st, "zeros", [P, J * NH])
                negs = sb(st, "negs", [P, NH])
                stage_constants(zeros, negs)
            yield "constants"

            with ExitStack() as lay0:
                deg_s = sb(lay0, "deg_s", [P, NT])
                end_s = sb(lay0, "end_s", [P, NT], I32)
                start_s = sb(lay0, "start_s", [P, NT], I32)
                keep_s = sb(lay0, "keep_s", [P, J])
                open_s = sb(lay0, "open_s", [P, 1])
                head_s = sb(lay0, "head_s", [P, 1], I32)
                dst_s = sb(lay0, "dst_s", [P, J])
                pseudo = sb(lay0, "pseudo", [P, J, D3])
                with ExitStack() as srt:
                    src_f = sb(srt, "src_f", [P, J])
                    pseudo_in = sb(srt, "pseudo_in", [P, J, D3])
                    dst_i = sb(srt, "dst_i", [P, J], I32)
                    payload = sb(srt, "payload", [P, J, 8])
                    stage_load_edges(src_f, key_d, pseudo_in, src_d, dst_i)
                    nxt = t["dst"].rearrange("(e o) -> e o", o=1)[J:E:J, :]
                    stage_order(key_d, nxt, True, keep_d, open_d, head_d)

                    def pack(v):
                        v.memset(payload[:, :, 5:8], 0.0)
                        v.tensor_copy(payload[:, :, 0], src_f[:, :])
                        v.tensor_copy(payload[:, :, 1], key_d[:, :])
                        v.tensor_copy(payload[:, :, 2:5], pseudo_in[:, :, :]).then_inc(dve_step, 1)
                        v.wait_ge(dve_step, 1)
                        v.sem_inc(dve_step, -1)
                    vector_stage(pack)
                    yield "loaded"
                    stage_radix(payload, 0, DLO, sorted1, deg_s, None)
                    copy_out([(payload[:, :, :], edges_of(sorted1, 8))])
                    stage_radix(payload, LOB, DHI, sorted2, None, (xcur, FX, t["L0_gnn_conv_w"], FX, z_conv))
                    stage_bounds(deg_s, end_s, start_s)
                    copy_out([(payload[:, :, :], edges_of(sorted2, 8))])
                    stage_order(payload[:, :, 0], sorted2[J:EP, 0:1][0::J, :], False, keep_s, open_s, head_s)

                    def unpack(v):
                        v.tensor_copy(dst_s[:, :], payload[:, :, 1])
                        v.tensor_copy(pseudo[:, :, :], payload[:, :, 2:5]).then_inc(dve_step, 1)
                        v.wait_ge(dve_step, 1)
                        v.sem_inc(dve_step, -1)
                    vector_stage(unpack)
                yield "sorted"

                rdeg = sb(lay0, "rdeg", [P, NT])

                def inv_deg(v):
                    v.tensor_scalar(rdeg[:, :], deg_s[:, :], 1.0, None, ALU.max).then_inc(dve_step, 1)
                    v.wait_ge(dve_step, 1)
                    v.sem_inc(dve_step, -1)
                    v.reciprocal(rdeg[:, :], rdeg[:, :]).then_inc(dve_step, 1)
                    v.wait_ge(dve_step, 1)
                    v.sem_inc(dve_step, -1)
                vector_stage(inv_deg)

                def normed(v, x, bias, w):
                    sh = [P, NT, w]
                    v.tensor_tensor(x[:, :, :], x[:, :, :], rdeg[:, :].unsqueeze(2).to_broadcast(sh), ALU.mult).then_inc(dve_step, 1)
                    v.wait_ge(dve_step, 1)
                    v.sem_inc(dve_step, -1)
                    v.tensor_tensor(x[:, :, :], x[:, :, :], row(B(bias), sh), ALU.add).then_inc(dve_step, 1)
                    v.wait_ge(dve_step, 1)
                    v.sem_inc(dve_step, -1)

                h1 = sb(lay0, "h1", [P, NT, H1])
                with ExitStack() as st:
                    tail = sb(st, "tail", [P, P])
                    with ExitStack() as s2:
                        hat = sb(s2, "hat", [P, BC, D3, KD])
                        hat2 = sb(s2, "hat2", [P, BC, KD * KD])
                        pos = sb(s2, "pos", [P, BC, D3])
                        bas = [sb(s2, f"bas{b}", [P, BC, P]) for b in range(2)]

                        def setup(v):
                            v.memset(tail[:, :], 0.0)
                            v.memset(bas[0][:, :, :], 0.0)
                            v.memset(bas[1][:, :, :], 0.0).then_inc(dve_step, 1)
                            v.wait_ge(dve_step, 1)
                            v.sem_inc(dve_step, -1)

                        def chunk(v, b, col):
                            v.tensor_scalar(pos[:, :, :], pseudo[:, bass.ds(col, BC), :], float(KD - 1), None, ALU.mult).then_inc(dve_step, 1)
                            v.wait_ge(dve_step, 1)
                            v.sem_inc(dve_step, -1)
                            hatf = hat[:, :, :, :].rearrange("p c d k -> p (c d) k")
                            posf = pos[:, :, :].rearrange("p c d -> p (c d)")
                            v.tensor_tensor(hatf, posf.unsqueeze(2).to_broadcast([P, BC * D3, KD]),
                             iota[:, 0:KD].unsqueeze(1).to_broadcast([P, BC * D3, KD]), ALU.subtract).then_inc(dve_step, 1)
                            v.wait_ge(dve_step, 1)
                            v.sem_inc(dve_step, -1)
                            v.scalar_tensor_tensor(hatf, hatf, -1.0, hatf, ALU.mult, ALU.max).then_inc(dve_step, 1)
                            v.wait_ge(dve_step, 1)
                            v.sem_inc(dve_step, -1)
                            v.tensor_scalar(hatf, hatf, -1.0, 1.0, ALU.mult, ALU.add).then_inc(dve_step, 1)
                            v.wait_ge(dve_step, 1)
                            v.sem_inc(dve_step, -1)
                            v.tensor_scalar(hatf, hatf, 0.0, None, ALU.max).then_inc(dve_step, 1)
                            v.wait_ge(dve_step, 1)
                            v.sem_inc(dve_step, -1)
                            v.tensor_tensor(hat2[:, :, :].rearrange("p c (a b) -> p c a b", a=KD),
                             hat[:, :, 1, :].unsqueeze(3).to_broadcast([P, BC, KD, KD]),
                             hat[:, :, 2, :].unsqueeze(2).to_broadcast([P, BC, KD, KD]), ALU.mult).then_inc(dve_step, 1)
                            v.wait_ge(dve_step, 1)
                            v.sem_inc(dve_step, -1)
                            v.tensor_tensor(bas[b][:, :, 0:K3].rearrange("p c (a b) -> p c a b", a=KD),
                             hat[:, :, 0, :].unsqueeze(3).to_broadcast([P, BC, KD, KD * KD]),
                             hat2[:, :, :].unsqueeze(2).to_broadcast([P, BC, KD, KD * KD]), ALU.mult).then_inc(dve_step, 1)
                            v.wait_ge(dve_step, 1)
                            v.sem_inc(dve_step, -1)
                            running_sum(v, bas[b], tail, keep_s, col, BC)
                        sweep([], BC, chunk, (bas, run_basis), setup)
                    got = node_sums(st, run_basis, end_s, open_s, tail, K3)
                    yield "basis"
                    linear(got, K3, W("L0_gnn_stn1_w")[:, :], H1, h1)

                    def act1(v):
                        normed(v, h1, "L0_gnn_stn1_b", H1)
                    vector_stage(act1)
                    stage_elu(h1)
                yield "h1"
                w8 = sb(lay0, "w8", [P, J, 8])
                cell_i = [sb(lay0, f"cell{n}", [P, J], I32) for n in range(2)]
                stage_z(h1, H1, t["L0_gnn_stn2_w"], H1, z_stn2)
                spline_setup(pseudo, w8, K3, cell_i, dst_s)
                yield "z2"
                tt = sb(lay0, "tt", [P, NT, 4])
                with ExitStack() as st:
                    tail = sb(st, "tail", [P, H1])
                    stage_spline_sweep(z_stn2, H1, cell_i, w8, keep_s, run_stn2, tail, CC)
                    got = node_sums(st, run_stn2, end_s, open_s, tail, H1)

                    def act2(v):
                        normed(v, got, "L0_gnn_stn2_b", H1)
                    vector_stage(act2)
                    stage_elu(got)
                    linear(got, H1, W("L0_gnn_stn3_w")[:, :], H1, h1)

                    def act3(v):
                        v.tensor_tensor(h1[:, :, :], h1[:, :, :], row(B("L0_gnn_stn3_b"), [P, NT, H1]), ALU.add).then_inc(dve_step, 1)
                        v.wait_ge(dve_step, 1)
                        v.sem_inc(dve_step, -1)
                        v.memset(tt[:, :, :], 0.0).then_inc(dve_step, 1)
                        v.wait_ge(dve_step, 1)
                        v.sem_inc(dve_step, -1)
                    vector_stage(act3)
                    stage_elu(h1)
                    linear(h1, H1, W("L0_gnn_stn4_w")[:, :], D3, tt)

                    def bias4(v):
                        v.tensor_tensor(tt[:, :, 0:D3], tt[:, :, 0:D3], row(B("L0_gnn_stn4_b"), [P, NT, D3]), ALU.add).then_inc(dve_step, 1)
                        v.wait_ge(dve_step, 1)
                        v.sem_inc(dve_step, -1)
                    vector_stage(bias4)
                yield "t"
                with ExitStack() as st:
                    spread = sb(st, "spread", [P, J + 1, 4])
                    stage_expand(tt, tab_t, starts_t, start_s, keep_s, head_s, spread)
                    dst_si = sb(st, "dst_si", [P, J], I32)

                    def targets(v):
                        v.tensor_copy(dst_si[:, :], dst_s[:, :]).then_inc(dve_step, 1)
                        v.wait_ge(dve_step, 1)
                        v.sem_inc(dve_step, -1)
                    vector_stage(targets)
                    ring = [sb(st, f"ring{b}", [P, CH, 4]) for b in range(2)]
                    hist = Histogram(st, key_d[:, :], deg_d)

                    def chunk(v, b, col):
                        hist.make(v, col)
                        hist.add(v)
                        ptr = pseudo[:, bass.ds(col, CH), :]
                        v.tensor_tensor(ring[b][:, :, 0:D3], ring[b][:, :, 0:D3], ptr, ALU.add).then_inc(dve_step, 1)
                        v.wait_ge(dve_step, 1)
                        v.sem_inc(dve_step, -1)
                        v.tensor_tensor(ring[b][:, :, 0:D3], ring[b][:, :, 0:D3], spread[:, bass.ds(col + 1, CH), 0:D3], ALU.subtract).then_inc(dve_step, 1)
                        v.wait_ge(dve_step, 1)
                        v.sem_inc(dve_step, -1)
                        v.tensor_scalar(ptr, ring[b][:, :, 0:D3], 0.0, 1.0, ALU.max, ALU.min).then_inc(dve_step, 1)
                        v.wait_ge(dve_step, 1)
                        v.sem_inc(dve_step, -1)
                    sweep([(tab_t, dst_si, ring, column)], CH, chunk, None, hist.setup, hist.tensor)
                stage_bounds(deg_d, end_d, start_d)
                spline_setup(pseudo, w8, K3P, cell_i[0:1], dst_s)
                yield "z3"
                with ExitStack() as st:
                    tail = sb(st, "tail", [P, FX])
                    stage_spline_sweep(z_conv, FX, cell_i[0:1], w8, keep_s, run_conv, tail, CH)
                    got = node_sums(st, run_conv, end_s, open_s, tail, FX)

                    def mean_bias(v):
                        normed(v, got, "L0_gnn_conv_b", FX)
                    vector_stage(mean_bias)
                    stage_layernorm(got)
            yield "layer0"

            with ExitStack() as lay1:
                neg_d = sb(lay1, "neg_d", [P, J])

                def marks(v):
                    v.tensor_scalar(neg_d[:, :], keep_d[:, :], -1.0, BIG, ALU.add, ALU.mult).then_inc(dve_step, 1)
                    v.wait_ge(dve_step, 1)
                    v.sem_inc(dve_step, -1)
                vector_stage(marks)
                h = sb(lay1, "h", [P, NT, HC])
                for layer in (1, 2, 3):
                    last = layer == 3
                    with ExitStack() as st:
                        vals = sb(st, "vals", [P, NT, HW])
                        al_d = sb(st, "al_d", [P, NT, NH])
                        mx = sb(st, "mx", [P, NT, NH])
                        e_self = sb(st, "e_self", [P, NT, NH])
                        width = NH * FX if last else HC
                        with ExitStack() as s2:
                            xw = sb(s2, "xw", [P, NT, width])
                            prod = sb(s2, "prod", [P, NT, width])
                            src_arr, k_in = (xcur, FX) if layer == 1 else (h, HC)
                            linear(src_arr, k_in, W(f"L1_gnn_W{layer}")[:, :], width, xw)

                            def terms(v):
                                sh = [P, NT, width]
                                per = width // NH
                                for name, res in (("src", vals[:, :, 0:NH]), ("dst", al_d[:, :, :])):
                                    v.tensor_tensor(prod[:, :, :], xw[:, :, :], row(B(f"L1_gnn_a_{name}{layer}"), sh), ALU.mult).then_inc(dve_step, 1)
                                    v.wait_ge(dve_step, 1)
                                    v.sem_inc(dve_step, -1)
                                    v.tensor_reduce(res, prod[:, :, :].rearrange("p t (h c) -> p t h c", h=NH), AXX, ALU.add).then_inc(dve_step, 1)
                                    v.wait_ge(dve_step, 1)
                                    v.sem_inc(dve_step, -1)
                                v.tensor_copy(vals[:, :, NH:HW], (h if last else xw)[:, :, :]).then_inc(dve_step, 1)
                                v.wait_ge(dve_step, 1)
                                v.sem_inc(dve_step, -1)
                                v.tensor_tensor(e_self[:, :, :], vals[:, :, 0:NH], al_d[:, :, :], ALU.add).then_inc(dve_step, 1)
                                v.wait_ge(dve_step, 1)
                                v.sem_inc(dve_step, -1)
                                v.scalar_tensor_tensor(e_self[:, :, :], e_self[:, :, :], 0.2, e_self[:, :, :], ALU.mult, ALU.max).then_inc(dve_step, 1)
                                v.wait_ge(dve_step, 1)
                                v.sem_inc(dve_step, -1)
                            vector_stage(terms)
                        copy_out([(nodes_of(tab_gat), vals[:, :, :])])
                        tail = sb(st, "tail", [P, HW3 if last else HW])
                        with ExitStack() as res:
                            edge = sb(res, "edge", [P, J, HW])
                            tmax = sb(res, "tmax", [P, NH])
                            per_edge = ExitStack()
                            spread = sb(per_edge, "spread", [P, J + 1, NH])
                            stage_expand(al_d, tab_h, starts_h, start_d, keep_d, head_d, spread)
                            with ExitStack() as s2:
                                ring = [sb(s2, f"ring{b}", [P, CH, HW]) for b in range(2)]
                                mxb = [sb(s2, f"mxb{b}", [P, CH, NH]) for b in range(2)]

                                def setup(v):
                                    v.memset(tmax[:, :], -BIG).then_inc(dve_step, 1)
                                    v.wait_ge(dve_step, 1)
                                    v.sem_inc(dve_step, -1)

                                def chunk(v, b, col):
                                    lg = edge[:, bass.ds(col, CH), 0:NH]
                                    v.tensor_copy(edge[:, bass.ds(col, CH), NH:HW], ring[b][:, :, NH:HW])
                                    v.tensor_tensor(ring[b][:, :, 0:NH], ring[b][:, :, 0:NH], spread[:, bass.ds(col + 1, CH), :], ALU.add).then_inc(dve_step, 1)
                                    v.wait_ge(dve_step, 1)
                                    v.sem_inc(dve_step, -1)
                                    v.scalar_tensor_tensor(lg, ring[b][:, :, 0:NH], 0.2, ring[b][:, :, 0:NH], ALU.mult, ALU.max).then_inc(dve_step, 1)
                                    v.wait_ge(dve_step, 1)
                                    v.sem_inc(dve_step, -1)
                                    for f in range(NH):
                                        scan = v.tensor_tensor_scan(mxb[b][:, :, f], neg_d[:, bass.ds(col, CH)],
                                                                    edge[:, bass.ds(col, CH), f:f + 1].rearrange("p j o -> p (j o)"),
                                                                    tmax[:, f:f + 1], ALU.add, ALU.max)
                                    scan.then_inc(dve_step, 1)
                                    v.wait_ge(dve_step, 1)
                                    v.sem_inc(dve_step, -1)
                                    v.tensor_copy(tmax[:, :], mxb[b][:, CH - 1, :]).then_inc(dve_step, 1)
                                    v.wait_ge(dve_step, 1)
                                    v.sem_inc(dve_step, -1)
                                sweep([(tab_gat, src_d, ring, column)], CH, chunk, (mxb, run_max), setup)
                            with ExitStack() as s2:
                                rhs = sb(s2, "rhs", [P, 2 * NH])
                                keys = sb(s2, "keys", [NH, P])
                                tmt = sb(s2, "tmt", [NH, P])
                                cut = sb(s2, "cut", [NH, P])
                                run2 = sb(s2, "run2", [NH, P])
                                lst = sb(s2, "lst", [NH, P])
                                with nc.Block() as block:
                                    a1 = ps(s2, "a1", [NH, P])
                                    a2 = ps(s2, "a2", [NH, P])
                                    a3 = ps(s2, "a3", [P, 2, 2 * NH])

                                    @block.tensor
                                    def _(pe):
                                        pe.transpose(a1[:, :], tmax[:, :], ident[:, :])
                                        pe.transpose(a2[:, :], open_d[:, 0:1].to_broadcast([P, NH]), ident[:, :]).then_inc(sem("tails_turned"), 1)
                                        pe.wait_ge(sem("tails_scanned"), 1)
                                        pe.sem_inc(sem("tails_scanned"), -1)
                                        pe.transpose(a3[:, 0, 0:NH], run2[:, :], ident[0:NH, 0:NH])
                                        pe.transpose(a3[:, 1, 0:NH], lst[:, :], ident[0:NH, 0:NH]).then_inc(sem("tails_back"), 1)

                                    @block.vector
                                    def _(v):
                                        v.wait_ge(sem("tails_turned"), 1)
                                        v.sem_inc(sem("tails_turned"), -1)
                                        v.tensor_copy(tmt[:, :], a1[:, :])
                                        v.memset(lst[:, :], 1.0)
                                        v.memset(cut[:, :], 0.0)
                                        v.tensor_copy(keys[:, :], a2[:, :]).then_inc(dve_step, 1)
                                        v.wait_ge(dve_step, 1)
                                        v.sem_inc(dve_step, -1)
                                        v.tensor_tensor(cut[:, 1:P], keys[:, 1:P], keys[:, 0:P - 1], ALU.is_equal)
                                        v.tensor_tensor(lst[:, 0:P - 1], keys[:, 1:P], keys[:, 0:P - 1], ALU.not_equal).then_inc(dve_step, 1)
                                        v.wait_ge(dve_step, 1)
                                        v.sem_inc(dve_step, -1)
                                        v.tensor_scalar(cut[:, :], cut[:, :], -1.0, BIG, ALU.add, ALU.mult).then_inc(dve_step, 1)
                                        v.wait_ge(dve_step, 1)
                                        v.sem_inc(dve_step, -1)
                                        v.tensor_tensor_scan(run2[:, :], cut[:, :], tmt[:, :], 0.0, ALU.add, ALU.max).then_inc(dve_step, 1)
                                        v.wait_ge(dve_step, 1)
                                        v.sem_inc(dve_step, -1)
                                        v.tensor_tensor(run2[:, :], run2[:, :], lst[:, :], ALU.mult).then_inc(dve_step, 1)
                                        v.wait_ge(dve_step, 1)
                                        v.sem_inc(dve_step, -1)
                                        v.sem_inc(sem("tails_scanned"), 1)
                                        v.wait_ge(sem("tails_back"), 1)
                                        v.sem_inc(sem("tails_back"), -1)
                                        v.tensor_copy(rhs[:, 0:NH], a3[:, 0, 0:NH])
                                        v.tensor_copy(rhs[:, NH:2 * NH], a3[:, 1, 0:NH]).then_inc(dve_step, 1)
                                        v.wait_ge(dve_step, 1)
                                        v.sem_inc(dve_step, -1)
                                tails = sb(s2, "tails", [P, NT, 2 * NH])
                                stage_ends(run_max, end_d, open_d, mx, rhs[:, :], tails)

                                def combine(v):
                                    v.tensor_scalar(tails[:, :, NH:2 * NH], tails[:, :, NH:2 * NH], -1.0, BIG, ALU.add, ALU.mult).then_inc(dve_step, 1)
                                    v.wait_ge(dve_step, 1)
                                    v.sem_inc(dve_step, -1)
                                    v.tensor_tensor(tails[:, :, 0:NH], tails[:, :, 0:NH], tails[:, :, NH:2 * NH], ALU.add).then_inc(dve_step, 1)
                                    v.wait_ge(dve_step, 1)
                                    v.sem_inc(dve_step, -1)
                                    v.tensor_tensor(mx[:, :, :], mx[:, :, :], tails[:, :, 0:NH], ALU.max).then_inc(dve_step, 1)
                                    v.wait_ge(dve_step, 1)
                                    v.sem_inc(dve_step, -1)
                                    v.tensor_tensor(mx[:, :, :], mx[:, :, :], e_self[:, :, :], ALU.max).then_inc(dve_step, 1)
                                    v.wait_ge(dve_step, 1)
                                    v.sem_inc(dve_step, -1)
                                    v.tensor_tensor(e_self[:, :, :], e_self[:, :, :], mx[:, :, :], ALU.subtract).then_inc(dve_step, 1)
                                    v.wait_ge(dve_step, 1)
                                    v.sem_inc(dve_step, -1)
                                    v.sem_inc(to_act, 1)

                                def exp_self(a):
                                    a.wait_ge(to_act, 1)
                                    a.sem_inc(to_act, -1)
                                    a.activation(e_self[:, :, :], e_self[:, :, :], ACT.Exp).then_inc(act_step, 1)
                                    a.wait_ge(act_step, 1)
                                    a.sem_inc(act_step, -1)
                                vector_stage(combine, exp_self)
                            stage_expand(mx, tab_h, starts_h, start_d, keep_d, head_d, spread)

                            def exps(v):
                                v.tensor_tensor(edge[:, :, 0:NH], edge[:, :, 0:NH], spread[:, 1:J + 1, :], ALU.subtract).then_inc(dve_step, 1)
                                v.wait_ge(dve_step, 1)
                                v.sem_inc(dve_step, -1)
                                v.sem_inc(to_act, 1)
                                v.wait_ge(from_act, 1)
                                v.sem_inc(from_act, -1)
                                if not last:
                                    ev = edge[:, :, NH:HW].rearrange("p j (h c) -> p j h c", h=NH)
                                    v.tensor_tensor(ev, ev, edge[:, :, 0:NH].unsqueeze(3).to_broadcast([P, J, NH, NC]), ALU.mult).then_inc(dve_step, 1)
                                    v.wait_ge(dve_step, 1)
                                    v.sem_inc(dve_step, -1)
                                    for f in range(HW):
                                        scan = v.tensor_tensor_scan(edge[:, :, f], keep_d[:, :], edge[:, :, f], 0.0, ALU.mult, ALU.add)
                                    scan.then_inc(dve_step, 1)
                                    v.wait_ge(dve_step, 1)
                                    v.sem_inc(dve_step, -1)
                                    v.tensor_copy(tail[:, :], edge[:, J - 1, :]).then_inc(dve_step, 1)
                                    v.wait_ge(dve_step, 1)
                                    v.sem_inc(dve_step, -1)

                            def exp_edges(a):
                                a.wait_ge(to_act, 1)
                                a.sem_inc(to_act, -1)
                                a.activation(edge[:, :, 0:NH], edge[:, :, 0:NH], ACT.Exp).then_inc(act_step, 1)
                                a.wait_ge(act_step, 1)
                                a.sem_inc(act_step, -1)
                                a.sem_inc(from_act, 1)
                            vector_stage(exps, exp_edges)
                            per_edge.close()
                            if not last:
                                copy_out([(edges_of(run_gat, HW), edge[:, :, :])])
                            else:
                                with ExitStack() as s2:
                                    third = HW3 // 3
                                    part_done = [sem(f"part_done{n}") for n in range(3)]
                                    wv = [sb(s2, f"wv{b}", [P, CC, HW3]) for b in range(2)]

                                    def setup3(v):
                                        v.memset(tail[:, :], 0.0).then_inc(dve_step, 1)
                                        v.wait_ge(dve_step, 1)
                                        v.sem_inc(dve_step, -1)

                                    def weigh(g, b, col):
                                        g.tensor_copy(wv[b][:, :, 0:NH], edge[:, bass.ds(col, CC), 0:NH])
                                        g.tensor_tensor(wv[b][:, :, NH:HW3].rearrange("p j (h c) -> p j h c", h=NH),
                                                        edge[:, bass.ds(col, CC), 0:NH].unsqueeze(3).to_broadcast([P, CC, NH, HC]),
                                                        edge[:, bass.ds(col, CC), NH:HW].unsqueeze(2).to_broadcast([P, CC, NH, HC]), ALU.mult).then_inc(pool_step, 1)
                                        g.wait_ge(pool_step, 1)
                                        g.sem_inc(pool_step, -1)

                                    def chunk3(v, b, col):
                                        for k in range(CC):
                                            for n in range(3):
                                                part = slice(n * third, (n + 1) * third)
                                                if k:
                                                    v.wait_ge(part_done[n], 1)
                                                    v.sem_inc(part_done[n], -1)
                                                v.scalar_tensor_tensor(wv[b][:, k, part], wv[b][:, k - 1, part] if k else tail[:, part],
                                                                       keep_d[:, bass.ds(col + k, 1)], wv[b][:, k, part],
                                                                       ALU.mult, ALU.add).then_inc(part_done[n], 1)
                                        for n in range(3):
                                            v.wait_ge(part_done[n], 1)
                                            v.sem_inc(part_done[n], -1)
                                        v.tensor_copy(tail[:, :], wv[b][:, CC - 1, :]).then_inc(dve_step, 1)
                                        v.wait_ge(dve_step, 1)
                                        v.sem_inc(dve_step, -1)
                                    sweep([], CC, chunk3, (wv, run_gat3), setup3, prepare=weigh)
                        width = HW3 if last else HW
                        got = node_sums(st, run_gat3 if last else run_gat, end_d, open_d, tail, width)
                        with ExitStack() as s2:
                            tmp = sb(s2, "tmp", [P, NT, width - NH])

                            def finish(v):
                                per = HC if last else NC
                                sh = [P, NT, NH, per]
                                tv = tmp[:, :, :].rearrange("p t (h c) -> p t h c", h=NH)
                                gv = got[:, :, NH:width].rearrange("p t (h c) -> p t h c", h=NH)
                                val = vals[:, :, NH:HW].unsqueeze(2).to_broadcast(sh) if last else \
                                    vals[:, :, NH:HW].rearrange("p t (h c) -> p t h c", h=NH)
                                v.tensor_tensor(tv, e_self[:, :, :].unsqueeze(3).to_broadcast(sh), val, ALU.mult).then_inc(dve_step, 1)
                                v.wait_ge(dve_step, 1)
                                v.sem_inc(dve_step, -1)
                                v.tensor_tensor(got[:, :, NH:width], got[:, :, NH:width], tmp[:, :, :], ALU.add).then_inc(dve_step, 1)
                                v.wait_ge(dve_step, 1)
                                v.sem_inc(dve_step, -1)
                                v.tensor_tensor(got[:, :, 0:NH], got[:, :, 0:NH], e_self[:, :, :], ALU.add).then_inc(dve_step, 1)
                                v.wait_ge(dve_step, 1)
                                v.sem_inc(dve_step, -1)
                                v.reciprocal(got[:, :, 0:NH], got[:, :, 0:NH]).then_inc(dve_step, 1)
                                v.wait_ge(dve_step, 1)
                                v.sem_inc(dve_step, -1)
                                v.tensor_tensor(gv, gv, got[:, :, 0:NH].unsqueeze(3).to_broadcast(sh), ALU.mult).then_inc(dve_step, 1)
                                v.wait_ge(dve_step, 1)
                                v.sem_inc(dve_step, -1)
                                if not last:
                                    v.tensor_tensor(h[:, :, :], got[:, :, NH:HW], row(B(f"L1_gnn_b{layer}"), [P, NT, HC]), ALU.add).then_inc(dve_step, 1)
                                    v.wait_ge(dve_step, 1)
                                    v.sem_inc(dve_step, -1)
                                    v.tensor_scalar(h[:, :, :], h[:, :, :], 0.0, None, ALU.max).then_inc(dve_step, 1)
                                    v.wait_ge(dve_step, 1)
                                    v.sem_inc(dve_step, -1)
                            vector_stage(finish)
                        if last:
                            o3 = sb(st, "o3", [P, NT, FX])
                            stage_linear(got, [(NH, NH + W3H, w3a[:, :]), (NH + W3H, HW3, w3b[:, :])], FX, o3)
                            full = N // P
                            y = sb(st, "y", [P, NT, FX])
                            m1 = sb(st, "m1", [P, FX])
                            m2 = sb(st, "m2", [P, FX])
                            with nc.Block() as block:
                                @block.vector
                                def _(v):
                                    sh = [P, NT, FX]
                                    v.tensor_scalar(o3[:, :, :], o3[:, :, :], 1.0 / NH, None, ALU.mult).then_inc(dve_step, 1)
                                    v.wait_ge(dve_step, 1)
                                    v.sem_inc(dve_step, -1)
                                    v.memset(y[:, :, :], -BIG).then_inc(dve_step, 1)
                                    v.wait_ge(dve_step, 1)
                                    v.sem_inc(dve_step, -1)
                                    v.tensor_tensor(y[:, 0:full, :], o3[:, 0:full, :], row(B("L1_gnn_b3"), [P, full, FX]), ALU.add)
                                    if N % P:
                                        q = N % P
                                        v.tensor_tensor(y[0:q, full, :], o3[0:q, full, :], B("L1_gnn_b3")[0:q, :], ALU.add)
                                    v.memset(m2[:, :], 0.0).then_inc(dve_step, 1)
                                    v.wait_ge(dve_step, 1)
                                    v.sem_inc(dve_step, -1)
                                    v.tensor_reduce(m1[:, :], y[:, :, :].rearrange("p t f -> p f t"), AXX, ALU.max).then_inc(dve_step, 1)
                                    v.wait_ge(dve_step, 1)
                                    v.sem_inc(dve_step, -1)
                                    v.sem_inc(sem("lane_max"), 1)
                                    v.wait_ge(sem("node_max"), 1)
                                    v.sem_inc(sem("node_max"), -1)
                                    v.tensor_tensor(y[:, :, :], y[:, :, :], row(m2, sh), ALU.subtract).then_inc(dve_step, 1)
                                    v.wait_ge(dve_step, 1)
                                    v.sem_inc(dve_step, -1)
                                    v.sem_inc(sem("shifted"), 1)
                                    v.wait_ge(sem("exp_done"), 1)
                                    v.sem_inc(sem("exp_done"), -1)
                                    v.tensor_reduce(m1[:, :], y[:, :, :].rearrange("p t f -> p f t"), AXX, ALU.add).then_inc(dve_step, 1)
                                    v.wait_ge(dve_step, 1)
                                    v.sem_inc(dve_step, -1)
                                    v.sem_inc(sem("lane_sum"), 1)
                                    v.wait_ge(sem("node_sum"), 1)
                                    v.sem_inc(sem("node_sum"), -1)
                                    v.reciprocal(m2[:, :], m2[:, :]).then_inc(dve_step, 1)
                                    v.wait_ge(dve_step, 1)
                                    v.sem_inc(dve_step, -1)
                                    v.tensor_tensor(y[:, :, :], y[:, :, :], row(m2, sh), ALU.mult).then_inc(dve_step, 1)
                                    v.wait_ge(dve_step, 1)
                                    v.sem_inc(dve_step, -1)

                                @block.scalar
                                def _(a):
                                    a.wait_ge(sem("shifted"), 1)
                                    a.sem_inc(sem("shifted"), -1)
                                    a.activation(y[:, :, :], y[:, :, :], ACT.Exp).then_inc(act_step, 1)
                                    a.wait_ge(act_step, 1)
                                    a.sem_inc(act_step, -1)
                                    a.sem_inc(sem("exp_done"), 1)

                                @block.gpsimd
                                def _(g):
                                    for op, need, done in ((RMAX, "lane_max", "node_max"), (RADD, "lane_sum", "node_sum")):
                                        g.wait_ge(sem(need), 1)
                                        g.sem_inc(sem(need), -1)
                                        g.partition_all_reduce(m2[:, :], m1[:, :], P, op).then_inc(pool_step, 1)
                                        g.wait_ge(pool_step, 1)
                                        g.sem_inc(pool_step, -1)
                                        g.sem_inc(sem(done), 1)
                            stage_layernorm(y)
                    yield f"gat{layer}"

            def gather_sums(st, rows, tab, run):
                w = tab.shape[1]
                copy_out([(nodes_of(tab), rows[:, :, :])])
                tail = sb(st, "tail", [P, w])
                with ExitStack() as s2:
                    ring = [sb(s2, f"ring{b}", [P, CH, w]) for b in range(2)]

                    def setup(v):
                        v.memset(tail[:, :], 0.0).then_inc(dve_step, 1)
                        v.wait_ge(dve_step, 1)
                        v.sem_inc(dve_step, -1)

                    def chunk(v, b, col):
                        running_sum(v, ring[b], tail, keep_d, col, CH)
                    sweep([(tab, src_d, ring, column)], CH, chunk, (ring, run), setup)
                return node_sums(st, run, end_d, open_d, tail, w)

            with ExitStack() as lay2:
                dinv = sb(lay2, "dinv", [P, NT])
                xn = sb(lay2, "xn", [P, NT, FG])
                g2 = sb(lay2, "g2", [P, NT, FX])
                with nc.Block() as block:
                    c = counted("vec_load")

                    @block.sync
                    def _(sp):
                        sp.wait_ge(sem("vec_zeroed"), 1)
                        sp.sem_inc(sem("vec_zeroed"), -1)
                        full = N // P
                        nv = t["node_vec1"]
                        with nc.allow_non_contiguous_dma(reason="one value per node"):
                            sp.dma_start(xn[:, 0:full, FX:FG], nv[0:full * P, :].rearrange("(t p) f -> p t f", p=P)).then_inc(c.sem, 16)
                            if N % P:
                                sp.dma_start(xn[0:N % P, full, FX:FG], nv[full * P:N, :]).then_inc(c.sem, 16)
                                c.base += 16
                        c.base += 16
                        sp.wait_ge(c.sem, c.base)

                    @block.vector
                    def _(v):
                        v.memset(xn[:, :, :], 0.0).then_inc(dve_step, 1)
                        v.wait_ge(dve_step, 1)
                        v.sem_inc(dve_step, -1)
                        v.sem_inc(sem("vec_zeroed"), 1)

                def scale_in(v):
                    v.tensor_copy(xn[:, :, 0:FX], xcur[:, :, :]).then_inc(dve_step, 1)
                    v.wait_ge(dve_step, 1)
                    v.sem_inc(dve_step, -1)
                    v.tensor_scalar(dinv[:, :], deg_d[:, :], 1.0, None, ALU.add).then_inc(dve_step, 1)
                    v.wait_ge(dve_step, 1)
                    v.sem_inc(dve_step, -1)
                    v.sem_inc(to_act, 1)
                    v.wait_ge(from_act, 1)
                    v.sem_inc(from_act, -1)
                    v.reciprocal(dinv[:, :], dinv[:, :]).then_inc(dve_step, 1)
                    v.wait_ge(dve_step, 1)
                    v.sem_inc(dve_step, -1)
                    v.tensor_tensor(xn[:, :, :], xn[:, :, :], dinv[:, :].unsqueeze(2).to_broadcast([P, NT, FG]), ALU.mult).then_inc(dve_step, 1)
                    v.wait_ge(dve_step, 1)
                    v.sem_inc(dve_step, -1)

                def root(a):
                    a.wait_ge(to_act, 1)
                    a.sem_inc(to_act, -1)
                    a.activation(dinv[:, :], dinv[:, :], ACT.Sqrt).then_inc(act_step, 1)
                    a.wait_ge(act_step, 1)
                    a.sem_inc(act_step, -1)
                    a.sem_inc(from_act, 1)
                vector_stage(scale_in, root)
                with ExitStack() as st:
                    got = gather_sums(st, xn, tab_gcn1, run_gcn)
                    hid = sb(st, "hid", [P, NT, HID])

                    def own(v):
                        v.tensor_tensor(got[:, :, :], got[:, :, :], xn[:, :, :], ALU.add).then_inc(dve_step, 1)
                        v.wait_ge(dve_step, 1)
                        v.sem_inc(dve_step, -1)
                        v.tensor_tensor(got[:, :, :], got[:, :, :], dinv[:, :].unsqueeze(2).to_broadcast([P, NT, FG]), ALU.mult).then_inc(dve_step, 1)
                        v.wait_ge(dve_step, 1)
                        v.sem_inc(dve_step, -1)
                    vector_stage(own)
                    linear(got, FG, W("L2_gnn_W1")[:, :], HID, hid)

                    def relu(v):
                        v.tensor_tensor(hid[:, :, :], hid[:, :, :], row(B("L2_gnn_b1"), [P, NT, HID]), ALU.add).then_inc(dve_step, 1)
                        v.wait_ge(dve_step, 1)
                        v.sem_inc(dve_step, -1)
                        v.tensor_scalar(hid[:, :, :], hid[:, :, :], 0.0, None, ALU.max).then_inc(dve_step, 1)
                        v.wait_ge(dve_step, 1)
                        v.sem_inc(dve_step, -1)
                    vector_stage(relu)
                    linear(hid, HID, W("L2_gnn_W2")[:, :], FX, g2)

                    def scale2(v):
                        v.tensor_tensor(g2[:, :, :], g2[:, :, :], dinv[:, :].unsqueeze(2).to_broadcast([P, NT, FX]), ALU.mult).then_inc(dve_step, 1)
                        v.wait_ge(dve_step, 1)
                        v.sem_inc(dve_step, -1)
                    vector_stage(scale2)
                with ExitStack() as st:
                    got = gather_sums(st, g2, tab_gcn2, run_conv)

                    def own2(v):
                        v.tensor_tensor(got[:, :, :], got[:, :, :], g2[:, :, :], ALU.add).then_inc(dve_step, 1)
                        v.wait_ge(dve_step, 1)
                        v.sem_inc(dve_step, -1)
                        v.tensor_tensor(got[:, :, :], got[:, :, :], dinv[:, :].unsqueeze(2).to_broadcast([P, NT, FX]), ALU.mult).then_inc(dve_step, 1)
                        v.wait_ge(dve_step, 1)
                        v.sem_inc(dve_step, -1)
                        v.tensor_tensor(got[:, :, :], got[:, :, :], row(B("L2_gnn_b2"), [P, NT, FX]), ALU.add).then_inc(dve_step, 1)
                        v.wait_ge(dve_step, 1)
                        v.sem_inc(dve_step, -1)
                    vector_stage(own2)
                    stage_layernorm(got)
            yield "gcn"

            with ExitStack() as lay3:
                rdeg = sb(lay3, "rdeg", [P, NT])
                hop = sb(lay3, "hop", [P, NT, FX])
                total = sb(lay3, "total", [P, NT, FX])

                def begin(v):
                    v.tensor_scalar(rdeg[:, :], deg_d[:, :], 1.0, None, ALU.max).then_inc(dve_step, 1)
                    v.wait_ge(dve_step, 1)
                    v.sem_inc(dve_step, -1)
                    v.reciprocal(rdeg[:, :], rdeg[:, :]).then_inc(dve_step, 1)
                    v.wait_ge(dve_step, 1)
                    v.sem_inc(dve_step, -1)
                    v.tensor_copy(hop[:, :, :], xcur[:, :, :])
                    v.tensor_scalar(total[:, :, :], xcur[:, :, :], 0.25, None, ALU.mult).then_inc(dve_step, 1)
                    v.wait_ge(dve_step, 1)
                    v.sem_inc(dve_step, -1)
                vector_stage(begin)
                for k in range(3):
                    with ExitStack() as st:
                        got = gather_sums(st, hop, tab_gcn2, run_conv)

                        def mean(v):
                            v.tensor_tensor(hop[:, :, :], got[:, :, :], rdeg[:, :].unsqueeze(2).to_broadcast([P, NT, FX]), ALU.mult).then_inc(dve_step, 1)
                            v.wait_ge(dve_step, 1)
                            v.sem_inc(dve_step, -1)
                            v.scalar_tensor_tensor(total[:, :, :], hop[:, :, :], 0.25, total[:, :, :], ALU.mult, ALU.add).then_inc(dve_step, 1)
                            v.wait_ge(dve_step, 1)
                            v.sem_inc(dve_step, -1)
                        vector_stage(mean)
                stage_layernorm(total)
            full = N // P
            pairs = [(out[0:full * P, :].rearrange("(t p) f -> p t f", p=P), xcur[:, 0:full, :])]
            if N % P:
                pairs.append((out[full * P:N, :], xcur[0:N % P, full, :]))
            copy_out(pairs)
            yield "out"

        steps = program()
        for name in steps:
            if name == stop:
                steps.close()
                break


_INS = ["x", "src", "dst", "edge_attr_3", "node_vec1",
        "L0_gnn_stn1_w", "L0_gnn_stn1_b", "L0_gnn_stn2_w", "L0_gnn_stn2_b", "L0_gnn_stn3_w", "L0_gnn_stn3_b",
        "L0_gnn_stn4_w", "L0_gnn_stn4_b", "L0_gnn_conv_w", "L0_gnn_conv_b",
        "L1_gnn_W1", "L1_gnn_a_src1", "L1_gnn_a_dst1", "L1_gnn_b1", "L1_gnn_W2", "L1_gnn_a_src2", "L1_gnn_a_dst2",
        "L1_gnn_b2", "L1_gnn_W3", "L1_gnn_a_src3", "L1_gnn_a_dst3", "L1_gnn_b3",
        "L2_gnn_W1", "L2_gnn_b1", "L2_gnn_W2", "L2_gnn_b2"]


def kernel(**inputs):
    import numpy as _np
    import concourse.bacc as _bacc
    from concourse import mybir as _mybir
    from concourse.bass_utils import run_bass_kernel_spmd as _run

    nc = _bacc.Bacc("TRN2", target_bir_lowering=False, num_devices=1)
    arrays, args = {}, {}
    for name in _INS:
        a = _np.ascontiguousarray(inputs[name])
        arrays[f"in_{name}"] = a
        args[name] = nc.dram_tensor(f"in_{name}", a.shape, _mybir.dt.from_np(a.dtype), kind="ExternalInput").ap()
    out = nc.dram_tensor("out_0", inputs["x"].shape, _mybir.dt.float32, kind="ExternalOutput").ap()
    gnn_stack_kernel(nc, args, out)
    r = _run(nc, [arrays], core_ids=[0])
    return r.results[0]["out_0"]
```
